# Optimizing a Trainium2 kernel written in Bass

```python
import numpy as np
import jax
import jax.numpy as jnp

def _softmax(x, axis=-1):
    return jax.nn.softmax(x, axis=axis)

def _gelu(x):
    return jax.nn.gelu(x, approximate=True)

def _silu(x):
    return jax.nn.silu(x)

def _sigmoid(x):
    return jax.nn.sigmoid(x)

def _layernorm(x, axis=-1, eps=1e-05):
    m = jnp.mean(x, axis=axis, keepdims=True)
    v = jnp.var(x, axis=axis, keepdims=True)
    return (x - m) / jnp.sqrt(v + eps)

def _scatter_add(tgt, idx, src, axis=0):
    return tgt.at[idx].add(src)

def _segment_sum(src, seg, n):
    return jax.ops.segment_sum(src, seg, n)
kernel_name = 'mk_gnn_preln_d4_gnn_r32_be0a08'

def setup_inputs(seed: int=0):
    np.random.seed(seed)
    _w = jnp.asarray

    def _rec_inputs():
        import jax
        import jax.numpy as jnp
        _gk = jax.random.key(seed)
        x = -0.000202 + 1 * jax.random.normal(jax.random.fold_in(_gk, 1), (3125, 128), jnp.float32)
        _s = jax.random.randint(jax.random.fold_in(_gk, 2), (50000,), 0, 3125, jnp.int32)
        _d = jax.random.randint(jax.random.fold_in(_gk, 3), (50000,), 0, 3125, jnp.int32)
        _loop = jnp.arange(3125, dtype=jnp.int32)
        src = jnp.concatenate([_s, _d, _loop])
        dst = jnp.concatenate([_d, _s, _loop])
        _o = jnp.argsort(dst, stable=True)
        src = src[_o]
        dst = dst[_o]
        edge_attr_64 = -9.77346e-05 + 0.999888 * jax.random.normal(jax.random.fold_in(_gk, 12), (103125, 64), jnp.float32)
        edge_type_16 = jax.random.randint(jax.random.fold_in(_gk, 14), (103125,), 0, 16, jnp.int32)
        edge_weight1 = jax.random.uniform(jax.random.fold_in(_gk, 15), (103125, 1), jnp.float32, 0.0, 0.999998)
        node_type_8 = jax.random.randint(jax.random.fold_in(_gk, 16), (3125,), 0, 8, jnp.int32)
        node_vec1 = jax.random.uniform(jax.random.fold_in(_gk, 17), (3125, 1), jnp.float32, 0.0, 0.999884)
        return (x, src, dst, edge_attr_64, edge_type_16, edge_weight1, node_type_8, node_vec1)
    x, src, dst, edge_attr_64, edge_type_16, edge_weight1, node_type_8, node_vec1 = _rec_inputs()

    def _L0_gnn_setup():
        import jax, jax.numpy as jnp
        import numpy as np
        D = 128
        STEPS = 2
        N = 50000
        E = 15625

        def _mlp2(h, W1, b1, W2, b2):
            return jax.nn.relu(h @ W1 + b1) @ W2 + b2
        key = jax.random.key(seed)
        ks = jax.random.split(key, 16)
        s = 1.0 / np.sqrt(2 * D)
        t = 1.0 / np.sqrt(D)
        inp = {'x': jax.random.normal(ks[0], (N, D), dtype=jnp.float32), 'edge_index': jax.random.randint(ks[1], (2, E), 0, N, dtype=jnp.int64), 'msg_W1': jax.random.uniform(ks[2], (2 * D, D), jnp.float32, -s, s), 'msg_b1': jnp.zeros((D,), jnp.float32), 'msg_W2': jax.random.uniform(ks[3], (D, D), jnp.float32, -t, t), 'msg_b2': jnp.zeros((D,), jnp.float32), 'upd_W1': jax.random.uniform(ks[4], (2 * D, D), jnp.float32, -s, s), 'upd_b1': jnp.zeros((D,), jnp.float32), 'upd_W2': jax.random.uniform(ks[5], (D, D), jnp.float32, -t, t), 'upd_b2': jnp.zeros((D,), jnp.float32), 'att_W1': jax.random.uniform(ks[6], (2 * D, D), jnp.float32, -s, s), 'att_b1': jnp.zeros((D,), jnp.float32), 'att_W2': jax.random.uniform(ks[7], (D, 1), jnp.float32, -t, t), 'att_b2': jnp.zeros((1,), jnp.float32), 'glb_W': jax.random.uniform(ks[8], (D, D), jnp.float32, -t, t), 'glb_b': jnp.zeros((D,), jnp.float32)}
        return inp
    _L0_gnn_all = _L0_gnn_setup()
    _L0_gnn_in = {k: v for k, v in _L0_gnn_all.items() if k in ('msg_W1', 'msg_b1', 'msg_W2', 'msg_b2', 'upd_W1', 'upd_b1', 'upd_W2', 'upd_b2', 'att_W1', 'att_b1', 'att_W2', 'att_b2', 'glb_W', 'glb_b')}
    del _L0_gnn_all

    def _L1_gnn_setup():
        import jax, jax.numpy as jnp
        import numpy as np
        N = 3125
        E = 50000
        F_IN = 128
        F_OUT = 128
        BN_EPS = 1e-05
        key = jax.random.key(seed)
        ks = jax.random.split(key, 8)
        x = jax.random.normal(ks[0], (N, F_IN), dtype=jnp.float32)
        edge_index = jax.random.randint(ks[1], (2, E), 0, N, dtype=jnp.int64)
        eps = jnp.zeros((), dtype=jnp.float32)
        lim1 = 1.0 / np.sqrt(F_IN)
        W1 = jax.random.uniform(ks[2], (F_OUT, F_IN), minval=-lim1, maxval=lim1, dtype=jnp.float32)
        b1 = jax.random.uniform(ks[3], (F_OUT,), minval=-lim1, maxval=lim1, dtype=jnp.float32)
        gamma = jnp.ones((F_OUT,), dtype=jnp.float32)
        beta = jnp.zeros((F_OUT,), dtype=jnp.float32)
        lim2 = 1.0 / np.sqrt(F_OUT)
        W2 = jax.random.uniform(ks[4], (F_OUT, F_OUT), minval=-lim2, maxval=lim2, dtype=jnp.float32)
        b2 = jax.random.uniform(ks[5], (F_OUT,), minval=-lim2, maxval=lim2, dtype=jnp.float32)
        return {'x': x, 'edge_index': edge_index, 'eps': eps, 'W1': W1, 'b1': b1, 'gamma': gamma, 'beta': beta, 'W2': W2, 'b2': b2}
    _L1_gnn_all = _L1_gnn_setup()
    _L1_gnn_in = {k: v for k, v in _L1_gnn_all.items() if k in ('eps', 'W1', 'b1', 'gamma', 'beta', 'W2', 'b2')}
    del _L1_gnn_all

    def _L2_gnn_setup():
        import jax, jax.numpy as jnp
        import numpy as np
        N = 50000
        E = 15625
        IN_C = 128
        OUT_C = 128
        N_NODE_TYPES = 8
        N_EDGE_TYPES = 16
        H = 8
        DH = OUT_C // H
        LN_EPS = 1e-05

        def _hgt_forward(x, node_types, edge_src, edge_dst, edge_rel, type_emb, Wk, Wq, Wv, rel_scale, Wo, bo, Wskip, gamma, beta):
            n = x.shape[0]
            x_aug = jnp.concatenate([x, type_emb[node_types]], axis=-1)
            K = (x_aug @ Wk).reshape(n, H, DH)
            Q = (x_aug @ Wq).reshape(n, H, DH)
            V = (x_aug @ Wv).reshape(n, H, DH)
            attn = jnp.einsum('ehd,ehd->eh', Q[edge_dst], K[edge_src])
            attn = attn * rel_scale[edge_rel] / np.sqrt(DH)
            attn = attn - jax.lax.stop_gradient(jnp.max(attn))
            attn_exp = jnp.exp(attn)
            attn_sum = jax.ops.segment_sum(attn_exp, edge_dst, num_segments=n)
            attn_norm = attn_exp / (attn_sum[edge_dst] + 1e-16)
            msg = attn_norm[..., None] * V[edge_src]
            out = jax.ops.segment_sum(msg, edge_dst, num_segments=n).reshape(n, OUT_C)
            out = out @ Wo + bo
            skip = x_aug @ Wskip
            h = out + skip
            mu = jnp.mean(h, axis=-1, keepdims=True)
            var = jnp.mean(jnp.square(h - mu), axis=-1, keepdims=True)
            h = (h - mu) * jax.lax.rsqrt(var + LN_EPS) * gamma + beta
            return jax.nn.elu(h)
        key = jax.random.key(seed)
        ks = jax.random.split(key, 16)
        inp = {'x': jax.random.normal(ks[0], (N, IN_C), dtype=jnp.float32), 'node_types': jax.random.randint(ks[1], (N,), 0, N_NODE_TYPES, dtype=jnp.int32), 'edge_src': jax.random.randint(ks[2], (E,), 0, N, dtype=jnp.int32), 'edge_dst': jax.random.randint(ks[3], (E,), 0, N, dtype=jnp.int32), 'edge_rel': jax.random.randint(ks[4], (E,), 0, N_EDGE_TYPES, dtype=jnp.int32), 'type_emb': 0.1 * jax.random.normal(ks[5], (N_NODE_TYPES, IN_C), dtype=jnp.float32), 'Wk': jax.random.normal(ks[6], (2 * IN_C, OUT_C), dtype=jnp.float32) * (1.0 / np.sqrt(2 * IN_C)), 'Wq': jax.random.normal(ks[7], (2 * IN_C, OUT_C), dtype=jnp.float32) * (1.0 / np.sqrt(2 * IN_C)), 'Wv': jax.random.normal(ks[8], (2 * IN_C, OUT_C), dtype=jnp.float32) * (1.0 / np.sqrt(2 * IN_C)), 'rel_scale': jnp.ones((N_EDGE_TYPES, H), dtype=jnp.float32), 'Wo': jax.random.normal(ks[9], (OUT_C, OUT_C), dtype=jnp.float32) * (1.0 / np.sqrt(OUT_C)), 'bo': jnp.zeros((OUT_C,), dtype=jnp.float32), 'Wskip': jax.random.normal(ks[10], (2 * IN_C, OUT_C), dtype=jnp.float32) * (1.0 / np.sqrt(2 * IN_C)), 'gamma': jnp.ones((OUT_C,), dtype=jnp.float32), 'beta': jnp.zeros((OUT_C,), dtype=jnp.float32)}
        return inp
    _L2_gnn_all = _L2_gnn_setup()
    _L2_gnn_in = {k: v for k, v in _L2_gnn_all.items() if k in ('type_emb', 'Wk', 'Wq', 'Wv', 'rel_scale', 'Wo', 'bo', 'Wskip', 'gamma', 'beta')}
    del _L2_gnn_all

    def _L3_gnn_setup():
        import jax, jax.numpy as jnp
        import numpy as np
        N_NODES, N_EDGES = (50000, 25000)
        NODE_DIM, EDGE_DIM, HIDDEN, HEADS = (128, 64, 128, 8)
        HEAD_DIM = HIDDEN // HEADS
        key = jax.random.key(seed)
        ks = jax.random.split(key, 24)

        def lin(k, fan_in, fan_out):
            lim = 1.0 / np.sqrt(fan_in)
            kw, kb = jax.random.split(k)
            W = jax.random.uniform(kw, (fan_in, fan_out), jnp.float32, -lim, lim)
            b = jax.random.uniform(kb, (fan_out,), jnp.float32, -lim, lim)
            return (W, b)
        inp = {}
        inp['nodes'] = jax.random.normal(ks[0], (N_NODES, NODE_DIM), jnp.float32)
        inp['edges'] = jax.random.normal(ks[1], (N_EDGES, EDGE_DIM), jnp.float32)
        inp['edge_index'] = jax.random.randint(ks[2], (2, N_EDGES), 0, N_NODES, jnp.int32)
        inp['conservation_scores'] = jax.random.uniform(ks[3], (N_NODES, 1), jnp.float32)
        inp['distances'] = jax.random.uniform(ks[4], (N_EDGES, 1), jnp.float32)
        inp['Wq'], inp['bq'] = lin(ks[5], NODE_DIM, HIDDEN)
        inp['Wk'], inp['bk'] = lin(ks[6], NODE_DIM, HIDDEN)
        inp['Wv'], inp['bv'] = lin(ks[7], NODE_DIM, HIDDEN)
        inp['We'], inp['be'] = lin(ks[8], EDGE_DIM, HEADS)
        inp['Wc1'], inp['bc1'] = lin(ks[9], 1, 32)
        inp['Wc2'], inp['bc2'] = lin(ks[10], 32, HEADS)
        inp['Wd1'], inp['bd1'] = lin(ks[11], 1, 16)
        inp['Wd2'], inp['bd2'] = lin(ks[12], 16, HEADS)
        inp['Wo'], inp['bo'] = lin(ks[13], HIDDEN, NODE_DIM)
        inp['gamma'] = jnp.ones((NODE_DIM,), jnp.float32)
        inp['beta'] = jnp.zeros((NODE_DIM,), jnp.float32)
        return inp
    _L3_gnn_all = _L3_gnn_setup()
    _L3_gnn_in = {k: v for k, v in _L3_gnn_all.items() if k in ('Wq', 'bq', 'Wk', 'bk', 'Wv', 'bv', 'We', 'be', 'Wc1', 'bc1', 'Wc2', 'bc2', 'Wd1', 'bd1', 'Wd2', 'bd2', 'Wo', 'bo', 'gamma', 'beta')}
    del _L3_gnn_all
    return {'x': x, 'src': src, 'dst': dst, 'edge_attr_64': edge_attr_64, 'edge_type_16': edge_type_16, 'edge_weight1': edge_weight1, 'node_type_8': node_type_8, 'node_vec1': node_vec1, 'L0_gnn_msg_W1': _L0_gnn_in['msg_W1'], 'L0_gnn_msg_b1': _L0_gnn_in['msg_b1'], 'L0_gnn_msg_W2': _L0_gnn_in['msg_W2'], 'L0_gnn_msg_b2': _L0_gnn_in['msg_b2'], 'L0_gnn_upd_W1': _L0_gnn_in['upd_W1'], 'L0_gnn_upd_b1': _L0_gnn_in['upd_b1'], 'L0_gnn_upd_W2': _L0_gnn_in['upd_W2'], 'L0_gnn_upd_b2': _L0_gnn_in['upd_b2'], 'L0_gnn_att_W1': _L0_gnn_in['att_W1'], 'L0_gnn_att_b1': _L0_gnn_in['att_b1'], 'L0_gnn_att_W2': _L0_gnn_in['att_W2'], 'L0_gnn_att_b2': _L0_gnn_in['att_b2'], 'L0_gnn_glb_W': _L0_gnn_in['glb_W'], 'L0_gnn_glb_b': _L0_gnn_in['glb_b'], 'L1_gnn_eps': _L1_gnn_in['eps'], 'L1_gnn_W1': _L1_gnn_in['W1'], 'L1_gnn_b1': _L1_gnn_in['b1'], 'L1_gnn_gamma': _L1_gnn_in['gamma'], 'L1_gnn_beta': _L1_gnn_in['beta'], 'L1_gnn_W2': _L1_gnn_in['W2'], 'L1_gnn_b2': _L1_gnn_in['b2'], 'L2_gnn_type_emb': _L2_gnn_in['type_emb'], 'L2_gnn_Wk': _L2_gnn_in['Wk'], 'L2_gnn_Wq': _L2_gnn_in['Wq'], 'L2_gnn_Wv': _L2_gnn_in['Wv'], 'L2_gnn_rel_scale': _L2_gnn_in['rel_scale'], 'L2_gnn_Wo': _L2_gnn_in['Wo'], 'L2_gnn_bo': _L2_gnn_in['bo'], 'L2_gnn_Wskip': _L2_gnn_in['Wskip'], 'L2_gnn_gamma': _L2_gnn_in['gamma'], 'L2_gnn_beta': _L2_gnn_in['beta'], 'L3_gnn_Wq': _L3_gnn_in['Wq'], 'L3_gnn_bq': _L3_gnn_in['bq'], 'L3_gnn_Wk': _L3_gnn_in['Wk'], 'L3_gnn_bk': _L3_gnn_in['bk'], 'L3_gnn_Wv': _L3_gnn_in['Wv'], 'L3_gnn_bv': _L3_gnn_in['bv'], 'L3_gnn_We': _L3_gnn_in['We'], 'L3_gnn_be': _L3_gnn_in['be'], 'L3_gnn_Wc1': _L3_gnn_in['Wc1'], 'L3_gnn_bc1': _L3_gnn_in['bc1'], 'L3_gnn_Wc2': _L3_gnn_in['Wc2'], 'L3_gnn_bc2': _L3_gnn_in['bc2'], 'L3_gnn_Wd1': _L3_gnn_in['Wd1'], 'L3_gnn_bd1': _L3_gnn_in['bd1'], 'L3_gnn_Wd2': _L3_gnn_in['Wd2'], 'L3_gnn_bd2': _L3_gnn_in['bd2'], 'L3_gnn_Wo': _L3_gnn_in['Wo'], 'L3_gnn_bo': _L3_gnn_in['bo'], 'L3_gnn_gamma': _L3_gnn_in['gamma'], 'L3_gnn_beta': _L3_gnn_in['beta']}

def reference(x, src, dst, edge_attr_64, edge_type_16, edge_weight1, node_type_8, node_vec1, L0_gnn_msg_W1, L0_gnn_msg_b1, L0_gnn_msg_W2, L0_gnn_msg_b2, L0_gnn_upd_W1, L0_gnn_upd_b1, L0_gnn_upd_W2, L0_gnn_upd_b2, L0_gnn_att_W1, L0_gnn_att_b1, L0_gnn_att_W2, L0_gnn_att_b2, L0_gnn_glb_W, L0_gnn_glb_b, L1_gnn_eps, L1_gnn_W1, L1_gnn_b1, L1_gnn_gamma, L1_gnn_beta, L1_gnn_W2, L1_gnn_b2, L2_gnn_type_emb, L2_gnn_Wk, L2_gnn_Wq, L2_gnn_Wv, L2_gnn_rel_scale, L2_gnn_Wo, L2_gnn_bo, L2_gnn_Wskip, L2_gnn_gamma, L2_gnn_beta, L3_gnn_Wq, L3_gnn_bq, L3_gnn_Wk, L3_gnn_bk, L3_gnn_Wv, L3_gnn_bv, L3_gnn_We, L3_gnn_be, L3_gnn_Wc1, L3_gnn_bc1, L3_gnn_Wc2, L3_gnn_bc2, L3_gnn_Wd1, L3_gnn_bd1, L3_gnn_Wd2, L3_gnn_bd2, L3_gnn_Wo, L3_gnn_bo, L3_gnn_gamma, L3_gnn_beta):
    import jax
    import jax.numpy as jnp

    def _L0_gnn_ref(x, edge_index, msg_W1, msg_b1, msg_W2, msg_b2, upd_W1, upd_b1, upd_W2, upd_b2, att_W1, att_b1, att_W2, att_b2, glb_W, glb_b):
        import jax, jax.numpy as jnp
        import numpy as np
        D = 128
        STEPS = 2
        N = 50000
        E = 15625

        def _mlp2(h, W1, b1, W2, b2):
            return jax.nn.relu(h @ W1 + b1) @ W2 + b2
        num_nodes = x.shape[0]
        src, dst = (edge_index[0], edge_index[1])
        global_repr = jax.nn.relu(jnp.mean(x, axis=0, keepdims=True) @ glb_W + glb_b)
        h = x
        for _ in range(STEPS):
            edge_feat = jnp.concatenate([h[src], h[dst]], axis=-1)
            messages = _mlp2(edge_feat, msg_W1, msg_b1, msg_W2, msg_b2)
            att = jax.nn.sigmoid(_mlp2(edge_feat, att_W1, att_b1, att_W2, att_b2))
            weighted = messages * att
            aggregated = jax.ops.segment_sum(weighted, dst, num_segments=num_nodes)
            combined = jnp.concatenate([h, aggregated], axis=-1)
            new_h = _mlp2(combined, upd_W1, upd_b1, upd_W2, upd_b2)
            h = new_h + h + global_repr
        return h

    def _L1_gnn_ref(x, edge_index, eps, W1, b1, gamma, beta, W2, b2):
        import jax, jax.numpy as jnp
        import numpy as np
        N = 3125
        E = 50000
        F_IN = 128
        F_OUT = 128
        BN_EPS = 1e-05
        row, col = (edge_index[0], edge_index[1])
        agg = jax.ops.segment_sum(x[col], row, num_segments=x.shape[0])
        h = (1.0 + eps) * x + agg
        h = h @ W1.T + b1
        mu = jnp.mean(h, axis=0)
        var = jnp.mean(jnp.square(h - mu), axis=0)
        h = (h - mu) * jax.lax.rsqrt(var + BN_EPS) * gamma + beta
        h = jax.nn.relu(h)
        return h @ W2.T + b2

    def _L2_gnn_ref(x, node_types, edge_src, edge_dst, edge_rel, type_emb, Wk, Wq, Wv, rel_scale, Wo, bo, Wskip, gamma, beta):
        import jax, jax.numpy as jnp
        import numpy as np
        N = 50000
        E = 15625
        IN_C = 128
        OUT_C = 128
        N_NODE_TYPES = 8
        N_EDGE_TYPES = 16
        H = 8
        DH = OUT_C // H
        LN_EPS = 1e-05

        def _hgt_forward(x, node_types, edge_src, edge_dst, edge_rel, type_emb, Wk, Wq, Wv, rel_scale, Wo, bo, Wskip, gamma, beta):
            n = x.shape[0]
            x_aug = jnp.concatenate([x, type_emb[node_types]], axis=-1)
            K = (x_aug @ Wk).reshape(n, H, DH)
            Q = (x_aug @ Wq).reshape(n, H, DH)
            V = (x_aug @ Wv).reshape(n, H, DH)
            attn = jnp.einsum('ehd,ehd->eh', Q[edge_dst], K[edge_src])
            attn = attn * rel_scale[edge_rel] / np.sqrt(DH)
            attn = attn - jax.lax.stop_gradient(jnp.max(attn))
            attn_exp = jnp.exp(attn)
            attn_sum = jax.ops.segment_sum(attn_exp, edge_dst, num_segments=n)
            attn_norm = attn_exp / (attn_sum[edge_dst] + 1e-16)
            msg = attn_norm[..., None] * V[edge_src]
            out = jax.ops.segment_sum(msg, edge_dst, num_segments=n).reshape(n, OUT_C)
            out = out @ Wo + bo
            skip = x_aug @ Wskip
            h = out + skip
            mu = jnp.mean(h, axis=-1, keepdims=True)
            var = jnp.mean(jnp.square(h - mu), axis=-1, keepdims=True)
            h = (h - mu) * jax.lax.rsqrt(var + LN_EPS) * gamma + beta
            return jax.nn.elu(h)
        return _hgt_forward(x, node_types, edge_src, edge_dst, edge_rel, type_emb, Wk, Wq, Wv, rel_scale, Wo, bo, Wskip, gamma, beta)

    def _L3_gnn_ref(nodes, edges, edge_index, conservation_scores, distances, Wq, bq, Wk, bk, Wv, bv, We, be, Wc1, bc1, Wc2, bc2, Wd1, bd1, Wd2, bd2, Wo, bo, gamma, beta):
        import jax, jax.numpy as jnp
        import numpy as np
        N_NODES, N_EDGES = (50000, 25000)
        NODE_DIM, EDGE_DIM, HIDDEN, HEADS = (128, 64, 128, 8)
        HEAD_DIM = HIDDEN // HEADS
        N = nodes.shape[0]
        src, tgt = (edge_index[0], edge_index[1])
        q = (nodes @ Wq + bq).reshape(N, HEADS, HEAD_DIM)
        k = (nodes @ Wk + bk).reshape(N, HEADS, HEAD_DIM)
        v = (nodes @ Wv + bv).reshape(N, HEADS, HEAD_DIM)
        scores = jnp.einsum('ehd,ehd->eh', q[src], k[tgt]) / np.sqrt(HEAD_DIM)
        scores = scores + edges @ We + be
        cons = jax.nn.sigmoid(jax.nn.relu(conservation_scores @ Wc1 + bc1) @ Wc2 + bc2)
        scores = scores * cons[tgt]
        scores = scores + jax.nn.relu(distances @ Wd1 + bd1) @ Wd2 + bd2
        seg_max = jax.ops.segment_max(scores, tgt, num_segments=N)
        w = jnp.exp(scores - seg_max[tgt])
        seg_sum = jax.ops.segment_sum(w, tgt, num_segments=N)
        weights = w / seg_sum[tgt]
        attended = weights[..., None] * v[tgt]
        agg = jax.ops.segment_sum(attended, tgt, num_segments=N).reshape(N, HIDDEN)
        out = agg @ Wo + bo
        x = nodes + out
        mu = jnp.mean(x, axis=-1, keepdims=True)
        var = jnp.var(x, axis=-1, keepdims=True)
        return (x - mu) / jnp.sqrt(var + 1e-05) * gamma + beta
    edge_index = jnp.stack([src, dst])
    h = jnp.maximum(_layernorm(x, axis=-1), 0.0)
    x = x + _L0_gnn_ref(h, edge_index, L0_gnn_msg_W1, L0_gnn_msg_b1, L0_gnn_msg_W2, L0_gnn_msg_b2, L0_gnn_upd_W1, L0_gnn_upd_b1, L0_gnn_upd_W2, L0_gnn_upd_b2, L0_gnn_att_W1, L0_gnn_att_b1, L0_gnn_att_W2, L0_gnn_att_b2, L0_gnn_glb_W, L0_gnn_glb_b)
    h = jnp.maximum(_layernorm(x, axis=-1), 0.0)
    x = x + _L1_gnn_ref(h, edge_index, L1_gnn_eps, L1_gnn_W1, L1_gnn_b1, L1_gnn_gamma, L1_gnn_beta, L1_gnn_W2, L1_gnn_b2)
    h = jnp.maximum(_layernorm(x, axis=-1), 0.0)
    x = x + _L2_gnn_ref(h, node_type_8, src, dst, edge_type_16, L2_gnn_type_emb, L2_gnn_Wk, L2_gnn_Wq, L2_gnn_Wv, L2_gnn_rel_scale, L2_gnn_Wo, L2_gnn_bo, L2_gnn_Wskip, L2_gnn_gamma, L2_gnn_beta)
    h = jnp.maximum(_layernorm(x, axis=-1), 0.0)
    x = x + _L3_gnn_ref(h, edge_attr_64, edge_index, node_vec1, edge_weight1, L3_gnn_Wq, L3_gnn_bq, L3_gnn_Wk, L3_gnn_bk, L3_gnn_Wv, L3_gnn_bv, L3_gnn_We, L3_gnn_be, L3_gnn_Wc1, L3_gnn_bc1, L3_gnn_Wc2, L3_gnn_bc2, L3_gnn_Wd1, L3_gnn_bd1, L3_gnn_Wd2, L3_gnn_bd2, L3_gnn_Wo, L3_gnn_bo, L3_gnn_gamma, L3_gnn_beta)
    return x

_drawn_inputs = setup_inputs


def setup_inputs(seed=0):
    import zlib

    import numpy as np

    out = dict(_drawn_inputs(seed))
    spreads = {'L0_gnn_msg_b1': (0.0, 0.1),
     'L0_gnn_msg_b2': (0.0, 0.1),
     'L0_gnn_upd_b1': (0.0, 0.1),
     'L0_gnn_upd_b2': (0.0, 0.1),
     'L0_gnn_att_b1': (0.0, 0.8),
     'L0_gnn_glb_b': (0.0, 0.1),
     'L1_gnn_gamma': (1.0, 0.2),
     'L1_gnn_beta': (0.0, 0.373),
     'L2_gnn_rel_scale': (1.0, 0.6),
     'L2_gnn_bo': (0.0, 0.1),
     'L2_gnn_gamma': (1.0, 0.2),
     'L2_gnn_beta': (0.0, 0.1),
     'L3_gnn_gamma': (1.0, 0.2),
     'L3_gnn_beta': (0.0, 0.277)}
    factors = {'edge_attr_64': 200.0,
     'edge_weight1': 200.0,
     'node_vec1': 64.0,
     'L1_gnn_b1': 200.0,
     'L2_gnn_Wk': 20.49,
     'L2_gnn_Wq': 109.732,
     'L3_gnn_Wq': 200.0,
     'L3_gnn_bq': 200.0,
     'L3_gnn_Wk': 200.0,
     'L3_gnn_bk': 200.0,
     'L3_gnn_bv': 4.23,
     'L3_gnn_We': 200.0,
     'L3_gnn_be': 200.0,
     'L3_gnn_Wc1': 200.0,
     'L3_gnn_bc1': 64.0,
     'L3_gnn_Wc2': 200.0,
     'L3_gnn_bc2': 64.0,
     'L3_gnn_Wd1': 200.0,
     'L3_gnn_bd1': 200.0,
     'L3_gnn_Wd2': 200.0,
     'L3_gnn_bd2': 64.0,
     'L2_gnn_Wv': 20.745,
     'L2_gnn_Wo': 24.049}
    for name, (base, spread) in spreads.items():
        noise = np.random.default_rng([zlib.crc32(name.encode()), seed]).standard_normal(out[name].shape)
        drawn = base * np.exp(spread * noise) if base else spread * noise
        out[name] = jnp.asarray(drawn.astype(out[name].dtype))
    for name, factor in factors.items():
        out[name] = (out[name] * factor).astype(out[name].dtype)
    return out
```

```python
import numpy as np
import concourse.bass as bass
from concourse import mybir
from contextlib import ExitStack

f32 = mybir.dt.float32
i32 = mybir.dt.int32
bf16 = mybir.dt.bfloat16
ALU = mybir.AluOpType
ACT = mybir.ActivationFunctionType
AX = mybir.AxisListType

P = 128
N = 3125
E = 103125
F = 128
NB = -(-N // P)
NP = NB * P
H = 8
DH = F // H
NC = -(-E // P)
TAIL = E - (NC - 1) * P
NV = -(-((E + NB * (P - 1)) // P) // 16) * 16
ROWS = NV * P
PADHI = 30
ds = bass.ds


class Core:

    def __init__(self, nc, ctx):
        self.nc, self.ctx, self.sems = nc, ctx, []
        ctx.callback(self.clear)

    def clear(self):
        if self.sems:
            self.nc.clear_and_free_semaphores(self.sems)
            self.nc.all_engine_barrier()

    def sb(self, name, shape, dt=f32):
        return self.ctx.enter_context(self.nc.sbuf_tensor(name, shape, dt))

    def sem(self, name):
        self.sems.append(self.nc.alloc_semaphore(name=name))
        return self.sems[-1]

    def psum(self, name, shape):
        return self.ctx.enter_context(self.nc.psum_tensor(name, shape, f32))

    def dram(self, name, shape, dt=f32):
        return self.nc.dram_tensor(name, shape, dt, kind="Internal").ap()


def constants(nc, top):
    k = {}
    k["ones"] = top.sb("ones", [P, P])
    k["zeros"] = top.sb("zeros", [P, P])
    k["zeros4"] = top.sb("zeros4", [P, 512])
    k["mean_of"] = top.sb("mean_of", [P, P])
    k["eps"] = top.sb("eps", [P, 1])
    k["ident"] = top.sb("ident", [P, P])
    k["tri"] = top.sb("tri", [P, P])
    k["before"] = top.sb("before", [P, P])
    k["iota"] = top.sb("iota", [P, P])
    k["iota_bf"] = top.sb("iota_bf", [P, P], bf16)
    k["part"] = top.sb("part", [P, 1])
    with ExitStack() as ctx:
        c = Core(nc, ctx)
        filled = c.sem("filled")
        block = ctx.enter_context(nc.Block())

        @block.gpsimd
        def _(pool):
            nc.gpsimd.memset(k["ones"][:, :], 1.0).then_inc(filled, 1)
            nc.gpsimd.memset(k["ident"][:, :], 0.0).then_inc(filled, 1)
            nc.gpsimd.iota(k["iota"][:, :], [[1, P]], base=0, channel_multiplier=0,
                           allow_small_or_imprecise_dtypes=True).then_inc(filled, 1)
            nc.gpsimd.iota(k["iota_bf"][:, :], [[1, P]], base=0, channel_multiplier=0,
                           allow_small_or_imprecise_dtypes=True).then_inc(filled, 1)
            nc.gpsimd.iota(k["part"][:, :], [[1, 1]], base=0, channel_multiplier=1,
                           allow_small_or_imprecise_dtypes=True).then_inc(filled, 1)
            nc.gpsimd.memset(k["zeros"][:, :], 0.0)
            nc.gpsimd.memset(k["zeros4"][:, :], 0.0)
            nc.gpsimd.memset(k["mean_of"][:, :], 1.0 / F)
            nc.gpsimd.memset(k["eps"][:, :], 1e-5)
            pool.wait_ge(filled, 5)
            nc.gpsimd.affine_select(out=k["ident"][:, :], in_=k["ident"][:, :], compare_op=ALU.not_equal,
                                    fill=1.0, base=0, pattern=[[-1, P]], channel_multiplier=1).then_inc(filled, 1)
            nc.gpsimd.affine_select(out=k["tri"][:, :], in_=k["ones"][:, :], compare_op=ALU.is_gt,
                                    fill=0.0, base=0, pattern=[[1, P]], channel_multiplier=-1).then_inc(filled, 1)
            nc.gpsimd.affine_select(out=k["before"][:, :], in_=k["ones"][:, :], compare_op=ALU.is_gt,
                                    fill=0.0, base=0, pattern=[[-1, P]], channel_multiplier=1).then_inc(filled, 1)
    return k


def load_keys(nc, k, key_in, key_col, lo_col, key_row, lo_row, ps, tag):
    NT = -(-NC // P)
    with ExitStack() as ctx:
        c = Core(nc, ctx)
        raw = c.sb("key_raw" + tag, [P, NT, P], i32)
        rows = c.sb("key_rows" + tag, [P, NT, P])
        lo = c.sb("key_lo" + tag, [P, NT, P], i32)
        lo_bf = c.sb("key_lo_bf" + tag, [P, NT, P], bf16)
        lo_f = c.sb("key_lo_f" + tag, [P, NT, P])
        padded = c.sem("padded" + tag)
        loaded = c.sem("keys_loaded" + tag)
        cast = c.sem("keys_cast" + tag)
        turned = c.sem("keys_turned" + tag)
        stored = c.sem("keys_stored" + tag)
        block = ctx.enter_context(nc.Block())
        full = NC - 1 - (NT - 1) * P

        @block.sync
        def _(sp):
            sp.wait_ge(padded, 1)
            sp.dma_start(raw[:, 0:NT - 1, :], key_in[0:(NT - 1) * P * P].rearrange("(t q p) -> q t p", q=P, p=P)).then_inc(loaded, 16)
            sp.dma_start(raw[0:full, NT - 1, :], key_in[(NT - 1) * P * P:(NC - 1) * P].rearrange("(q p) -> q p", p=P)).then_inc(loaded, 16)
            sp.dma_start(raw[full:full + 1, NT - 1, 0:TAIL], key_in[(NC - 1) * P:E].rearrange("(q p) -> q p", q=1)).then_inc(loaded, 16)
            sp.wait_ge(cast, 3)
            sp.dma_start(key_row[0:NT * P * P].rearrange("(t q p) -> q t p", q=P, p=P), rows[:, :, :]).then_inc(stored, 16)
            sp.dma_start(lo_row[0:NT * P * P].rearrange("(t q p) -> q t p", q=P, p=P), lo_bf[:, :, :]).then_inc(stored, 16)
            sp.wait_ge(stored, 32)

        @block.vector
        def _(dve):
            nc.vector.memset(raw[:, :, :], PADHI * P).then_inc(padded, 1)
            dve.wait_ge(loaded, 48)
            nc.vector.tensor_copy(rows[:, :, :], raw[:, :, :]).then_inc(cast, 1)
            nc.vector.tensor_scalar(lo[:, :, :], raw[:, :, :], P - 1, None, ALU.bitwise_and).then_inc(cast, 1)
            dve.wait_ge(cast, 2)
            nc.vector.tensor_copy(lo_bf[:, :, :], lo[:, :, :]).then_inc(cast, 1)
            nc.vector.tensor_copy(lo_f[:, :, :], lo[:, :, :]).then_inc(cast, 1)
            for t in range(NT):
                w = min(P, NC - t * P)
                dve.wait_ge(turned, 2 * t + 2)
                nc.vector.tensor_copy(key_col[:, t * P:t * P + w], ps[:, t, 0:w])
                nc.vector.tensor_copy(lo_col[:, t * P:t * P + w], ps[:, t, P:P + w])

        @block.tensor
        def _(pe):
            pe.wait_ge(cast, 4)
            for t in range(NT):
                nc.tensor.transpose(ps[:, t, 0:P], rows[:, t, :], k["ident"][:, :]).then_inc(turned, 1)
                nc.tensor.transpose(ps[:, t, P:2 * P], lo_f[:, t, :], k["ident"][:, :]).then_inc(turned, 1)


def sort_edges(nc, k, key_col, lo_col, fields, rec, chunk_block, ps, scratch, tag):
    W = rec.shape[1]
    key_row, lo_row = scratch
    G = 4
    STEPS = NC // G
    with ExitStack() as ctx:
        c = Core(nc, ctx)
        hi_col = c.sb("hi_col" + tag, [P, NC])
        pad_col = c.sb("pad_col" + tag, [P, NC])
        key_int = c.sb("key_int" + tag, [P, NC], i32)
        tmp_int = c.sb("tmp_int" + tag, [P, NC], i32)
        hist = c.sb("hist" + tag, [P, NB])
        start = c.sb("start" + tag, [P, NB])

        with ExitStack() as ctx2:
            s = Core(nc, ctx2)
            onehot_lo = s.sb("count_lo" + tag, [P, 2, 13, P], bf16)
            onehot_hi = s.sb("count_hi" + tag, [P, 2, 13, NB], bf16)
            split = s.sem("split" + tag)
            hots = s.sem("hots" + tag)
            used = [s.sem(f"hots_used{j}" + tag) for j in range(2)]
            block = ctx2.enter_context(nc.Block())
            GC = 13

            @block.vector
            def _(dve):
                nc.vector.tensor_copy(key_int[:, :], key_col[:, :]).then_inc(split, 1)
                dve.wait_ge(split, 1)
                nc.vector.tensor_scalar(tmp_int[:, :], key_int[:, :], 7, None, ALU.arith_shift_right).then_inc(split, 1)
                dve.wait_ge(split, 2)
                nc.vector.tensor_copy(hi_col[:, :], tmp_int[:, :]).then_inc(split, 1)
                dve.wait_ge(split, 3)
                nc.vector.tensor_scalar(pad_col[:, :], hi_col[:, :], float(PADHI), float(ROWS), ALU.is_ge, ALU.mult)
                with dve.Fori(0, NC // (2 * GC)) as i:
                    for j in range(2):
                        dve.wait_ge(used[j], i + 1)
                        at = i * (2 * GC) + j * GC
                        nc.vector.tensor_tensor(onehot_lo[:, j, :, :], k["iota"][:, None, :].to_broadcast([P, GC, P]),
                                                lo_col[:, ds(at, GC)].rearrange("p (c o) -> p c o", o=1).to_broadcast([P, GC, P]),
                                                ALU.is_equal)
                        nc.vector.tensor_tensor(onehot_hi[:, j, :, :], k["iota"][:, None, 0:NB].to_broadcast([P, GC, NB]),
                                                hi_col[:, ds(at, GC)].rearrange("p (c o) -> p c o", o=1).to_broadcast([P, GC, NB]),
                                                ALU.is_equal).then_inc(hots, 1)

            @block.tensor
            def _(pe):
                for j in range(2):
                    pe.sem_inc(used[j], 1)
                pe.wait_ge(split, 1)
                nc.tensor.matmul(ps[:, 0, 0:NB], k["zeros"][:, :], k["zeros"][:, 0:NB], start=True, stop=True,
                                 skip_group_check=True)
                with pe.Fori(0, NC // (2 * GC)) as i:
                    for j in range(2):
                        pe.wait_ge(hots, i * 2 + (j + 1))
                        for q in range(GC):
                            last = nc.tensor.matmul(ps[:, 0, 0:NB], onehot_lo[:, j, q, :], onehot_hi[:, j, q, :],
                                                    start=False, stop=True, skip_group_check=True)
                        last.then_inc(used[j], 1)

        with ExitStack() as ctx2:
            s = Core(nc, ctx2)
            tot = s.sb("tot" + tag, [P, NB], i32)
            chunks = s.sb("chunks" + tag, [P, NB])
            upto = s.sb("upto" + tag, [P, NB])
            first = s.sb("first" + tag, [P, NB])
            first_t = s.sb("first_t" + tag, [NB, P])
            iota_v = s.sb("iota_v" + tag, [NB, NV])
            reached = s.sb("reached" + tag, [NB, NV])
            step = s.sem("start_steps" + tag)
            made = s.sem("iota_v_made" + tag)
            block = ctx2.enter_context(nc.Block())

            @block.gpsimd
            def _(pool):
                nc.gpsimd.iota(iota_v[:, :], [[1, NV]], base=0, channel_multiplier=0,
                               allow_small_or_imprecise_dtypes=True).then_inc(made, 1)

            @block.vector
            def _(dve):
                nc.vector.tensor_copy(hist[:, :], ps[:, 0, 0:NB]).then_inc(step, 1)
                dve.wait_ge(step, 3)
                nc.vector.tensor_scalar(tot[:, :], ps[:, 1, 0:NB], float(P - 1), None, ALU.add).then_inc(step, 1)
                dve.wait_ge(step, 4)
                nc.vector.tensor_scalar(tot[:, :], tot[:, :], 7, None, ALU.arith_shift_right).then_inc(step, 1)
                dve.wait_ge(step, 5)
                nc.vector.tensor_copy(chunks[:, :], tot[:, :]).then_inc(step, 1)
                dve.wait_ge(step, 6)
                nc.vector.tensor_tensor_scan(upto[:, :], k["ones"][:, 0:NB], chunks[:, :], 0.0, ALU.mult, ALU.add).then_inc(step, 1)
                dve.wait_ge(step, 7)
                nc.vector.tensor_tensor(first[:, :], upto[:, :], chunks[:, :], ALU.subtract).then_inc(step, 1)
                dve.wait_ge(step, 8)
                nc.vector.scalar_tensor_tensor(start[:, :], first[:, :], float(P), ps[:, 2, 0:NB], ALU.mult, ALU.add).then_inc(step, 1)
                dve.wait_ge(step, 10)
                nc.vector.tensor_copy(first_t[:, :], ps[0:NB, 3, 0:P]).then_inc(step, 1)
                dve.wait_ge(step, 11)
                dve.wait_ge(made, 1)
                nc.vector.tensor_scalar(reached[:, :], iota_v[:, :], first_t[:, 0:1], None, ALU.is_ge).then_inc(step, 1)
                dve.wait_ge(step, 13)
                nc.vector.tensor_scalar(chunk_block[0:1, :], ps[0:1, 4:6, 0:NV // 2], -1.0, None, ALU.add)

            @block.tensor
            def _(pe):
                pe.wait_ge(step, 1)
                nc.tensor.matmul(ps[:, 1, 0:NB], k["ones"][:, :], hist[:, :], start=True, stop=True).then_inc(step, 1)
                nc.tensor.matmul(ps[:, 2, 0:NB], k["tri"][:, :], hist[:, :], start=True, stop=True).then_inc(step, 1)
                pe.wait_ge(step, 9)
                nc.tensor.transpose(ps[0:NB, 3, 0:P], first[:, :], k["ident"][:, :]).then_inc(step, 1)
                pe.wait_ge(step, 12)
                for j in range(2):
                    last = nc.tensor.matmul(ps[0:1, 4 + j, 0:NV // 2], k["ones"][0:NB, 0:1],
                                            reached[:, j * (NV // 2):(j + 1) * (NV // 2)], start=True, stop=True)
                last.then_inc(step, 1)

        with ExitStack() as ctx2:
            s = Core(nc, ctx2)
            krow = s.sb("krow" + tag, [P, 2, G, P])
            lrow = s.sb("lrow" + tag, [P, 2, G, P], bf16)
            hot_lo = s.sb("hot_lo" + tag, [P, 2, G, P], bf16)
            hot_hi = s.sb("hot_hi" + tag, [P, 2, G, NB], bf16)
            hot_lo_t = s.sb("hot_lo_t" + tag, [P, 2, G, P])
            run = s.sb("run" + tag, [P, 2, G, NB])
            junk = s.sb("junk" + tag, [P, 2, G, P + NB])
            inside = s.sb("inside" + tag, [P, 2, G])
            base = s.sb("base" + tag, [P, 2, G])
            slot = s.sb("slot" + tag, [P, 2, G], i32)
            place = s.sb("place" + tag, [P, 2, G], i32)
            chunk = s.sb("chunk" + tag, [P, 2, G], i32)
            pos = s.sb("pos" + tag, [P, 2, G], i32)
            out = s.sb("out_rec" + tag, [P, 2, G, W])
            rows_in = [s.sem(f"rows_in{j}" + tag) for j in range(2)]
            hots = s.sem("one_hots" + tag)
            looked = s.sem("looked_up" + tag)
            copied = s.sem("run_copied" + tag)
            counted = s.sem("counted" + tag)
            free = [s.sem(f"rows_used{j}" + tag) for j in range(2)]
            placed = s.sem("placed" + tag)
            chain = s.sem("chain" + tag)
            packed = s.sem("packed" + tag)
            admitted = s.sem("admitted" + tag)
            sent = [[s.sem(f"sent{j}{g}" + tag) for g in range(G)] for j in range(2)]
            block = ctx2.enter_context(nc.Block())
            PAIRS = NC // (2 * G)
            rest = NC - PAIRS * 2 * G
            peeled = [(0, min(G, rest)), (1, rest - min(G, rest))]
            peeled = [(j, n) for j, n in peeled if n > 0]

            @block.sync
            def _(sp):
                def load(i, j, n):
                    sp.wait_ge(free[j], i + 1)
                    at = (i * (2 * G) + j * G) * P
                    sp.dma_start(krow[:, j, 0:n, :], key_row[ds(at, n * P)].rearrange("(o n) -> o n", o=1).to_broadcast([P, n * P]).rearrange("q (c p) -> q c p", p=P)).then_inc(rows_in[j], 16)
                    sp.dma_start(lrow[:, j, 0:n, :], lo_row[ds(at, n * P)].rearrange("(o n) -> o n", o=1).to_broadcast([P, n * P]).rearrange("q (c p) -> q c p", p=P)).then_inc(rows_in[j], 16)

                with sp.Fori(0, PAIRS) as i:
                    for j in range(2):
                        load(i, j, G)
                for j, n in peeled:
                    load(PAIRS, j, n)

            @block.vector
            def _(dve):
                for j in range(2):
                    dve.sem_inc(free[j], 1)
                dve.sem_inc(chain, 4)

                def step(i, j, n, before):
                    at = i * (2 * G) + j * G
                    dve.wait_ge(rows_in[j], i * 32 + 32)
                    dve.wait_ge(counted, i * (2 * G) + (j * G + 1))
                    nc.vector.tensor_tensor(hot_lo[:, j, 0:n, :], k["iota"][:, None, :].to_broadcast([P, n, P]),
                                            lo_col[:, ds(at, n)].rearrange("p (c o) -> p c o", o=1).to_broadcast([P, n, P]), ALU.is_equal)
                    nc.vector.tensor_tensor(hot_hi[:, j, 0:n, :], k["iota"][:, None, 0:NB].to_broadcast([P, n, NB]),
                                            hi_col[:, ds(at, n)].rearrange("p (c o) -> p c o", o=1).to_broadcast([P, n, NB]), ALU.is_equal)
                    nc.vector.tensor_scalar(hot_lo_t[:, j, 0:n, :], lrow[:, j, 0:n, :], k["part"][:, 0:1], None, ALU.is_equal).then_inc(hots, 1)
                    for g in range(n):
                        last = nc.vector.scalar_tensor_tensor(junk[:, j, g, 0:P], krow[:, j, g, :], key_col[:, ds(at + g, 1)], k["before"][:, :],
                                                              ALU.is_equal, ALU.mult, accum_out=inside[:, j, g:g + 1])
                    last.then_inc(free[j], 1)
                    for g in range(n):
                        dve.wait_ge(looked, at + (g + 1))
                        last = nc.vector.scalar_tensor_tensor(junk[:, j, g, P:P + NB], k["iota"][:, 0:NB], hi_col[:, ds(at + g, 1)], ps[:, 2 + (j * G + g) % 4, 0:NB],
                                                              ALU.is_equal, ALU.mult, accum_out=base[:, j, g:g + 1])
                        last.then_inc(chain, 1)
                    dve.wait_ge(chain, at + (n + 4))
                    if before:
                        for g in range(n):
                            dve.wait_ge(sent[j][g], i * 16)
                    nc.vector.tensor_tensor(base[:, j, 0:n], base[:, j, 0:n], inside[:, j, 0:n], ALU.add).then_inc(placed, 1)
                    dve.wait_ge(placed, i * 10 + (5 * j + 1))
                    nc.vector.tensor_tensor(slot[:, j, 0:n], base[:, j, 0:n], pad_col[:, ds(at, n)], ALU.add).then_inc(placed, 1)
                    dve.wait_ge(placed, i * 10 + (5 * j + 2))
                    nc.vector.tensor_scalar(place[:, j, 0:n], slot[:, j, 0:n], P - 1, None, ALU.bitwise_and).then_inc(placed, 1)
                    nc.vector.tensor_scalar(chunk[:, j, 0:n], slot[:, j, 0:n], 7, None, ALU.arith_shift_right).then_inc(placed, 1)
                    dve.wait_ge(placed, i * 10 + (5 * j + 4))
                    nc.vector.scalar_tensor_tensor(pos[:, j, 0:n], place[:, j, 0:n], float(NV + 1), chunk[:, j, 0:n],
                                                   ALU.mult, ALU.add).then_inc(placed, 1)

                for j in range(2):
                    step(0, j, G, False)
                with dve.Fori(1, PAIRS) as i:
                    for j in range(2):
                        step(i, j, G, True)
                for j, n in peeled:
                    step(PAIRS, j, n, True)

            @block.tensor
            def _(pe):
                pe.sem_inc(counted, 1)
                nc.tensor.matmul(ps[:, 0, 0:NB], k["ident"][:, :], start[:, :], start=True, stop=True,
                                 skip_group_check=True).then_inc(counted, 1)

                def step(i, j, n):
                    at = i * (2 * G) + j * G
                    pe.wait_ge(hots, i * 2 + (j + 1))
                    for g in range(n):
                        pe.wait_ge(copied, at + (g + 1))
                        nc.tensor.matmul(ps[:, 0, 0:NB], hot_lo[:, j, g, :], hot_hi[:, j, g, :],
                                         start=False, stop=True, skip_group_check=True).then_inc(counted, 1)
                        pe.wait_ge(chain, at + (g + 1))
                        nc.tensor.matmul(ps[:, 2 + (j * G + g) % 4, 0:NB], hot_lo_t[:, j, g, :], run[:, j, g, :],
                                         start=True, stop=True).then_inc(looked, 1)

                with pe.Fori(0, PAIRS) as i:
                    for j in range(2):
                        step(i, j, G)
                for j, n in peeled:
                    step(PAIRS, j, n)

            @block.scalar
            def _(act):
                def step(i, j, n, before):
                    at = i * (2 * G) + j * G
                    for g in range(n):
                        act.wait_ge(counted, at + (g + 2))
                        nc.scalar.activation(run[:, j, g, :], ps[:, 0, 0:NB], ACT.Copy).then_inc(copied, 1)
                    if before:
                        for g in range(n):
                            act.wait_ge(sent[j][g], i * 16)
                    nc.scalar.activation(out[:, j, 0:n, :], fields(at, n), ACT.Copy).then_inc(packed, 1)

                for j in range(2):
                    step(0, j, G, False)
                with act.Fori(1, PAIRS) as i:
                    for j in range(2):
                        step(i, j, G, True)
                for j, n in peeled:
                    step(PAIRS, j, n, True)

            @block.gpsimd
            def _(pool):
                def step(i, j, n):
                    pool.wait_ge(placed, i * 10 + (5 * j + 5))
                    pool.wait_ge(packed, i * 2 + (j + 1))
                    pool.sem_inc(admitted, 1)
                    for g in range(n):
                        nc.gpsimd.indirect_dma_start(rec, bass.IndirectOffsetOnAxis(pos[:, j, g:g + 1], 0),
                                                     out[:, j, g, :], None).then_inc(sent[j][g], 16)

                with pool.Fori(0, PAIRS) as i:
                    for j in range(2):
                        step(i, j, G)
                for j, n in peeled:
                    step(PAIRS, j, n)
                for j in range(2):
                    for g in range(G):
                        n = dict(peeled).get(j, 0)
                        pool.wait_ge(sent[j][g], 16 * (PAIRS + (g < n)))


W_REC = 2 + 3 * H
ATTR = 64
HID_D = 16
TYPES = 16


def edge_terms(nc, k, a, feat, ps):
    G = 8
    PAIRS = NC // (2 * G)
    TAIL_CHUNKS = NC - 2 * PAIRS * G
    TAIL_EDGES = E - 2 * PAIRS * G * P
    HID0, TYPE0 = ATTR, 96
    HID1 = HID0 + HID_D
    K = TYPE0 + TYPES
    attr, dist, kind = a["edge_attr_64"], a["edge_weight1"], a["edge_type_16"]
    with ExitStack() as ctx:
        c = Core(nc, ctx)
        raw = c.sb("attr_raw", [P, 2, G, ATTR])
        drow = c.sb("dist_rows", [P, 2, G * P])
        trow = c.sb("type_rows", [P, 2, G * P], i32)
        stack = c.sb("stack", [K, 2, G * P])
        weight = c.sb("term_weight", [K, 3 * H])
        type_of = c.sb("type_of", [P, 1])
        wd1 = c.sb("wd1", [P, 1])
        bd1 = c.sb("bd1", [P, 1])
        bias = c.sb("term_bias", [P, 3, H])
        zeroed = c.sem("zeroed")
        weights = c.sem("term_weights")
        arrived = [c.sem(f"attr_in{j}") for j in range(2)]
        rows_in = [c.sem(f"term_rows_in{j}") for j in range(2)]
        types_in = [c.sem(f"term_types_in{j}") for j in range(2)]
        hots, hidden = c.sem("type_hots"), c.sem("dist_hidden")
        turned = c.sem("attr_turned")
        moved = c.sem("attr_moved")
        done = c.sem("terms_done")
        kept = c.sem("terms_kept")
        admitted, let = c.sem("loads_admitted"), c.sem("turns_admitted")
        block = ctx.enter_context(nc.Block())

        @block.sync
        def _(sp):
            sp.wait_ge(zeroed, 4)
            sp.dma_start(weight[0:HID0, 0:H], a["L3_gnn_We"]).then_inc(weights, 16)
            sp.dma_start(weight[HID0:HID1, H:2 * H], a["L3_gnn_Wd2"]).then_inc(weights, 16)
            sp.dma_start(weight[TYPE0:K, 2 * H:3 * H], a["L2_gnn_rel_scale"]).then_inc(weights, 16)
            sp.dma_start(wd1[HID0:HID1, :], a["L3_gnn_Wd1"].rearrange("o p -> p o")).then_inc(weights, 16)
            sp.dma_start(bd1[HID0:HID1, :], a["L3_gnn_bd1"].rearrange("(p o) -> p o", o=1)).then_inc(weights, 16)
            sp.dma_start(bias[:, 0, :], a["L3_gnn_be"].rearrange("(o h) -> o h", o=1).to_broadcast([P, H])).then_inc(weights, 16)
            sp.dma_start(bias[:, 1, :], a["L3_gnn_bd2"].rearrange("(o h) -> o h", o=1).to_broadcast([P, H])).then_inc(weights, 16)

            def load_rows(i, j, at, n):
                sp.wait_ge(hidden, i * 2 + (j + 1))
                sp.sem_inc(admitted, 1)
                sp.dma_start(drow[HID0:HID1, j, 0:n], dist[ds(at, n), :].rearrange("p o -> o p").to_broadcast([HID_D, n])).then_inc(rows_in[j], 16)
                sp.wait_ge(hots, i * 2 + (j + 1))
                sp.sem_inc(admitted, 1)
                sp.dma_start(trow[TYPE0:K, j, 0:n], kind[ds(at, n)].rearrange("(o p) -> o p", o=1).to_broadcast([TYPES, n])).then_inc(types_in[j], 16)

            with sp.Fori(0, PAIRS) as i:
                for j in range(2):
                    at = (i * (2 * G) + j * G) * P
                    sp.wait_ge(turned, i * 2 + (j + 1))
                    sp.sem_inc(admitted, 1)
                    sp.dma_start(raw[:, j, :, :], attr[ds(at, G * P), :].rearrange("(c p) f -> p c f", p=P)).then_inc(arrived[j], 16)
                    load_rows(i, j, at, G * P)
            at = 2 * PAIRS * G * P
            sp.wait_ge(turned, PAIRS * 2 + 1)
            for q in range(TAIL_CHUNKS):
                w = min(P, TAIL_EDGES - q * P)
                sp.dma_start(raw[0:w, 0, q, :], attr[at + q * P:at + q * P + w, :]).then_inc(arrived[0], 16)
            load_rows(PAIRS, 0, at, TAIL_EDGES)

        @block.vector
        def _(dve):
            dve.sem_inc(hots, 2)
            nc.vector.memset(weight[:, :], 0.0).then_inc(zeroed, 1)
            nc.vector.memset(bias[:, :, :], 0.0).then_inc(zeroed, 1)
            nc.vector.tensor_scalar(type_of[:, :], k["part"][:, :], float(-TYPE0), None, ALU.add).then_inc(zeroed, 1)
            nc.vector.memset(stack[HID0:TYPE0, :, :], 0.0).then_inc(zeroed, 1)
            dve.wait_ge(zeroed, 4)

            def hot_types(i, j, n):
                dve.wait_ge(types_in[j], i * 16 + 16)
                dve.wait_ge(done, i * 2 + (j + 1))
                nc.vector.tensor_scalar(stack[TYPE0:K, j, 0:n], trow[TYPE0:K, j, 0:n], type_of[TYPE0:K, 0:1], None, ALU.is_equal).then_inc(hots, 1)

            def keep(i, j, n):
                at = i * (2 * G) + j * G
                dve.wait_ge(done, i * 2 + (j + 3))
                nc.vector.tensor_tensor(feat[:, ds(at, n), 2:W_REC], ps[:, 4 + j, 0:n * 3 * H].rearrange("p (g w) -> p g w", g=n),
                                        bias[:, :, :].rearrange("p k h -> p (k h)")[:, None, :].to_broadcast([P, n, 3 * H]),
                                        ALU.add).then_inc(kept, 1)

            dve.wait_ge(weights, 112)
            hot_types(0, 0, G * P)
            with dve.Fori(0, PAIRS - 1) as i:
                hot_types(i, 1, G * P)
                keep(i, 0, G)
                hot_types(i + 1, 0, G * P)
                keep(i, 1, G)
            hot_types(PAIRS - 1, 1, G * P)
            keep(PAIRS - 1, 0, G)
            hot_types(PAIRS, 0, TAIL_EDGES)
            keep(PAIRS - 1, 1, G)
            keep(PAIRS, 0, TAIL_CHUNKS)

        @block.tensor
        def _(pe):
            pe.sem_inc(turned, 2)
            pe.sem_inc(done, 2)

            def turn(i, j, n, n_dmas=1):
                pe.wait_ge(arrived[j], i * 16 + 16 * n_dmas)
                pe.wait_ge(moved, i * 2 + (j + 1))
                pe.sem_inc(let, 1)
                for q in range(n):
                    last = nc.tensor.transpose(ps[0:ATTR, 2 * j + q // 4, (q % 4) * P:(q % 4 + 1) * P], raw[:, j, q, :], k["ident"][:, :])
                last.then_inc(turned, 1)

            def multiply(i, j, n):
                pe.wait_ge(moved, i * 2 + (j + 3))
                pe.wait_ge(hidden, i * 2 + (j + 3))
                pe.wait_ge(hots, i * 2 + (j + 3))
                pe.wait_ge(kept, i * 2 + (j + 1))
                for g in range(n):
                    last = nc.tensor.matmul(ps[:, 4 + j, g * 3 * H:(g + 1) * 3 * H], stack[:, j, g * P:(g + 1) * P], weight[:, :],
                                            start=True, stop=True, skip_group_check=True)
                last.then_inc(done, 1)

            pe.sem_inc(kept, 2)
            pe.wait_ge(weights, 112)
            turn(0, 0, G)
            with pe.Fori(0, PAIRS - 1) as i:
                turn(i, 1, G)
                multiply(i, 0, G)
                turn(i + 1, 0, G)
                multiply(i, 1, G)
            turn(PAIRS - 1, 1, G)
            multiply(PAIRS - 1, 0, G)
            turn(PAIRS, 0, TAIL_CHUNKS, TAIL_CHUNKS)
            multiply(PAIRS - 1, 1, G)
            multiply(PAIRS, 0, TAIL_CHUNKS)

        @block.scalar
        def _(act):
            act.sem_inc(moved, 2)
            act.sem_inc(hidden, 2)

            def fill(i, j, n, chunks):
                act.wait_ge(rows_in[j], i * 16 + 16)
                act.wait_ge(done, i * 2 + (j + 1))
                nc.scalar.activation(stack[HID0:HID1, j, 0:n], drow[HID0:HID1, j, 0:n], ACT.Relu, bias=bd1[HID0:HID1, 0:1],
                                     scale=wd1[HID0:HID1, 0:1]).then_inc(hidden, 1)
                act.wait_ge(turned, i * 2 + (j + 3))
                nc.scalar.activation(stack[0:ATTR, j, 0:chunks * P], ps[0:ATTR, 2 * j:2 * j + 2, :].rearrange("p b n -> p (b n)")[:, 0:chunks * P], ACT.Copy).then_inc(moved, 1)

            act.wait_ge(zeroed, 4)
            act.wait_ge(weights, 112)
            with act.Fori(0, PAIRS) as i:
                for j in range(2):
                    fill(i, j, G * P, G)
            fill(PAIRS, 0, TAIL_EDGES, TAIL_CHUNKS)


def sorted_index(nc, k, rec, src_i, loc, loc_row, ps, tag):
    NT = -(-NV // P)
    W = rec.shape[1]
    with ExitStack() as ctx:
        c = Core(nc, ctx)
        r = c.sb("rec_in" + tag, [P, NV + 1, W])
        turned_sb = c.sb("loc_t" + tag, [P, NT, P], bf16)
        loaded = c.sem("rec_loaded" + tag)
        split = c.sem("rec_split" + tag)
        turned = c.sem("loc_turned" + tag)
        moved = c.sem("loc_moved" + tag)
        stored = c.sem("loc_stored" + tag)
        block = ctx.enter_context(nc.Block())

        @block.sync
        def _(sp):
            sp.dma_start(r[:, :, :], rec.rearrange("(p v) w -> p v w", p=P)).then_inc(loaded, 16)
            sp.wait_ge(moved, NT)
            full = NV // P
            sp.dma_start(loc_row[0:full * P * P].rearrange("(t v p) -> v t p", v=P, p=P), turned_sb[:, 0:full, :]).then_inc(stored, 16)
            sp.dma_start(loc_row[full * P * P:NV * P].rearrange("(v p) -> v p", p=P), turned_sb[0:NV - full * P, full, :]).then_inc(stored, 16)
            sp.wait_ge(stored, 32)

        @block.vector
        def _(dve):
            dve.wait_ge(loaded, 16)
            nc.vector.tensor_copy(loc[:, :], r[:, 0:NV, 1]).then_inc(split, 1)
            nc.vector.tensor_copy(src_i[:, :], r[:, 0:NV, 0])
            for t in range(NT):
                w = min(P, NV - t * P)
                dve.wait_ge(turned, t + 1)
                nc.vector.tensor_copy(turned_sb[0:w, t, :], ps[0:w, t, 0:P]).then_inc(moved, 1)

        @block.tensor
        def _(pe):
            pe.wait_ge(split, 1)
            for t in range(NT):
                w = min(P, NV - t * P)
                nc.tensor.transpose(ps[0:w, t, 0:P], loc[:, t * P:t * P + w], k["ident"][:, :]).then_inc(turned, 1)


HIDC = 32


def load_weights(nc, top, a):
    w = {}
    jobs = []

    def mat(name, src, rows, cols):
        w[name] = top.sb("w_" + name, [rows, cols])
        jobs.append((w[name][:, :], src))

    def part(name, c0, c1, src):
        jobs.append((w[name][:, c0:c1], src))

    def col(name, src, n=P):
        w[name] = top.sb("w_" + name, [n, 1])
        jobs.append((w[name][:, :], src.rearrange("(p o) -> p o", o=1)))

    def row(name, src, n):
        w[name] = top.sb("w_" + name, [P, n])
        jobs.append((w[name][:, :], src.rearrange("(o f) -> o f", o=1).to_broadcast([P, n])))

    w["src0"] = top.sb("w_src0", [P, 2 * F])
    w["dst0"] = top.sb("w_dst0", [P, 2 * F])
    w["bias0"] = top.sb("w_bias0", [P, 2 * F])
    for n, name in enumerate(("msg", "att")):
        part("src0", n * F, (n + 1) * F, a[f"L0_gnn_{name}_W1"][0:F, :])
        part("dst0", n * F, (n + 1) * F, a[f"L0_gnn_{name}_W1"][F:2 * F, :])
        part("bias0", n * F, (n + 1) * F, a[f"L0_gnn_{name}_b1"].rearrange("(o f) -> o f", o=1).to_broadcast([P, F]))
    mat("msg_w2", a["L0_gnn_msg_W2"], F, F)
    row("msg_b2", a["L0_gnn_msg_b2"], F)
    mat("upd_w1h", a["L0_gnn_upd_W1"][0:F, :], F, F)
    mat("upd_w1a", a["L0_gnn_upd_W1"][F:2 * F, :], F, F)
    col("upd_b1", a["L0_gnn_upd_b1"])
    mat("upd_w2", a["L0_gnn_upd_W2"], F, F)
    col("upd_b2", a["L0_gnn_upd_b2"])
    row("att_w2", a["L0_gnn_att_W2"].rearrange("f o -> (f o)"), F)
    row("att_b2", a["L0_gnn_att_b2"], 1)
    mat("glb_w", a["L0_gnn_glb_W"], F, F)
    col("glb_b", a["L0_gnn_glb_b"])
    row("eps1", a["L1_gnn_eps"], 1)
    mat("w1_t", a["L1_gnn_W1"], F, F)
    mat("w2_t", a["L1_gnn_W2"], F, F)
    for name in ("b1", "gamma", "beta", "b2"):
        col("l1_" + name, a["L1_gnn_" + name])
    mat("type_emb", a["L2_gnn_type_emb"], 8, F)
    w["kv_h"] = top.sb("w_kv_h", [P, 2 * F])
    w["kv_t"] = top.sb("w_kv_t", [P, 2 * F])
    for n, name in enumerate(("Wk", "Wv")):
        part("kv_h", n * F, (n + 1) * F, a["L2_gnn_" + name][0:F, :])
        part("kv_t", n * F, (n + 1) * F, a["L2_gnn_" + name][F:2 * F, :])
    for name in ("Wq", "Wskip"):
        mat(name + "_h", a["L2_gnn_" + name][0:F, :], F, F)
        mat(name + "_t", a["L2_gnn_" + name][F:2 * F, :], F, F)
    mat("l2_Wo", a["L2_gnn_Wo"], F, F)
    for name in ("bo", "gamma", "beta"):
        col("l2_" + name, a["L2_gnn_" + name])
    for name in ("Wq", "Wk", "Wv"):
        mat("l3_" + name, a["L3_gnn_" + name], F, F)
    for name in ("bq", "bk", "bv"):
        row("l3_" + name, a["L3_gnn_" + name], F)
    mat("l3_Wo", a["L3_gnn_Wo"], F, F)
    for name in ("bo", "gamma", "beta"):
        col("l3_" + name, a["L3_gnn_" + name])
    mat("Wc1", a["L3_gnn_Wc1"], 1, HIDC)
    col("bc1", a["L3_gnn_bc1"], HIDC)
    mat("Wc2", a["L3_gnn_Wc2"], HIDC, H)
    row("bc2", a["L3_gnn_bc2"], H)
    with ExitStack() as ctx:
        c = Core(nc, ctx)
        loaded = c.sem("weights_loaded")
        block = ctx.enter_context(nc.Block())

        @block.sync
        def _(sp):
            for dst, src in jobs:
                sp.dma_start(dst, src).then_inc(loaded, 16)
            sp.wait_ge(loaded, 16 * len(jobs))
    return w


def wide(ps):
    return ps[:, :, :].rearrange("p b n -> p (b n)")


SPANS = [(a, min(a + 512, NP)) for a in range(0, NP, 512)]


def load_nodes(nc, k, x_in, xt, ps):
    LAST = N - (NB - 1) * P
    with ExitStack() as ctx:
        c = Core(nc, ctx)
        raw = c.sb("x_raw", [P, NB, F])
        zeroed, loaded, turned = c.sem("x_zeroed"), c.sem("x_loaded"), c.sem("x_turned")
        block = ctx.enter_context(nc.Block())

        @block.sync
        def _(sp):
            sp.dma_start(raw[:, 0:NB - 1, :], x_in[0:(NB - 1) * P, :].rearrange("(t p) f -> p t f", p=P)).then_inc(loaded, 16)
            sp.wait_ge(zeroed, 1)
            sp.dma_start(raw[0:LAST, NB - 1, :], x_in[(NB - 1) * P:N, :]).then_inc(loaded, 16)

        @block.tensor
        def _(pe):
            pe.wait_ge(loaded, 32)
            for t in range(NB):
                last = nc.tensor.transpose(wide(ps)[:, t * P:(t + 1) * P], raw[:, t, :], k["ident"][:, :])
            last.then_inc(turned, 1)

        @block.vector
        def _(dve):
            nc.vector.memset(raw[:, NB - 1, :], 0.0).then_inc(zeroed, 1)
            dve.wait_ge(turned, 1)
            nc.vector.tensor_copy(xt[:, :], wide(ps)[:, 0:NP])


def layernorm(nc, k, xt, out, ps, tag, relu=True):
    with ExitStack() as ctx:
        c = Core(nc, ctx)
        cen = c.sb("cen" + tag, [P, NP])
        sq = c.sb("sq" + tag, [P, NP])
        mean_ready, centred, squared = c.sem("mean_ready" + tag), c.sem("centred" + tag), c.sem("squared" + tag)
        var_ready, rooted, inverted = c.sem("var_ready" + tag), c.sem("rooted" + tag), c.sem("inverted" + tag)
        block = ctx.enter_context(nc.Block())

        @block.tensor
        def _(pe):
            for a, b in SPANS:
                last = nc.tensor.matmul(wide(ps)[:, a:b], k["mean_of"][:, :], xt[:, a:b], start=True, stop=True)
            last.then_inc(mean_ready, 1)
            pe.wait_ge(squared, 1)
            for a, b in SPANS:
                last = nc.tensor.matmul(wide(ps)[:, a:b], k["mean_of"][:, :], sq[:, a:b], start=True, stop=True)
            last.then_inc(var_ready, 1)

        @block.vector
        def _(dve):
            dve.wait_ge(mean_ready, 1)
            nc.vector.tensor_tensor(cen[:, :], xt[:, :], wide(ps)[:, 0:NP], ALU.subtract).then_inc(centred, 1)
            dve.wait_ge(rooted, 1)
            nc.vector.reciprocal(sq[:, :], sq[:, :]).then_inc(inverted, 1)
            dve.wait_ge(inverted, 1)
            if relu:
                nc.vector.scalar_tensor_tensor(out[:, :], cen[:, :], 0.0, sq[:, :], ALU.max, ALU.mult)
            else:
                nc.vector.tensor_tensor(out[:, :], cen[:, :], sq[:, :], ALU.mult)

        @block.scalar
        def _(act):
            act.wait_ge(centred, 1)
            nc.scalar.activation(sq[:, :], cen[:, :], ACT.Square).then_inc(squared, 1)
            act.wait_ge(var_ready, 1)
            nc.scalar.activation(sq[:, :], wide(ps)[:, 0:NP], ACT.Sqrt, bias=k["eps"][:, 0:1]).then_inc(rooted, 1)


def node_rows(nc, k, parts, width, bias, dest, ps, tag, dram=None):
    with ExitStack() as ctx:
        c = Core(nc, ctx)
        made = c.sem("rows_made" + tag)
        kept = c.sem("rows_kept" + tag)
        stored = c.sem("rows_stored" + tag)
        block = ctx.enter_context(nc.Block())

        @block.tensor
        def _(pe):
            for t in range(NB):
                if t >= 8:
                    pe.wait_ge(kept, t - 7)
                for n, (xt, w) in enumerate(parts):
                    last = nc.tensor.matmul(ps[:, t % 8, 0:width], xt[:, t * P:(t + 1) * P], w,
                                            start=n == 0, stop=n == len(parts) - 1)
                last.then_inc(made, 1)

        @block.vector
        def _(dve):
            for t in range(NB):
                dve.wait_ge(made, t + 1)
                if bias is None:
                    nc.vector.tensor_copy(dest[:, t, 0:width], ps[:, t % 8, 0:width]).then_inc(kept, 1)
                else:
                    nc.vector.tensor_tensor(dest[:, t, 0:width], ps[:, t % 8, 0:width], bias, ALU.add).then_inc(kept, 1)

        @block.sync
        def _(sp):
            if dram is not None:
                sp.wait_ge(kept, NB)
                sp.dma_start(dram.rearrange("(t p) f -> p t f", p=P), dest[:, :, 0:width]).then_inc(stored, 16)
                sp.wait_ge(stored, 16)


U = 8
ITERS = NV // (2 * U)
BLKCOLS = NP
WORK = 7


def load_blocks(nc, chunk_block, at, n, most):
    return nc.values_load_multi_w_load_instructions(chunk_block[0:1, ds(at, n)], engines=[mybir.EngineType.PE],
                                                    min_val=0, max_val=most, skip_runtime_bounds_check_because=
                                                    "sort_edges counts the node blocks begun: 1 to NB, less one")[1]


def zero_accumulators(nc, k, ps):
    for b in range(WORK):
        last = nc.tensor.matmul(ps[:, b, :], k["zeros"][:, :], k["zeros4"][:, :], start=True, stop=True, skip_group_check=True)
    return last


def attention_messages(nc, k, w, g, table, here, ps, tag):
    with ExitStack() as ctx:
        c = Core(nc, ctx)
        idx = c.sb("idx" + tag, [P, 2, U], i32)
        there = c.sb("there" + tag, [P, 2, U, 2 * F])
        rows = c.sb("locrows" + tag, [P, 2, U * P], bf16)
        hot_t = c.sb("hot_t" + tag, [P, 2, U * P])
        hot_s = c.sb("hot_s" + tag, [P, 2, U, P])
        relu = c.sb("relu" + tag, [P, 2, U, F])
        prod = c.sb("prod" + tag, [P, 2, U, F])
        dot = c.sb("dot" + tag, [P, 2, U])
        att = c.sb("att" + tag, [P, 2, U])
        indexed = c.sem("indexed" + tag)
        admitted = c.sem("adm" + tag)
        gathered = [[c.sem(f"gat{j}{q}" + tag) for q in range(U)] for j in range(2)]
        rows_in = [c.sem(f"rin{j}" + tag) for j in range(2)]
        hots = c.sem("hots" + tag)
        spread = c.sem("spread" + tag)
        summed, cut, dotted = c.sem("summed" + tag), c.sem("cut" + tag), c.sem("dotted" + tag)
        gated, weighted, added = c.sem("gated" + tag), c.sem("weighted" + tag), c.sem("added" + tag)
        block = ctx.enter_context(nc.Block())
        CH = 2 * U
        PR = U // 2

        @block.sync
        def _(sp):
            with sp.Fori(0, ITERS) as i:
                for j in range(2):
                    sp.wait_ge(hots, i * 2 + (j + 1))
                    sp.dma_start(rows[:, j, :], g["loc_row"][ds((i * CH + j * U) * P, U * P)].rearrange("(o n) -> o n", o=1)
                                 .to_broadcast([P, U * P])).then_inc(rows_in[j], 16)

        @block.gpsimd
        def _(pool):
            with pool.Fori(0, ITERS) as i:
                for j in range(2):
                    pool.wait_ge(indexed, i * 2 + (j + 1))
                    for q in range(U):
                        if q % 2 == 0:
                            pool.wait_ge(cut, i * CH // 2 + (j * PR + q // 2 + 1))
                        pool.wait_ge(dotted, i * CH + (j * U + q + 1))
                        pool.sem_inc(admitted, 1)
                        nc.gpsimd.indirect_dma_start(there[:, j, q, :], None, table,
                                                     bass.IndirectOffsetOnAxis(idx[:, j, q:q + 1], 0)).then_inc(gathered[j][q], 16)

        @block.vector
        def _(dve):
            dve.sem_inc(hots, 2)
            dve.sem_inc(dotted, CH)
            for j in range(2):
                nc.vector.tensor_copy(idx[:, j, :], g["src"][:, j * U:(j + 1) * U]).then_inc(indexed, 1)

            def hot_nodes(i, j):
                dve.wait_ge(rows_in[j], i * 16 + 16)
                dve.wait_ge(spread, i * (2 * PR) + (j * PR + PR))
                nc.vector.tensor_scalar(hot_t[:, j, :], rows[:, j, :], k["part"][:, 0:1], None, ALU.is_equal).then_inc(hots, 1)

            def dot_att(i, j, m):
                dve.wait_ge(summed, i * (2 * PR) + (j * PR + m + 1))
                for q in (2 * m, 2 * m + 1):
                    nc.vector.scalar_tensor_tensor(prod[:, j, q, :], there[:, j, q, F:2 * F], 0.0, w["att_w2"][:, :],
                                                   ALU.max, ALU.mult, accum_out=dot[:, j, q:q + 1]).then_inc(dotted, 1)

            def weigh(i, j, m):
                if m == 0:
                    dve.wait_ge(gated, i * 2 + (j + 1))
                    dve.wait_ge(added, i * CH + (j * U + U))
                for q in (2 * m, 2 * m + 1):
                    nc.vector.tensor_scalar(hot_s[:, j, q, :], k["iota"][:, :], g["loc"][:, ds(i * CH + (j * U + q), 1)],
                                            att[:, j, q:q + 1], ALU.is_equal, ALU.mult).then_inc(weighted, 1)

            def combine(i, j, before, after):
                for m in range(PR):
                    if before is not None and m:
                        weigh(*before, m)
                    for q in (2 * m, 2 * m + 1):
                        dve.wait_ge(gathered[j][q], i * 16 + 16)
                    dve.wait_ge(spread, i * (2 * PR) + (2 * PR + j * PR + m + 1))
                    pair = there[:, j, 2 * m:2 * m + 2, :].rearrange("p q f -> p (q f)")
                    nc.vector.tensor_tensor(pair, pair, ps[:, WORK, :], ALU.add).then_inc(summed, 1)
                    if m == PR - 1:
                        nc.vector.tensor_copy(idx[:, j, :], g["src"][:, ds(i * CH + (CH + j * U), U)]).then_inc(indexed, 1)
                    if before is not None and m == 0:
                        weigh(*before, 0)
                    if m:
                        dot_att(i, j, m - 1)
                    if m == 1 and after is not None:
                        hot_nodes(*after)
                dot_att(i, j, PR - 1)

            hot_nodes(0, 0)
            combine(0, 0, None, (0, 1))
            with dve.Fori(0, ITERS - 1) as i:
                combine(i, 1, (i, 0), (i + 1, 0))
                combine(i + 1, 0, (i, 1), (i + 1, 1))
            combine(ITERS - 1, 1, (ITERS - 1, 0), None)
            for m in range(PR):
                weigh(ITERS - 1, 1, m)

        @block.scalar
        def _(act):
            act.sem_inc(cut, 2 * PR)

            def step(i, j):
                act.wait_ge(added, i * CH + (j * U + U))
                for m in range(PR):
                    act.wait_ge(summed, i * (2 * PR) + (j * PR + m + 1))
                    nc.scalar.activation(relu[:, j, 2 * m:2 * m + 2, :], there[:, j, 2 * m:2 * m + 2, 0:F], ACT.Relu).then_inc(cut, 1)
                act.wait_ge(dotted, i * CH + (CH + j * U + U))
                nc.scalar.activation(att[:, j, :], dot[:, j, :], ACT.Sigmoid, bias=w["att_b2"][:, 0:1]).then_inc(gated, 1)

            with act.Fori(0, ITERS) as i:
                for j in range(2):
                    step(i, j)

        @block.tensor
        def _(pe):
            pe.sem_inc(spread, 2 * PR)
            pe.sem_inc(added, CH)
            zero_accumulators(nc, k, ps)

            def target_pair(i, j, m, blocks):
                if not isinstance(i, int) or i + j + m:
                    pe.wait_ge(summed, i * (2 * PR) + (j * PR + m))
                for q in (2 * m, 2 * m + 1):
                    last = nc.tensor.matmul(ps[:, WORK, (q % 2) * 2 * F:(q % 2 + 1) * 2 * F], hot_t[:, j, q * P:(q + 1) * P],
                                            here[:, :, :].rearrange("p t f -> p (t f)")[:, ds(blocks[q] * (2 * F), 2 * F)],
                                            start=True, stop=True, skip_group_check=True)
                last.then_inc(spread, 1)

            def add_pair(i, j, m, blocks):
                for q in (2 * m, 2 * m + 1):
                    pe.wait_ge(weighted, i * CH + (j * U + q + 1))
                    nc.tensor.matmul(wide(ps)[:, ds(blocks[q] * F, F)], hot_s[:, j, q, :], relu[:, j, q, :],
                                     start=False, stop=True, skip_group_check=True)
                    nc.tensor.matmul(wide(ps)[:, ds(blocks[q] + NP, 1)], hot_s[:, j, q, :], k["ones"][:, 0:1],
                                     start=False, stop=True, skip_group_check=True).then_inc(added, 1)

            def half_step(now, before):
                if now is not None:
                    blocks = load_blocks(nc, g["block"], now[0] * CH + now[1] * U, U, NB - 1)
                if before is not None:
                    blocks_before = load_blocks(nc, g["block"], before[0] * CH + before[1] * U, U, NB - 1)
                if now is not None:
                    pe.wait_ge(hots, now[0] * 2 + (now[1] + 3))
                for m in range(PR):
                    if now is not None:
                        target_pair(*now, m, blocks)
                    if before is not None:
                        add_pair(*before, m, blocks_before)

            half_step((0, 0), None)
            with pe.Fori(0, ITERS - 1) as i:
                half_step((i, 1), (i, 0))
                half_step((i + 1, 0), (i, 1))
            half_step((ITERS - 1, 1), (ITERS - 1, 0))
            half_step(None, (ITERS - 1, 1))


def collect(nc, k, ps, acc_t, sums, n_sums, tag, scale=None):
    with ExitStack() as ctx:
        c = Core(nc, ctx)
        rows = c.sb("acc_rows" + tag, [P, NP])
        out, ready, turned = c.sem("acc_out" + tag), c.sem("acc_ready" + tag), c.sem("acc_turned" + tag)
        block = ctx.enter_context(nc.Block())

        @block.vector
        def _(dve):
            if n_sums:
                nc.vector.tensor_copy(sums[:, :], wide(ps)[:, NP:NP + n_sums]).then_inc(out, 1)
            else:
                dve.sem_inc(out, 1)
            nc.vector.tensor_copy(rows[:, :], wide(ps)[:, 0:NP]).then_inc(out, 1)
            if scale is not None:
                dve.wait_ge(out, 2)
                scale(dve, rows, out)
            dve.wait_ge(turned, 1)
            nc.vector.tensor_copy(acc_t[:, :], wide(ps)[:, 0:NP])

        @block.tensor
        def _(pe):
            pe.wait_ge(out, 5 if scale is not None else 2)
            for t in range(NB):
                last = nc.tensor.transpose(wide(ps)[:, t * P:(t + 1) * P], rows[:, t * P:(t + 1) * P], k["ident"][:, :])
            last.then_inc(turned, 1)


def global_vector(nc, k, w, ht, glob, ps):
    with ExitStack() as ctx:
        c = Core(nc, ctx)
        mean = c.sb("node_mean", [P, 1])
        meaned, scaled, ready = c.sem("meaned"), c.sem("mean_scaled"), c.sem("glob_ready")
        block = ctx.enter_context(nc.Block())

        @block.vector
        def _(dve):
            nc.vector.tensor_reduce(mean[:, :], ht[:, 0:N], AX.X, ALU.add).then_inc(meaned, 1)
            dve.wait_ge(meaned, 1)
            nc.vector.tensor_scalar(mean[:, :], mean[:, :], 1.0 / N, None, ALU.mult).then_inc(scaled, 1)

        @block.tensor
        def _(pe):
            pe.wait_ge(scaled, 1)
            nc.tensor.matmul(ps[:, 0, 0:1], w["glb_w"][:, :], mean[:, :], start=True, stop=True).then_inc(ready, 1)

        @block.scalar
        def _(act):
            act.wait_ge(ready, 1)
            nc.scalar.activation(glob[:, :], ps[:, 0, 0:1], ACT.Relu, bias=w["glb_b"][:, 0:1])


def update_nodes(nc, k, w, ht, acc_t, sums, glob, ps, tag):
    with ExitStack() as ctx:
        c = Core(nc, ctx)
        bias = c.sb("msg_bias" + tag, [P, NB, F])
        agg = c.sb("agg" + tag, [P, NP])
        hid = c.sb("hid" + tag, [P, NP])
        biased, agg_made, agg_kept = c.sem("biased" + tag), c.sem("agg_made" + tag), c.sem("agg_kept" + tag)
        hid_made, hid_kept, new_made, moved = c.sem("hid_made" + tag), c.sem("hid_kept" + tag), c.sem("new_made" + tag), c.sem("h_moved" + tag)
        block = ctx.enter_context(nc.Block())

        @block.vector
        def _(dve):
            nc.vector.tensor_tensor(bias[:, :, :], w["msg_b2"][:, None, :].to_broadcast([P, NB, F]),
                                    sums[:, 0:NB].rearrange("p (t o) -> p t o", o=1).to_broadcast([P, NB, F]), ALU.mult).then_inc(biased, 1)
            dve.wait_ge(agg_made, 1)
            nc.vector.tensor_copy(agg[:, :], wide(ps)[:, 0:NP]).then_inc(agg_kept, 1)
            dve.wait_ge(hid_made, 1)
            nc.vector.tensor_scalar(ht[:, :], ht[:, :], w["upd_b2"][:, 0:1], glob[:, 0:1], ALU.add, ALU.add).then_inc(moved, 1)
            dve.wait_ge(moved, 1)
            dve.wait_ge(new_made, 1)
            nc.vector.tensor_tensor(ht[:, :], ht[:, :], wide(ps)[:, 0:NP], ALU.add)

        @block.tensor
        def _(pe):
            pe.wait_ge(biased, 1)
            for t in range(NB):
                at = slice(t * P, (t + 1) * P)
                nc.tensor.matmul(wide(ps)[:, at], w["msg_w2"][:, :], acc_t[:, at], start=True, stop=False)
                last = nc.tensor.matmul(wide(ps)[:, at], bias[:, t, :], k["ident"][:, :], start=False, stop=True)
            last.then_inc(agg_made, 1)
            pe.wait_ge(agg_kept, 1)
            for a, b in SPANS:
                nc.tensor.matmul(wide(ps)[:, a:b], w["upd_w1h"][:, :], ht[:, a:b], start=True, stop=False)
                last = nc.tensor.matmul(wide(ps)[:, a:b], w["upd_w1a"][:, :], agg[:, a:b], start=False, stop=True)
            last.then_inc(hid_made, 1)
            pe.wait_ge(hid_kept, 1)
            for a, b in SPANS:
                last = nc.tensor.matmul(wide(ps)[:, a:b], w["upd_w2"][:, :], hid[:, a:b], start=True, stop=True)
            last.then_inc(new_made, 1)

        @block.scalar
        def _(act):
            act.wait_ge(hid_made, 1)
            nc.scalar.activation(hid[:, :], wide(ps)[:, 0:NP], ACT.Relu, bias=w["upd_b1"][:, 0:1]).then_inc(hid_kept, 1)


def add_into(nc, xt, terms, tag):
    with ExitStack() as ctx:
        c = Core(nc, ctx)
        added = c.sem("x_added" + tag)
        block = ctx.enter_context(nc.Block())

        @block.vector
        def _(dve):
            for n, term in enumerate(terms):
                if n:
                    dve.wait_ge(added, n)
                nc.vector.tensor_tensor(xt[:, :], xt[:, :], term, ALU.add).then_inc(added, 1)


STEPS0 = 2


def layer0(nc, k, w, g, table, xt, ps):
    with ExitStack() as ctx:
        c = Core(nc, ctx)
        ht = c.sb("ht0", [P, NP])
        glob = c.sb("glob", [P, 1])
        layernorm(nc, k, xt, ht, ps, "0")
        global_vector(nc, k, w, ht, glob, ps)
        for step in range(STEPS0):
            tag = f"0{step}"
            with ExitStack() as rctx:
                r = Core(nc, rctx)
                here = r.sb("here" + tag, [P, NB, 2 * F])
                node_rows(nc, k, [(ht, w["src0"][:, :])], 2 * F, None, here, ps, tag + "a", dram=table)
                node_rows(nc, k, [(ht, w["dst0"][:, :])], 2 * F, w["bias0"][:, :], here, ps, tag + "b")
                attention_messages(nc, k, w, g, table, here, ps, tag)
            with ExitStack() as rctx:
                r = Core(nc, rctx)
                acc_t = r.sb("acc_t" + tag, [P, NP])
                sums = r.sb("att_sums" + tag, [P, NB])
                collect(nc, k, ps, acc_t, sums, NB, tag)
                update_nodes(nc, k, w, ht, acc_t, sums, glob, ps, tag)
        add_into(nc, xt, [ht[:, :]], "0")


def neighbour_sums(nc, k, g, table, ps, tag):
    with ExitStack() as ctx:
        c = Core(nc, ctx)
        idx = c.sb("idx" + tag, [P, 2, U], i32)
        there = c.sb("there" + tag, [P, 2, U, F])
        hot = c.sb("hot" + tag, [P, 2, U, P])
        indexed, admitted, weighted, added = c.sem("indexed" + tag), c.sem("adm" + tag), c.sem("hotted" + tag), c.sem("added" + tag)
        gathered = [[c.sem(f"gat{j}{q}" + tag) for q in range(U)] for j in range(2)]
        block = ctx.enter_context(nc.Block())
        CH = 2 * U

        @block.gpsimd
        def _(pool):
            with pool.Fori(0, ITERS) as i:
                for j in range(2):
                    pool.wait_ge(indexed, i * 2 + (j + 1))
                    for q in range(U):
                        pool.wait_ge(added, i * CH + (j * U + q + 1))
                        pool.sem_inc(admitted, 1)
                        nc.gpsimd.indirect_dma_start(there[:, j, q, :], None, table,
                                                     bass.IndirectOffsetOnAxis(idx[:, j, q:q + 1], 0)).then_inc(gathered[j][q], 16)

        @block.vector
        def _(dve):
            for j in range(2):
                nc.vector.tensor_copy(idx[:, j, :], g["src"][:, j * U:(j + 1) * U]).then_inc(indexed, 1)
            with dve.Fori(0, ITERS) as i:
                for j in range(2):
                    dve.wait_ge(added, i * CH + (j * U + U))
                    for q in range(U):
                        nc.vector.tensor_scalar(hot[:, j, q, :], k["iota"][:, :], g["loc"][:, ds(i * CH + (j * U + q), 1)],
                                                None, ALU.is_equal).then_inc(weighted, 1)
                    for q in range(U):
                        dve.wait_ge(gathered[j][q], i * 16 + 16)
                    nc.vector.tensor_copy(idx[:, j, :], g["src"][:, ds(i * CH + (CH + j * U), U)]).then_inc(indexed, 1)

        @block.tensor
        def _(pe):
            pe.sem_inc(added, CH)
            zero_accumulators(nc, k, ps)
            with pe.Fori(0, ITERS) as i:
                for j in range(2):
                    blocks = load_blocks(nc, g["block"], i * CH + j * U, U, NB - 1)
                    for q in range(U):
                        pe.wait_ge(gathered[j][q], i * 16 + 16)
                        pe.wait_ge(weighted, i * CH + (j * U + q + 1))
                        nc.tensor.matmul(wide(ps)[:, ds(blocks[q] * F, F)], hot[:, j, q, :], there[:, j, q, :],
                                         start=False, stop=True, skip_group_check=True).then_inc(added, 1)


def gin_nodes(nc, k, w, ht, acc_t, out, ps):
    with ExitStack() as ctx:
        c = Core(nc, ctx)
        cen = c.sb("gin_cen", [P, NP])
        sq = c.sb("gin_sq", [P, NP])
        st = c.sb("gin_stats", [P, 4])
        onep = c.sb("one_plus_eps", [P, 1])
        mixed, made, kept, step = c.sem("gin_mixed"), c.sem("gin_made"), c.sem("gin_kept"), c.sem("gin_steps")
        squared, rooted, cut, last_made = c.sem("gin_squared"), c.sem("gin_rooted"), c.sem("gin_cut"), c.sem("gin_last")
        block = ctx.enter_context(nc.Block())

        @block.vector
        def _(dve):
            nc.vector.tensor_scalar(onep[:, :], w["eps1"][:, :], 1.0, None, ALU.add).then_inc(mixed, 1)
            dve.wait_ge(mixed, 1)
            nc.vector.scalar_tensor_tensor(acc_t[:, :], ht[:, :], onep[:, 0:1], acc_t[:, :], ALU.mult, ALU.add).then_inc(mixed, 1)
            dve.wait_ge(made, 1)
            nc.vector.tensor_scalar(cen[:, :], wide(ps)[:, 0:NP], w["l1_b1"][:, 0:1], None, ALU.add).then_inc(step, 1)
            dve.wait_ge(step, 1)
            nc.vector.tensor_reduce(st[:, 0:1], cen[:, 0:N], AX.X, ALU.add).then_inc(step, 1)
            dve.wait_ge(step, 2)
            nc.vector.tensor_scalar(st[:, 0:1], st[:, 0:1], 1.0 / N, None, ALU.mult).then_inc(step, 1)
            dve.wait_ge(step, 3)
            nc.vector.tensor_scalar(cen[:, :], cen[:, :], st[:, 0:1], None, ALU.subtract).then_inc(step, 1)
            dve.wait_ge(squared, 1)
            nc.vector.tensor_reduce(st[:, 1:2], sq[:, 0:N], AX.X, ALU.add).then_inc(step, 1)
            dve.wait_ge(rooted, 1)
            nc.vector.reciprocal(st[:, 2:3], st[:, 2:3]).then_inc(step, 1)
            dve.wait_ge(step, 6)
            nc.vector.tensor_scalar(cen[:, :], cen[:, :], st[:, 2:3], w["l1_gamma"][:, 0:1], ALU.mult, ALU.mult).then_inc(step, 1)
            dve.wait_ge(last_made, 1)
            nc.vector.tensor_scalar(out[:, :], wide(ps)[:, 0:NP], w["l1_b2"][:, 0:1], None, ALU.add)

        @block.scalar
        def _(act):
            act.wait_ge(step, 4)
            nc.scalar.activation(sq[:, :], cen[:, :], ACT.Square).then_inc(squared, 1)
            act.wait_ge(step, 5)
            nc.scalar.activation(st[:, 2:3], st[:, 1:2], ACT.Sqrt, bias=k["eps"][:, 0:1], scale=1.0 / N).then_inc(rooted, 1)
            act.wait_ge(step, 7)
            nc.scalar.activation(sq[:, :], cen[:, :], ACT.Relu, bias=w["l1_beta"][:, 0:1]).then_inc(cut, 1)

        @block.tensor
        def _(pe):
            pe.wait_ge(mixed, 2)
            for a, b in SPANS:
                last = nc.tensor.matmul(wide(ps)[:, a:b], w["w1_t"][:, :], acc_t[:, a:b], start=True, stop=True)
            last.then_inc(made, 1)
            pe.wait_ge(cut, 1)
            for a, b in SPANS:
                last = nc.tensor.matmul(wide(ps)[:, a:b], w["w2_t"][:, :], sq[:, a:b], start=True, stop=True)
            last.then_inc(last_made, 1)


def layer1(nc, k, w, g, table, xt, ps):
    with ExitStack() as ctx:
        c = Core(nc, ctx)
        ht = c.sb("ht1", [P, NP])
        acc_t = c.sb("acc_t1", [P, NP])
        layernorm(nc, k, xt, ht, ps, "1")
        with ExitStack() as rctx:
            rows = Core(nc, rctx).sb("rows1", [P, NB, F])
            node_rows(nc, k, [(ht, k["ident"][:, :])], F, None, rows, ps, "1", dram=table)
        neighbour_sums(nc, k, g, table, ps, "1")
        collect(nc, k, ps, acc_t, None, 0, "1")
        gin_nodes(nc, k, w, ht, acc_t, acc_t, ps)
        add_into(nc, xt, [acc_t[:, :]], "1")


SQ = NV // 4


def edge_products(nc, k, g, table, wide_row, here, width, got, spool, ps, tag):
    with ExitStack() as ctx:
        c = Core(nc, ctx)
        extra = width - F
        idx = c.sb("idx" + tag, [P, 2, U], i32)
        there = c.sb("there" + tag, [P, 2, U, wide_row])
        rows = c.sb("locrows" + tag, [P, 2, U * P], bf16)
        hot_t = c.sb("hot_t" + tag, [P, 2, U * P])
        prod = c.sb("prod" + tag, [P, 2, U, F])
        indexed, admitted, hots, spread = c.sem("indexed" + tag), c.sem("adm" + tag), c.sem("hots" + tag), c.sem("spread" + tag)
        multiplied, summed = c.sem("multiplied" + tag), c.sem("headed" + tag)
        gathered = [[c.sem(f"gat{j}{q}" + tag) for q in range(U)] for j in range(2)]
        rows_in = [c.sem(f"rin{j}" + tag) for j in range(2)]
        spooled = [c.sem(f"spooled{j}" + tag) for j in range(2)]
        block = ctx.enter_context(nc.Block())
        CH = 2 * U
        PR = U // 2

        @block.sync
        def _(sp):
            with sp.Fori(0, ITERS) as i:
                for j in range(2):
                    sp.wait_ge(hots, i * 2 + (j + 1))
                    sp.dma_start(rows[:, j, :], g["loc_row"][ds((i * CH + j * U) * P, U * P)].rearrange("(o n) -> o n", o=1)
                                 .to_broadcast([P, U * P])).then_inc(rows_in[j], 16)

        @block.scalar
        def _(act):
            if spool is not None:
                with act.Fori(0, ITERS) as i:
                    for j in range(2):
                        for q in range(U):
                            act.wait_ge(gathered[j][q], i * 16 + 16)
                        act.dma_start(spool[:, ds(i * CH + j * U, U), :], there[:, j, :, F:wide_row]).then_inc(spooled[j], 16)
                for j in range(2):
                    act.wait_ge(spooled[j], 16 * ITERS)

        @block.gpsimd
        def _(pool):
            def gather(i, j, again):
                pool.wait_ge(indexed, i * 2 + (j + 1))
                if again and spool is not None:
                    pool.wait_ge(spooled[j], i * 16)
                for q in range(U):
                    if q % 2 == 0:
                        pool.wait_ge(multiplied, i * (2 * PR) + (j * PR + q // 2 + 1))
                        pool.sem_inc(admitted, 1)
                    nc.gpsimd.indirect_dma_start(there[:, j, q, :], None, table,
                                                 bass.IndirectOffsetOnAxis(idx[:, j, q:q + 1], 0)).then_inc(gathered[j][q], 16)

            for j in range(2):
                gather(0, j, False)
            with pool.Fori(1, ITERS) as i:
                for j in range(2):
                    gather(i, j, True)

        @block.vector
        def _(dve):
            dve.sem_inc(hots, 2)
            dve.sem_inc(multiplied, 2 * PR)
            for j in range(2):
                nc.vector.tensor_copy(idx[:, j, :], g["src"][:, j * U:(j + 1) * U]).then_inc(indexed, 1)

            def one_hots(i, j):
                dve.wait_ge(rows_in[j], i * 16 + 16)
                dve.wait_ge(spread, i * (2 * PR) + (j * PR + PR))
                nc.vector.tensor_scalar(hot_t[:, j, :], rows[:, j, :], k["part"][:, 0:1], None, ALU.is_equal).then_inc(hots, 1)

            def combine(i, j):
                at = i * CH + j * U

                def heads(m):
                    dve.wait_ge(multiplied, i * (2 * PR) + (2 * PR + j * PR + m + 1))
                    nc.vector.tensor_reduce(got[:, ds(at + 2 * m, 2), 0, :], prod[:, j, 2 * m:2 * m + 2, :].rearrange("p q (h d) -> p q h d", h=H),
                                            AX.X, ALU.add).then_inc(summed, 1)

                for m in range(PR):
                    for q in (2 * m, 2 * m + 1):
                        dve.wait_ge(gathered[j][q], i * 16 + 16)
                    dve.wait_ge(spread, i * (2 * PR) + (2 * PR + j * PR + m + 1))
                    bank = ps[:, WORK, 0:2 * width].rearrange("p (q f) -> p q f", q=2)
                    if extra:
                        nc.vector.tensor_copy(got[:, ds(at + 2 * m, 2), 1, :], bank[:, :, F:width])
                    nc.vector.tensor_tensor(prod[:, j, 2 * m:2 * m + 2, :], there[:, j, 2 * m:2 * m + 2, 0:F], bank[:, :, 0:F],
                                            ALU.mult).then_inc(multiplied, 1)
                    if m:
                        heads(m - 1)
                heads(PR - 1)
                nc.vector.tensor_copy(idx[:, j, :], g["src"][:, ds(at + CH, U)]).then_inc(indexed, 1)

            one_hots(0, 0)
            with dve.Fori(0, ITERS - 1) as i:
                one_hots(i, 1)
                combine(i, 0)
                one_hots(i + 1, 0)
                combine(i, 1)
            one_hots(ITERS - 1, 1)
            combine(ITERS - 1, 0)
            combine(ITERS - 1, 1)

        @block.tensor
        def _(pe):
            pe.sem_inc(spread, 2 * PR)

            def target_rows(i, j):
                blocks = load_blocks(nc, g["block"], i * CH + j * U, U, NB - 1)
                pe.wait_ge(hots, i * 2 + (j + 3))
                for m in range(PR):
                    pe.wait_ge(multiplied, i * (2 * PR) + (2 * PR + j * PR + m))
                    for q in (2 * m, 2 * m + 1):
                        last = nc.tensor.matmul(ps[:, WORK, (q % 2) * width:(q % 2 + 1) * width], hot_t[:, j, q * P:(q + 1) * P],
                                                here[:, :, :].rearrange("p t f -> p (t f)")[:, ds(blocks[q] * width, width)],
                                                start=True, stop=True, skip_group_check=True)
                    last.then_inc(spread, 1)

            with pe.Fori(0, ITERS) as i:
                for j in range(2):
                    target_rows(i, j)


def hgt_weights(nc, k, g, rec, got, ex, ps):
    with ExitStack() as ctx:
        c = Core(nc, ctx)
        rel = c.sb("rel_in", [P, 2, SQ, H])
        empty = c.sb("empty", [P, NV])
        top1 = c.sb("top1", [P, 1])
        row = c.sb("top_row", [1, P])
        rel_in = [c.sem(f"rel_in{j}") for j in range(2)]
        used, step, turned = c.sem("rel_used"), c.sem("hgt_steps"), c.sem("top_turned")
        spread = c.sem("top_spread")
        block = ctx.enter_context(nc.Block())
        records = rec.rearrange("(p v) w -> p v w", p=P)

        @block.sync
        def _(sp):
            for n in range(4):
                if n >= 2:
                    sp.wait_ge(used, n - 1)
                sp.dma_start(rel[:, n % 2, :, :], records[:, n * SQ:(n + 1) * SQ, 2 + 2 * H:2 + 3 * H]).then_inc(rel_in[n % 2], 16)

        @block.vector
        def _(dve):
            nc.vector.tensor_scalar(empty[:, :], g["loc"][:, :], 0.0, -1e30, ALU.is_lt, ALU.mult).then_inc(step, 1)
            for n in range(4):
                dve.wait_ge(rel_in[n % 2], 16 * (n // 2 + 1))
                at = slice(n * SQ, (n + 1) * SQ)
                nc.vector.scalar_tensor_tensor(ex[:, at, :], got[:, at, 0, :], float(DH) ** -0.5, rel[:, n % 2, :, :], ALU.mult, ALU.mult).then_inc(used, 1)
            dve.wait_ge(step, 1)
            dve.wait_ge(used, 4)
            nc.vector.tensor_tensor(ex[:, :, :], ex[:, :, :], empty[:, :].rearrange("p (v o) -> p v o", o=1).to_broadcast([P, NV, H]), ALU.add).then_inc(step, 1)
            dve.wait_ge(step, 2)
            nc.vector.tensor_reduce(top1[:, :], ex[:, :, :], AX.XY, ALU.max).then_inc(step, 1)
            dve.wait_ge(turned, 1)
            nc.vector.tensor_reduce(row[:, 0:1], ps[0:1, 0, 0:P], AX.X, ALU.max).then_inc(step, 1)
            dve.wait_ge(spread, 1)
            nc.vector.tensor_scalar(top1[:, :], ps[:, 1, 0:1], -1.0, None, ALU.mult).then_inc(step, 1)

        @block.tensor
        def _(pe):
            pe.wait_ge(step, 3)
            nc.tensor.transpose(ps[0:1, 0, 0:P], top1[:, :], k["ident"][:, :]).then_inc(turned, 1)
            pe.wait_ge(step, 4)
            nc.tensor.matmul(ps[:, 1, 0:1], k["ones"][0:1, :], row[:, 0:1], start=True, stop=True).then_inc(spread, 1)

        @block.scalar
        def _(act):
            act.wait_ge(step, 5)
            nc.scalar.activation(ex[:, :, :], ex[:, :, :], ACT.Exp, bias=top1[:, 0:1])


def hgt_messages(nc, k, g, ex, spool, ps):
    tag = "2m"
    with ExitStack() as ctx:
        c = Core(nc, ctx)
        val = c.sb("val" + tag, [P, 2, U, F])
        msg = c.sb("msg" + tag, [P, 2, U, F])
        hot = c.sb("hot" + tag, [P, 2, U, P])
        val_in = [c.sem(f"val_in{j}" + tag) for j in range(2)]
        multiplied, weighted, added = c.sem("multiplied" + tag), c.sem("hotted" + tag), c.sem("added" + tag)
        block = ctx.enter_context(nc.Block())
        CH = 2 * U

        @block.sync
        def _(sp):
            with sp.Fori(0, ITERS) as i:
                for j in range(2):
                    sp.wait_ge(multiplied, i * 2 + (j + 1))
                    sp.dma_start(val[:, j, :, :], spool[:, ds(i * CH + j * U, U), :]).then_inc(val_in[j], 16)

        @block.vector
        def _(dve):
            dve.sem_inc(multiplied, 2)
            with dve.Fori(0, ITERS) as i:
                for j in range(2):
                    at = i * CH + j * U
                    dve.wait_ge(added, i * 2 + (j + 1))
                    for q in range(U):
                        nc.vector.tensor_scalar(hot[:, j, q, :], k["iota"][:, :], g["loc"][:, ds(at + q, 1)], None, ALU.is_equal)
                    dve.wait_ge(val_in[j], i * 16 + 16)
                    nc.vector.tensor_tensor(msg[:, j, :, :].rearrange("p q (h d) -> p (q h) d", h=H), val[:, j, :, :].rearrange("p q (h d) -> p (q h) d", h=H),
                                            ex[:, ds(at, U), :].rearrange("p q (h o) -> p (q h) o", o=1).to_broadcast([P, U * H, DH]),
                                            ALU.mult).then_inc(multiplied, 1)

        @block.tensor
        def _(pe):
            pe.sem_inc(added, 2)
            zero_accumulators(nc, k, ps)
            with pe.Fori(0, ITERS) as i:
                for j in range(2):
                    at = i * CH + j * U
                    blocks = load_blocks(nc, g["block"], at, U, NB - 1)
                    pe.wait_ge(multiplied, i * 2 + (j + 3))
                    for q in range(U):
                        nc.tensor.matmul(wide(ps)[:, ds(blocks[q] * F, F)], hot[:, j, q, :], msg[:, j, q, :],
                                         start=False, stop=True, skip_group_check=True)
                        last = nc.tensor.matmul(wide(ps)[:, ds(blocks[q] * H + NP, H)], hot[:, j, q, :], ex[:, ds(at + q, 1), :].rearrange("p o h -> p (o h)"),
                                                start=False, stop=True, skip_group_check=True)
                    last.then_inc(added, 1)


def type_rows(nc, k, w, kinds, tet, ps):
    T = 8
    with ExitStack() as ctx:
        c = Core(nc, ctx)
        kind = c.sb("node_kind", [T, NP], i32)
        hot = c.sb("node_kind_hot", [T, NP])
        padded, loaded, hotted, made = c.sem("kind_padded"), c.sem("kind_loaded"), c.sem("kind_hot"), c.sem("tet_made")
        block = ctx.enter_context(nc.Block())

        @block.sync
        def _(sp):
            sp.wait_ge(padded, 1)
            sp.dma_start(kind[:, 0:N], kinds.rearrange("(o n) -> o n", o=1).to_broadcast([T, N])).then_inc(loaded, 16)

        @block.vector
        def _(dve):
            nc.vector.memset(kind[:, :], -1).then_inc(padded, 1)
            dve.wait_ge(loaded, 16)
            nc.vector.tensor_scalar(hot[:, :], kind[:, :], k["part"][0:T, 0:1], None, ALU.is_equal).then_inc(hotted, 1)
            dve.wait_ge(made, 1)
            nc.vector.tensor_copy(tet[:, :], wide(ps)[:, 0:NP])

        @block.tensor
        def _(pe):
            pe.wait_ge(hotted, 1)
            for a, b in SPANS:
                last = nc.tensor.matmul(wide(ps)[:, a:b], w["type_emb"][:, :], hot[:, a:b], start=True, stop=True)
            last.then_inc(made, 1)


def project(nc, k, parts, bias, add, out, ps, tag):
    with ExitStack() as ctx:
        c = Core(nc, ctx)
        made, kept = c.sem("proj_made" + tag), c.sem("proj_kept" + tag)
        block = ctx.enter_context(nc.Block())

        @block.tensor
        def _(pe):
            for a, b in SPANS:
                for n, (wt, xt) in enumerate(parts):
                    last = nc.tensor.matmul(wide(ps)[:, a:b], wt, xt[:, a:b], start=n == 0, stop=n == len(parts) - 1)
            last.then_inc(made, 1)

        @block.vector
        def _(dve):
            dve.wait_ge(made, 1)
            if add is None:
                nc.vector.tensor_scalar(out[:, :], wide(ps)[:, 0:NP], bias, None, ALU.add)
            else:
                nc.vector.scalar_tensor_tensor(out[:, :], wide(ps)[:, 0:NP], bias, add[:, :], ALU.add, ALU.add)


def elu_into(nc, xt, y, low, gamma, beta):
    with ExitStack() as ctx:
        c = Core(nc, ctx)
        step, done = c.sem("elu_steps"), c.sem("elu_exp")
        block = ctx.enter_context(nc.Block())

        @block.vector
        def _(dve):
            nc.vector.tensor_scalar(y[:, :], y[:, :], gamma, beta, ALU.mult, ALU.add).then_inc(step, 1)
            dve.wait_ge(step, 1)
            nc.vector.tensor_scalar(low[:, :], y[:, :], 0.0, None, ALU.min).then_inc(step, 1)
            nc.vector.scalar_tensor_tensor(xt[:, :], y[:, :], 0.0, xt[:, :], ALU.max, ALU.add).then_inc(step, 1)
            dve.wait_ge(done, 1)
            dve.wait_ge(step, 3)
            nc.vector.scalar_tensor_tensor(xt[:, :], low[:, :], -1.0, xt[:, :], ALU.add, ALU.add)

        @block.scalar
        def _(act):
            act.wait_ge(step, 2)
            nc.scalar.activation(low[:, :], low[:, :], ACT.Exp).then_inc(done, 1)


def layer2(nc, k, w, g, rec, table, spool, xt, kinds, ps):
    with ExitStack() as ctx:
        c = Core(nc, ctx)
        ht = c.sb("ht2", [P, NP])
        tet = c.sb("tet", [P, NP])
        layernorm(nc, k, xt, ht, ps, "2")
        type_rows(nc, k, w, kinds, tet, ps)
        with ExitStack() as ectx:
            e = Core(nc, ectx)
            ex = e.sb("ex", [P, NV, H])
            with ExitStack() as gctx:
                got = Core(nc, gctx).sb("got2", [P, NV, 1, H])
                with ExitStack() as rctx:
                    rows = Core(nc, rctx).sb("rows2", [P, NB, 2 * F])
                    node_rows(nc, k, [(ht, w["kv_h"][:, :]), (tet, w["kv_t"][:, :])], 2 * F, None, rows, ps, "2kv", dram=table)
                with ExitStack() as rctx:
                    here = Core(nc, rctx).sb("here2", [P, NB, F])
                    node_rows(nc, k, [(ht, w["Wq_h"][:, :]), (tet, w["Wq_t"][:, :])], F, None, here, ps, "2q")
                    edge_products(nc, k, g, table, 2 * F, here, F, got, spool, ps, "2")
                hgt_weights(nc, k, g, rec, got, ex, ps)
            hgt_messages(nc, k, g, ex, spool, ps)
        acc_t = c.sb("acc_t2", [P, NP])
        sums = c.sb("sums2", [P, NB * H])

        def normalise(dve, rows, out):
            nc.vector.tensor_scalar(sums[:, :], sums[:, :], 1e-16, None, ALU.add).then_inc(out, 1)
            dve.wait_ge(out, 3)
            nc.vector.reciprocal(sums[:, :], sums[:, :]).then_inc(out, 1)
            dve.wait_ge(out, 4)
            heads = rows[:, :].rearrange("p (g d) -> p g d", d=DH)
            nc.vector.tensor_tensor(heads, heads, sums[:, :].rearrange("p (g o) -> p g o", o=1).to_broadcast([P, NB * H, DH]), ALU.mult).then_inc(out, 1)

        collect(nc, k, ps, acc_t, sums, NB * H, "2", scale=normalise)
        project(nc, k, [(w["l2_Wo"][:, :], acc_t), (w["Wskip_h"][:, :], ht), (w["Wskip_t"][:, :], tet)], w["l2_bo"][:, 0:1], None, acc_t, ps, "2")
        layernorm(nc, k, acc_t, ht, ps, "2b", relu=False)
        elu_into(nc, xt, ht, acc_t, w["l2_gamma"][:, 0:1], w["l2_beta"][:, 0:1])


SEGS = P // H
SEGC = NV // SEGS
SEGE = SEGC * P
BIG = 1.5e38


def segment_rows(nc, k, g, got, row, same, gid_row, gid8, ps):
    with ExitStack() as ctx:
        c = Core(nc, ctx)
        blk = c.sb("blk_f", [1, NV])
        gid = c.sb("gid", [P, NV])
        before = c.sb("last_before", [P, 1])
        inner = c.sb("inner", [P, 1], i32)
        inner_f = c.sb("inner_f", [P, 1])
        ready, spread, ids, turned, kept = c.sem("blk_ready"), c.sem("blk_spread"), c.sem("ids_ready"), c.sem("seg_turned"), c.sem("seg_kept")
        before_set = c.sem("before_set")
        shifted, masks, firsts = c.sem("shifted"), c.sem("masks_made"), c.sem("firsts")
        block = ctx.enter_context(nc.Block())

        @block.gpsimd
        def _(pool):
            nc.gpsimd.iota(inner[:, :], [[1, 1]], base=0, channel_multiplier=1).then_inc(masks, 1)

        @block.vector
        def _(dve):
            nc.vector.tensor_copy(blk[:, :], g["block"][:, :]).then_inc(ready, 1)
            dve.wait_ge(spread, 1)
            for n in range(2):
                half = slice(n * (NV // 2), (n + 1) * (NV // 2))
                nc.vector.scalar_tensor_tensor(gid[:, half], ps[:, n, 0:NV // 2], float(P), g["loc"][:, half], ALU.mult, ALU.add).then_inc(ids, 1)
            dve.wait_ge(ids, 2)
            nc.vector.tensor_copy(gid8[:, :].rearrange("p (c h s) -> p c h s", h=H, s=SEGS),
                                  gid[:, :].rearrange("p (s c) -> p c s", s=SEGS)[:, :, None, :].to_broadcast([P, SEGC, H, SEGS])).then_inc(ids, 1)
            for t in range(SEGC):
                dve.wait_ge(turned, t + 1)
                nc.vector.tensor_copy(row[:, t * P:(t + 1) * P], ps[:, 2 + t % 6, 0:P])
                nc.vector.tensor_copy(gid_row[:, t * P:(t + 1) * P], ps[:, 2 + t % 6, P:2 * P]).then_inc(kept, 1)
            dve.wait_ge(kept, SEGC)
            nc.vector.tensor_tensor(same[:, 1:SEGE], gid_row[:, 1:SEGE], gid_row[:, 0:SEGE - 1], ALU.is_equal)
            dve.wait_ge(masks, 1)
            nc.vector.tensor_scalar(inner[:, :], inner[:, :], SEGS - 1, None, ALU.bitwise_and).then_inc(firsts, 1)
            dve.wait_ge(firsts, 1)
            nc.vector.tensor_scalar(inner_f[:, :], inner[:, :], 0.0, None, ALU.is_gt).then_inc(firsts, 1)
            dve.wait_ge(firsts, 2)
            dve.wait_ge(shifted, 16)
            nc.vector.scalar_tensor_tensor(same[:, 0:1], gid_row[:, 0:1], before[:, 0:1], inner_f[:, :], ALU.is_equal, ALU.mult)

        @block.sync
        def _(sp):
            sp.wait_ge(kept, SEGC)
            sp.wait_ge(before_set, 1)
            sp.dma_start(before[1:P, :], gid_row[0:P - 1, SEGE - 1:SEGE]).then_inc(shifted, 16)

        @block.scalar
        def _(act):
            nc.scalar.activation(before[:, :], k["ones"][:, 0:1], ACT.Copy).then_inc(before_set, 1)

        @block.tensor
        def _(pe):
            pe.wait_ge(ready, 1)
            for n in range(2):
                last = nc.tensor.matmul(ps[:, n, 0:NV // 2], k["ones"][0:1, :], blk[:, n * (NV // 2):(n + 1) * (NV // 2)], start=True, stop=True)
            last.then_inc(spread, 1)
            pe.wait_ge(ids, 3)
            scores = got[:, :, :].rearrange("p v h -> p (v h)")
            for t in range(SEGC):
                if t >= 6:
                    pe.wait_ge(kept, t - 5)
                nc.tensor.transpose(ps[:, 2 + t % 6, 0:P], scores[:, t * P:(t + 1) * P], k["ident"][:, :])
                nc.tensor.transpose(ps[:, 2 + t % 6, P:2 * P], gid8[:, t * P:(t + 1) * P], k["ident"][:, :]).then_inc(turned, 1)


def carried(nc, k, gate, first, carry, local, over, ps, tag, reverse, most):
    with ExitStack() as ctx:
        c = Core(nc, ctx)
        loc_r = c.sb("loc_r" + tag, [1, P])
        over_r = c.sb("over_r" + tag, [1, P])
        run_r = c.sb("run_r" + tag, [1, P + 2])
        turned, step, back = c.sem("carry_turned" + tag), c.sem("carry_steps" + tag), c.sem("carry_back" + tag)
        block = ctx.enter_context(nc.Block())

        @block.tensor
        def _(pe):
            nc.tensor.transpose(ps[0:1, 0, 0:P], local, k["ident"][:, :])
            nc.tensor.transpose(ps[0:1, 0, P:2 * P], over, k["ident"][:, :]).then_inc(turned, 1)
            pe.wait_ge(step, 4)
            at = 2 if reverse else 0
            nc.tensor.matmul(ps[:, 1, 0:1], run_r[:, at:at + P], k["ones"][0:1, 0:1], start=True, stop=True).then_inc(back, 1)

        @block.vector
        def _(dve):
            nc.vector.memset(run_r[:, :], 0.0).then_inc(step, 1)
            dve.wait_ge(turned, 1)
            nc.vector.tensor_copy(loc_r[:, :], ps[0:1, 0, 0:P]).then_inc(step, 1)
            nc.vector.tensor_copy(over_r[:, :], ps[0:1, 0, P:2 * P]).then_inc(step, 1)
            dve.wait_ge(step, 3)
            out, a, b = run_r[:, 1:P + 1], over_r[:, :], loc_r[:, :]
            if reverse:
                out, a, b = out[:, ::-1], a[:, ::-1], b[:, ::-1]
            nc.vector.tensor_tensor_scan(out, a, b, 0.0 if not most else -BIG, ALU.min if most else ALU.mult,
                                         ALU.max if most else ALU.add).then_inc(step, 1)
            dve.wait_ge(back, 1)
            nc.vector.tensor_copy(carry[:, :], ps[:, 1, 0:1])


def spans_of(nc, k, row, same, gate, out, ps, tag, most):
    with ExitStack() as ctx:
        c = Core(nc, ctx)
        whole = c.sb("whole" + tag, [P, 1])
        over = c.sb("over" + tag, [P, 1])
        carry = c.sb("carry" + tag, [P, 1])
        nxt = c.sb("next" + tag, [P, 1])
        ops = (ALU.min, ALU.max) if most else (ALU.mult, ALU.add)
        neutral = -BIG if most else 0.0

        with ExitStack() as s:
            step, moved, zeroed = Core(nc, s).sem("span_a" + tag), Core(nc, s).sem("span_m" + tag), Core(nc, s).sem("span_z" + tag)
            block = s.enter_context(nc.Block())

            @block.sync
            def _(sp):
                sp.wait_ge(zeroed, 1)
                sp.dma_start(nxt[0:P - 1, :], same[1:P, 0:1]).then_inc(moved, 16)
                sp.wait_ge(moved, 16)

            @block.vector
            def _(dve):
                nc.vector.memset(nxt[:, :], 0.0).then_inc(zeroed, 1)
                if most:
                    nc.vector.tensor_scalar(gate[:, :], same[:, :], 2 * BIG, BIG, ALU.mult, ALU.subtract).then_inc(step, 1)
                else:
                    nc.vector.tensor_copy(gate[:, :], same[:, :]).then_inc(step, 1)
                nc.vector.tensor_reduce(whole[:, :], same[:, :], AX.X, ALU.min).then_inc(step, 1)
                dve.wait_ge(step, 2)
                nc.vector.tensor_tensor_scan(out[:, :], gate[:, :], row[:, :], neutral, *ops).then_inc(step, 1)
                if most:
                    nc.vector.tensor_scalar(over[:, :], whole[:, :], 2 * BIG, BIG, ALU.mult, ALU.subtract)
                else:
                    nc.vector.tensor_copy(over[:, :], whole[:, :])
        carried(nc, k, gate, same, carry, out[:, SEGE - 1:SEGE], over[:, :], ps, tag + "f", False, most)
        with ExitStack() as s:
            step = Core(nc, s).sem("span_b" + tag)
            block = s.enter_context(nc.Block())

            @block.vector
            def _(dve):
                nc.vector.tensor_tensor_scan(out[:, :], gate[:, :], row[:, :], carry[:, 0:1], *ops).then_inc(step, 1)
                dve.wait_ge(step, 1)
                nc.vector.tensor_copy(gate[:, 0:SEGE - 1], same[:, 1:SEGE]).then_inc(step, 1)
                nc.vector.tensor_copy(gate[:, SEGE - 1:SEGE], nxt[:, :]).then_inc(step, 1)
                dve.wait_ge(step, 3)
                nc.vector.scalar_tensor_tensor(out[:, :], gate[:, :], 0.0, out[:, :], ALU.is_equal, ALU.mult).then_inc(step, 1)
                nc.vector.tensor_reduce(over[:, :], gate[:, :], AX.X, ALU.min).then_inc(step, 1)
                dve.wait_ge(step, 5)
                nc.vector.tensor_tensor_scan(whole_row(out), whole_row(gate), whole_row(out), 0.0, ALU.mult, ALU.add).then_inc(step, 1)

        carried(nc, k, gate, same, carry, out[:, 0:1], over[:, :], ps, tag + "b", True, False)
        with ExitStack() as s:
            step = Core(nc, s).sem("span_c" + tag)
            block = s.enter_context(nc.Block())

            @block.vector
            def _(dve):
                nc.vector.tensor_tensor_scan(whole_row(gate), whole_row(gate), k["zeros"][:, 0:1].to_broadcast([P, SEGE]), carry[:, 0:1], ALU.mult, ALU.add).then_inc(step, 1)
                dve.wait_ge(step, 1)
                nc.vector.tensor_tensor(out[:, :], out[:, :], gate[:, :], ALU.add)


def whole_row(t):
    return t[:, ::-1]


def softmax_mass(nc, k, row, same, gate, tmp, ps):
    def alone(fn):
        with ExitStack() as s:
            c = Core(nc, s)
            block = s.enter_context(nc.Block())
            fn(block, c)

    spans_of(nc, k, row, same, gate, tmp, ps, "x", True)

    def exps(block, c):
        centred = c.sem("row_centred")

        @block.vector
        def _(dve):
            nc.vector.tensor_tensor(row[:, :], row[:, :], tmp[:, :], ALU.subtract).then_inc(centred, 1)

        @block.scalar
        def _(act):
            act.wait_ge(centred, 1)
            nc.scalar.activation(row[:, :], row[:, :], ACT.Exp)

    alone(exps)
    spans_of(nc, k, row, same, gate, tmp, ps, "s", False)

    def divide(block, c):
        inverted = c.sem("row_inverted")

        @block.vector
        def _(dve):
            nc.vector.reciprocal(tmp[:, :], tmp[:, :]).then_inc(inverted, 1)
            dve.wait_ge(inverted, 1)
            nc.vector.tensor_tensor(row[:, :], row[:, :], tmp[:, :], ALU.mult)

    alone(divide)


def rows_back(nc, k, row, got, ps):
    with ExitStack() as ctx:
        c = Core(nc, ctx)
        turned, kept = c.sem("back_turned"), c.sem("back_kept")
        block = ctx.enter_context(nc.Block())
        dest = got[:, :, :].rearrange("p (s c) h -> p c h s", s=SEGS)

        @block.tensor
        def _(pe):
            for t in range(SEGC):
                if t >= 8:
                    pe.wait_ge(kept, t - 7)
                nc.tensor.transpose(ps[:, t % 8, 0:P], row[:, t * P:(t + 1) * P], k["ident"][:, :]).then_inc(turned, 1)

        @block.vector
        def _(dve):
            for t in range(SEGC):
                dve.wait_ge(turned, t + 1)
                nc.vector.tensor_copy(dest[:, t, :, :], ps[:, t % 8, 0:P].rearrange("p (h s) -> p h s", h=H)).then_inc(kept, 1)


def weight_sums(nc, k, g, got, ps):
    with ExitStack() as ctx:
        c = Core(nc, ctx)
        hot = c.sb("hot3m", [P, 2, U, P])
        weighted, added = c.sem("hotted3m"), c.sem("added3m")
        block = ctx.enter_context(nc.Block())
        CH = 2 * U

        @block.vector
        def _(dve):
            with dve.Fori(0, ITERS) as i:
                for j in range(2):
                    dve.wait_ge(added, i * 2 + (j + 1))
                    for q in range(U):
                        last = nc.vector.tensor_scalar(hot[:, j, q, :], k["iota"][:, :], g["loc"][:, ds(i * CH + (j * U + q), 1)], None, ALU.is_equal)
                    last.then_inc(weighted, 1)

        @block.tensor
        def _(pe):
            pe.sem_inc(added, 2)
            nc.tensor.matmul(ps[:, 0, 0:NB * H], k["zeros"][:, :], k["zeros4"][:, 0:NB * H], start=True, stop=True, skip_group_check=True)
            with pe.Fori(0, ITERS) as i:
                for j in range(2):
                    at = i * CH + j * U
                    blocks = load_blocks(nc, g["block"], at, U, NB - 1)
                    pe.wait_ge(weighted, i * 2 + (j + 1))
                    for q in range(U):
                        last = nc.tensor.matmul(wide(ps)[:, ds(blocks[q] * H, H)], hot[:, j, q, :], got[:, ds(at + q, 1), :].rearrange("p o h -> p (o h)"),
                                                start=False, stop=True, skip_group_check=True)
                    last.then_inc(added, 1)


def edge_scores(nc, k, rec, pairs, got):
    with ExitStack() as ctx:
        c = Core(nc, ctx)
        term = c.sb("terms_in", [P, 2, SQ, 2 * H])
        score = c.sb("score", [P, SQ, H])
        term_in = [c.sem(f"term_in{j}") for j in range(2)]
        a1, a2, a3 = c.sem("score_a"), c.sem("score_b"), c.sem("score_c")
        block = ctx.enter_context(nc.Block())
        records = rec.rearrange("(p v) w -> p v w", p=P)

        @block.sync
        def _(sp):
            for n in range(4):
                if n >= 2:
                    sp.wait_ge(a3, n - 1)
                sp.dma_start(term[:, n % 2, :, :], records[:, n * SQ:(n + 1) * SQ, 2:2 + 2 * H]).then_inc(term_in[n % 2], 16)

        by_run = got[:, :, :].rearrange("p v h -> p (v h)").rearrange("p (c h s) -> p s c h", h=H, s=SEGS)

        @block.vector
        def _(dve):
            for n in range(4):
                dve.wait_ge(term_in[n % 2], 16 * (n // 2 + 1))
                at = slice(n * SQ, (n + 1) * SQ)
                nc.vector.scalar_tensor_tensor(score[:, :, :], pairs[:, at, 0, :], float(DH) ** -0.5, term[:, n % 2, :, 0:H], ALU.mult, ALU.add).then_inc(a1, 1)
                dve.wait_ge(a1, n + 1)
                nc.vector.tensor_tensor(score[:, :, :], score[:, :, :], pairs[:, at, 1, :], ALU.mult).then_inc(a2, 1)
                dve.wait_ge(a2, n + 1)
                nc.vector.tensor_tensor(by_run[:, n * 4:(n + 1) * 4, :, :], score[:, :, :].rearrange("p (s c) h -> p s c h", c=SEGC),
                                        term[:, n % 2, :, H:2 * H].rearrange("p (s c) h -> p s c h", c=SEGC), ALU.add).then_inc(a3, 1)
                dve.wait_ge(a3, n + 1)


def keep_sums(nc, sums, ps):
    with ExitStack() as ctx:
        block = ctx.enter_context(nc.Block())

        @block.vector
        def _(dve):
            nc.vector.tensor_copy(sums[:, :], ps[:, 0, 0:NB * H])


def conservation(nc, k, w, vec, here, ps):
    with ExitStack() as ctx:
        c = Core(nc, ctx)
        row = c.sb("vec_row", [1, NP])
        hid = c.sb("vec_hid", [HIDC, NP])
        padded, loaded, made, kept, out, biased = c.sem("vec_padded"), c.sem("vec_loaded"), c.sem("vec_made"), c.sem("vec_kept"), c.sem("vec_out"), c.sem("vec_biased")
        block = ctx.enter_context(nc.Block())

        @block.sync
        def _(sp):
            sp.wait_ge(padded, 1)
            sp.dma_start(row[:, 0:N], vec.rearrange("n o -> o n")).then_inc(loaded, 16)

        @block.vector
        def _(dve):
            nc.vector.memset(row[:, :], 0.0).then_inc(padded, 1)
            dve.wait_ge(out, 1)
            nc.vector.tensor_tensor(here[:, :, F:F + H], ps[:, 7, 0:NB * H].rearrange("p (t h) -> p t h", h=H),
                                    w["bc2"][:, None, :].to_broadcast([P, NB, H]), ALU.add).then_inc(biased, 1)

        @block.tensor
        def _(pe):
            pe.wait_ge(loaded, 16)
            for a, b in SPANS:
                last = nc.tensor.matmul(wide(ps)[0:HIDC, a:b], w["Wc1"][:, :], row[:, a:b], start=True, stop=True)
            last.then_inc(made, 1)
            pe.wait_ge(kept, 1)
            for t in range(NB):
                last = nc.tensor.matmul(ps[:, 7, t * H:(t + 1) * H], hid[:, t * P:(t + 1) * P], w["Wc2"][:, :], start=True, stop=True, skip_group_check=True)
            last.then_inc(out, 1)

        @block.scalar
        def _(act):
            act.wait_ge(made, 1)
            nc.scalar.activation(hid[:, :], wide(ps)[0:HIDC, 0:NP], ACT.Relu, bias=w["bc1"][:, 0:1]).then_inc(kept, 1)
            act.wait_ge(biased, 1)
            nc.scalar.activation(here[:, :, F:F + H], here[:, :, F:F + H], ACT.Sigmoid)


def weigh_values(nc, k, v_rows, sums, acc_t, ps):
    with ExitStack() as ctx:
        c = Core(nc, ctx)
        turned, done = c.sem("wv_turned"), c.sem("wv_done")
        block = ctx.enter_context(nc.Block())

        @block.vector
        def _(dve):
            heads = v_rows[:, :, :].rearrange("p t (h d) -> p (t h) d", d=DH)
            nc.vector.tensor_tensor(heads, heads, sums[:, :].rearrange("p (g o) -> p g o", o=1).to_broadcast([P, NB * H, DH]), ALU.mult).then_inc(done, 1)
            dve.wait_ge(turned, 1)
            nc.vector.tensor_copy(acc_t[:, :], wide(ps)[:, 0:NP])

        @block.tensor
        def _(pe):
            pe.wait_ge(done, 1)
            for t in range(NB):
                last = nc.tensor.transpose(wide(ps)[:, t * P:(t + 1) * P], v_rows[:, t, :], k["ident"][:, :])
            last.then_inc(turned, 1)


def scale_add_store(nc, k, xt, y, gamma, beta, out, ps):
    LAST = N - (NB - 1) * P
    with ExitStack() as ctx:
        c = Core(nc, ctx)
        rows = c.sb("out_rows", [P, NB, F])
        step, turned, stored = c.sem("fin_steps"), c.sem("fin_turned"), c.sem("out_stored")
        block = ctx.enter_context(nc.Block())

        @block.vector
        def _(dve):
            nc.vector.tensor_scalar(y[:, :], y[:, :], gamma, beta, ALU.mult, ALU.add).then_inc(step, 1)
            dve.wait_ge(step, 1)
            nc.vector.tensor_tensor(xt[:, :], xt[:, :], y[:, :], ALU.add).then_inc(step, 1)
            dve.wait_ge(turned, 1)
            nc.vector.tensor_copy(rows[:, :, :].rearrange("p t f -> p (t f)"), wide(ps)[:, 0:NP]).then_inc(step, 1)

        @block.tensor
        def _(pe):
            pe.wait_ge(step, 2)
            for t in range(NB):
                last = nc.tensor.transpose(wide(ps)[:, t * P:(t + 1) * P], xt[:, t * P:(t + 1) * P], k["ident"][:, :])
            last.then_inc(turned, 1)

        @block.sync
        def _(sp):
            sp.wait_ge(step, 3)
            sp.dma_start(out[0:(NB - 1) * P, :].rearrange("(t p) f -> p t f", p=P), rows[:, 0:NB - 1, :]).then_inc(stored, 16)
            sp.dma_start(out[(NB - 1) * P:N, :], rows[0:LAST, NB - 1, :]).then_inc(stored, 16)
            sp.wait_ge(stored, 32)


def layer3(nc, k, w, g, rec, table, xt, vec, out, ps):
    with ExitStack() as ctx:
        c = Core(nc, ctx)
        ht = c.sb("ht3", [P, NP])
        sums = c.sb("sums3", [P, NB * H])
        layernorm(nc, k, xt, ht, ps, "3")
        with ExitStack() as ectx:
            got = Core(nc, ectx).sb("got3", [P, NV, H])
            with ExitStack() as gctx:
                pairs = Core(nc, gctx).sb("pairs3", [P, NV, 2, H])
                with ExitStack() as rctx:
                    here = Core(nc, rctx).sb("here3", [P, NB, F + H])
                    node_rows(nc, k, [(ht, w["l3_Wq"][:, :])], F, w["l3_bq"][:, :], here, ps, "3q", dram=table)
                    node_rows(nc, k, [(ht, w["l3_Wk"][:, :])], F, w["l3_bk"][:, :], here, ps, "3k")
                    conservation(nc, k, w, vec, here, ps)
                    edge_products(nc, k, g, table, F, here, F + H, pairs, None, ps, "3")
                edge_scores(nc, k, rec, pairs, got)
            with ExitStack() as rctx:
                r = Core(nc, rctx)
                row = r.sb("score_rows", [P, SEGE])
                same = r.sb("same", [P, SEGE])
                gate = r.sb("gate", [P, SEGE])
                tmp = r.sb("span", [P, SEGE])
                segment_rows(nc, k, g, got, row, same, gate, tmp, ps)
                softmax_mass(nc, k, row, same, gate, tmp, ps)
                rows_back(nc, k, row, got, ps)
            weight_sums(nc, k, g, got, ps)
        acc_t = c.sb("acc_t3", [P, NP])
        with ExitStack() as rctx:
            v_rows = Core(nc, rctx).sb("v_rows", [P, NB, F])
            keep_sums(nc, sums, ps)
            node_rows(nc, k, [(ht, w["l3_Wv"][:, :])], F, w["l3_bv"][:, :], v_rows, ps, "3v")
            weigh_values(nc, k, v_rows, sums, acc_t, ps)
        project(nc, k, [(w["l3_Wo"][:, :], acc_t)], w["l3_bo"][:, 0:1], ht, acc_t, ps, "3")
        layernorm(nc, k, acc_t, ht, ps, "3b", relu=False)
        scale_add_store(nc, k, xt, ht, w["l3_gamma"][:, 0:1], w["l3_beta"][:, 0:1], out, ps)


def fill_records(nc, feat, feat_s, rec, rec_s):
    with ExitStack() as ctx:
        c = Core(nc, ctx)
        zeroed, marked, stored = c.sem("feat_zeroed"), c.sem("feat_marked"), c.sem("rec_filled")
        block = ctx.enter_context(nc.Block())

        @block.vector
        def _(dve):
            nc.vector.memset(feat[:, :, :], 0.0).then_inc(zeroed, 1)
            nc.vector.memset(feat_s[:, :, :], 0.0).then_inc(zeroed, 1)
            dve.wait_ge(zeroed, 2)
            nc.vector.memset(feat[:, :, 1:2], -1.0).then_inc(marked, 1)
            nc.vector.memset(feat_s[:, :, 1:2], -1.0).then_inc(marked, 1)

        @block.sync
        def _(sp):
            sp.wait_ge(marked, 2)
            sp.dma_start(rec.rearrange("(p v) w -> p v w", p=P), feat[:, :, :]).then_inc(stored, 16)
            sp.dma_start(rec_s.rearrange("(p v) w -> p v w", p=P), feat_s[:, :, :]).then_inc(stored, 16)
            sp.wait_ge(stored, 32)


def clear_index(nc, indices):
    with ExitStack() as ctx:
        block = ctx.enter_context(nc.Block())

        @block.vector
        def _(dve):
            for g in indices:
                nc.vector.memset(g["src"][:, NV:NV + 2 * U], 0)


def build(nc, a, out):
    with ExitStack() as ctx:
        top = Core(nc, ctx)
        ps = top.psum("ps", [P, 8, 512])
        k = constants(nc, top)
        rec = top.dram("rec", [P * (NV + 1), W_REC])
        rec_s = top.dram("rec_s", [P * (NV + 1), 2])
        by_dst, by_src = {}, {}
        for name, g in (("d", by_dst), ("s", by_src)):
            g["block"] = top.sb("block_" + name, [1, NV], i32)
            g["src"] = top.sb("gather_" + name, [P, NV + 2 * U], i32)
            g["loc"] = top.sb("loc_" + name, [P, NV])
            g["loc_row"] = top.dram("loc_row_" + name, [NV * P], bf16)
        KEYS = -(-NC // P) * P * P
        rows_d = (top.dram("key_row_d", [KEYS]), top.dram("lo_row_d", [KEYS], bf16))
        rows_s = (top.dram("key_row_s", [KEYS]), top.dram("lo_row_s", [KEYS], bf16))
        with ExitStack() as sctx:
            s = Core(nc, sctx)
            feat = s.sb("feat", [P, NV + 1, W_REC])
            feat_s = s.sb("feat_s", [P, NV + 1, 2])
            fill_records(nc, feat, feat_s, rec, rec_s)
            load_keys(nc, k, a["src"], feat[:, 0:NC, 0], feat_s[:, 0:NC, 1], *rows_s, ps, "s")
            load_keys(nc, k, a["dst"], feat_s[:, 0:NC, 0], feat[:, 0:NC, 1], *rows_d, ps, "d")
            edge_terms(nc, k, a, feat, ps)
            sort_edges(nc, k, feat_s[:, 0:NC, 0], feat[:, 0:NC, 1], lambda c, n: feat[:, ds(c, n), :], rec, by_dst["block"], ps, rows_d, "d")
            sort_edges(nc, k, feat[:, 0:NC, 0], feat_s[:, 0:NC, 1], lambda c, n: feat_s[:, ds(c, n), :], rec_s, by_src["block"], ps, rows_s, "s")
        clear_index(nc, [by_dst, by_src])
        sorted_index(nc, k, rec, by_dst["src"][:, 0:NV], by_dst["loc"], by_dst["loc_row"], ps, "id")
        sorted_index(nc, k, rec_s, by_src["src"][:, 0:NV], by_src["loc"], by_src["loc_row"], ps, "is")
        w = load_weights(nc, top, a)
        xt = top.sb("xt", [P, NP])
        load_nodes(nc, k, a["x"], xt, ps)
        table2 = top.dram("table_wide", [NP, 2 * F])
        table1 = top.dram("table_narrow", [NP, F])
        spool = top.dram("value_spool", [P, NV, F])
        layer0(nc, k, w, by_dst, table2, xt, ps)
        layer1(nc, k, w, by_src, table1, xt, ps)
        layer2(nc, k, w, by_dst, rec, table2, spool, xt, a["node_type_8"], ps)
        layer3(nc, k, w, by_dst, rec, table1, xt, a["node_vec1"], out, ps)


def kernel(**inputs):
    import concourse.bacc as bacc
    from concourse.bass_utils import run_bass_kernel_spmd

    nc = bacc.Bacc("TRN2", target_bir_lowering=False, num_devices=1)
    arrays, a = {}, {}
    for name, value in inputs.items():
        v = np.asarray(value)
        if name in ("L1_gnn_W1", "L1_gnn_W2"):
            v = v.T
        if v.ndim == 0:
            v = v.reshape(1)
        v = np.ascontiguousarray(v)
        arrays["in_" + name] = v
        a[name] = nc.dram_tensor("in_" + name, v.shape, mybir.dt.from_np(v.dtype), kind="ExternalInput").ap()
    out = nc.dram_tensor("out", (N, F), f32, kind="ExternalOutput").ap()
    build(nc, a, out)
    result = run_bass_kernel_spmd(nc, [arrays], core_ids=[0])
    return result.results[0]["out"]
```

```python
import numpy as np
import concourse.bass as bass
from concourse import mybir
from contextlib import ExitStack

f32 = mybir.dt.float32
i32 = mybir.dt.int32
bf16 = mybir.dt.bfloat16
ALU = mybir.AluOpType
ACT = mybir.ActivationFunctionType
AX = mybir.AxisListType

P = 128
N = 3125
E = 103125
F = 128
NB = -(-N // P)
NP = NB * P
H = 8
DH = F // H
NC = -(-E // P)
TAIL = E - (NC - 1) * P
NV = -(-((E + NB * (P - 1)) // P) // 16) * 16
ROWS = NV * P
PADHI = 30
ds = bass.ds


class Core:

    spent = []

    def __init__(self, nc, ctx):
        self.nc, self.ctx, self.sems = nc, ctx, []
        ctx.callback(self.retire)

    def retire(self):
        self.spent.extend(self.sems)
        if len(self.spent) > 110:
            self.nc.clear_and_free_semaphores(list(self.spent))
            self.nc.all_engine_barrier()
            self.spent.clear()

    def sb(self, name, shape, dt=f32):
        return self.ctx.enter_context(self.nc.sbuf_tensor(name, shape, dt))

    def sem(self, name):
        self.sems.append(self.nc.alloc_semaphore(name=name))
        return self.sems[-1]

    def psum(self, name, shape):
        return self.ctx.enter_context(self.nc.psum_tensor(name, shape, f32))

    def dram(self, name, shape, dt=f32):
        return self.nc.dram_tensor(name, shape, dt, kind="Internal").ap()


def constants(nc, top):
    k = {}
    k["ones"] = top.sb("ones", [P, P])
    k["zeros"] = top.sb("zeros", [P, P])
    k["zeros4"] = top.sb("zeros4", [P, 512])
    k["mean_of"] = top.sb("mean_of", [P, P])
    k["eps"] = top.sb("eps", [P, 1])
    k["ident"] = top.sb("ident", [P, P])
    k["tri"] = top.sb("tri", [P, P])
    k["before"] = top.sb("before", [P, P])
    k["iota"] = top.sb("iota", [P, P])
    k["iota_bf"] = top.sb("iota_bf", [P, P], bf16)
    k["part"] = top.sb("part", [P, 1])
    with ExitStack() as ctx:
        c = Core(nc, ctx)
        filled = c.sem("filled")
        block = ctx.enter_context(nc.Block())

        @block.gpsimd
        def _(pool):
            nc.gpsimd.memset(k["ones"][:, :], 1.0).then_inc(filled, 1)
            nc.gpsimd.memset(k["ident"][:, :], 0.0).then_inc(filled, 1)
            nc.gpsimd.iota(k["iota"][:, :], [[1, P]], base=0, channel_multiplier=0,
                           allow_small_or_imprecise_dtypes=True).then_inc(filled, 1)
            nc.gpsimd.iota(k["iota_bf"][:, :], [[1, P]], base=0, channel_multiplier=0,
                           allow_small_or_imprecise_dtypes=True).then_inc(filled, 1)
            nc.gpsimd.iota(k["part"][:, :], [[1, 1]], base=0, channel_multiplier=1,
                           allow_small_or_imprecise_dtypes=True).then_inc(filled, 1)
            nc.gpsimd.memset(k["zeros"][:, :], 0.0)
            nc.gpsimd.memset(k["zeros4"][:, :], 0.0)
            nc.gpsimd.memset(k["mean_of"][:, :], 1.0 / F)
            nc.gpsimd.memset(k["eps"][:, :], 1e-5)
            pool.wait_ge(filled, 5)
            nc.gpsimd.affine_select(out=k["ident"][:, :], in_=k["ident"][:, :], compare_op=ALU.not_equal,
                                    fill=1.0, base=0, pattern=[[-1, P]], channel_multiplier=1).then_inc(filled, 1)
            nc.gpsimd.affine_select(out=k["tri"][:, :], in_=k["ones"][:, :], compare_op=ALU.is_gt,
                                    fill=0.0, base=0, pattern=[[1, P]], channel_multiplier=-1).then_inc(filled, 1)
            nc.gpsimd.affine_select(out=k["before"][:, :], in_=k["ones"][:, :], compare_op=ALU.is_gt,
                                    fill=0.0, base=0, pattern=[[-1, P]], channel_multiplier=1).then_inc(filled, 1)
    return k


def load_keys(nc, k, key_in, key_col, lo_col, key_row, lo_row, ps, tag):
    NT = -(-NC // P)
    with ExitStack() as ctx:
        c = Core(nc, ctx)
        raw = c.sb("key_raw" + tag, [P, NT, P], i32)
        rows = c.sb("key_rows" + tag, [P, NT, P])
        lo = c.sb("key_lo" + tag, [P, NT, P], i32)
        lo_bf = c.sb("key_lo_bf" + tag, [P, NT, P], bf16)
        lo_f = c.sb("key_lo_f" + tag, [P, NT, P])
        padded = c.sem("padded" + tag)
        loaded = c.sem("keys_loaded" + tag)
        cast = c.sem("keys_cast" + tag)
        turned = c.sem("keys_turned" + tag)
        stored = c.sem("keys_stored" + tag)
        block = ctx.enter_context(nc.Block())
        full = NC - 1 - (NT - 1) * P

        @block.sync
        def _(sp):
            sp.wait_ge(padded, 1)
            sp.dma_start(raw[:, 0:NT - 1, :], key_in[0:(NT - 1) * P * P].rearrange("(t q p) -> q t p", q=P, p=P)).then_inc(loaded, 16)
            sp.dma_start(raw[0:full, NT - 1, :], key_in[(NT - 1) * P * P:(NC - 1) * P].rearrange("(q p) -> q p", p=P)).then_inc(loaded, 16)
            sp.dma_start(raw[full:full + 1, NT - 1, 0:TAIL], key_in[(NC - 1) * P:E].rearrange("(q p) -> q p", q=1)).then_inc(loaded, 16)
            sp.wait_ge(cast, 3)
            sp.dma_start(key_row[0:NT * P * P].rearrange("(t q p) -> q t p", q=P, p=P), rows[:, :, :]).then_inc(stored, 16)
            sp.dma_start(lo_row[0:NT * P * P].rearrange("(t q p) -> q t p", q=P, p=P), lo_bf[:, :, :]).then_inc(stored, 16)
            sp.wait_ge(stored, 32)

        @block.vector
        def _(dve):
            nc.vector.memset(raw[:, :, :], PADHI * P).then_inc(padded, 1)
            dve.wait_ge(loaded, 48)
            nc.vector.tensor_copy(rows[:, :, :], raw[:, :, :]).then_inc(cast, 1)
            nc.vector.tensor_scalar(lo[:, :, :], raw[:, :, :], P - 1, None, ALU.bitwise_and).then_inc(cast, 1)
            dve.wait_ge(cast, 2)
            nc.vector.tensor_copy(lo_bf[:, :, :], lo[:, :, :]).then_inc(cast, 1)
            nc.vector.tensor_copy(lo_f[:, :, :], lo[:, :, :]).then_inc(cast, 1)
            for t in range(NT):
                w = min(P, NC - t * P)
                dve.wait_ge(turned, 2 * t + 2)
                nc.vector.tensor_copy(key_col[:, t * P:t * P + w], ps[:, t, 0:w])
                nc.vector.tensor_copy(lo_col[:, t * P:t * P + w], ps[:, t, P:P + w])

        @block.tensor
        def _(pe):
            pe.wait_ge(cast, 4)
            for t in range(NT):
                nc.tensor.transpose(ps[:, t, 0:P], rows[:, t, :], k["ident"][:, :]).then_inc(turned, 1)
                nc.tensor.transpose(ps[:, t, P:2 * P], lo_f[:, t, :], k["ident"][:, :]).then_inc(turned, 1)


W_REC = 2 + 3 * H
ATTR = 64
HID_D = 16
TYPES = 16


class EdgeTerms:
    G = 4
    PAIRS = NC // (2 * G)
    TAIL_CHUNKS = NC - (2 * PAIRS + 1) * G
    TAIL_EDGES = E - (2 * PAIRS + 1) * G * P
    HID0, TYPE0 = ATTR, 96
    HID1 = HID0 + HID_D
    K = TYPE0 + TYPES

    def __init__(self, nc, k, c, a, feat, ps):
        G, K = self.G, self.K
        self.nc, self.k, self.a, self.feat, self.ps = nc, k, a, feat, ps
        self.raw = c.sb("attr_raw", [P, 2, G, ATTR])
        self.drow = c.sb("dist_rows", [P, 2, G * P])
        self.trow = c.sb("type_rows", [P, 2, G * P], i32)
        self.stack = c.sb("stack", [K, 2, G * P])
        self.weight = c.sb("term_weight", [K, 3 * H])
        self.type_of = c.sb("type_of", [P, 1])
        self.wd1 = c.sb("wd1", [P, 1])
        self.bd1 = c.sb("bd1", [P, 1])
        self.bias = c.sb("term_bias", [P, 3, H])
        self.zeroed, self.weights = c.sem("zeroed"), c.sem("term_weights")
        self.arrived = [c.sem(f"attr_in{j}") for j in range(2)]
        self.rows_in = [c.sem(f"term_rows_in{j}") for j in range(2)]
        self.types_in = [c.sem(f"term_types_in{j}") for j in range(2)]
        self.hots, self.hidden = c.sem("type_hots"), c.sem("dist_hidden")
        self.turned, self.moved = c.sem("attr_turned"), c.sem("attr_moved")
        self.done, self.kept = c.sem("terms_done"), c.sem("terms_kept")
        self.admitted, self.let = c.sem("loads_admitted"), c.sem("turns_admitted")

    def load_weights(self, sp):
        a, HID0, HID1, TYPE0, K = self.a, self.HID0, self.HID1, self.TYPE0, self.K
        sp.wait_ge(self.zeroed, 4)
        sp.dma_start(self.weight[0:HID0, 0:H], a["L3_gnn_We"]).then_inc(self.weights, 16)
        sp.dma_start(self.weight[HID0:HID1, H:2 * H], a["L3_gnn_Wd2"]).then_inc(self.weights, 16)
        sp.dma_start(self.weight[TYPE0:K, 2 * H:3 * H], a["L2_gnn_rel_scale"]).then_inc(self.weights, 16)
        sp.dma_start(self.wd1[HID0:HID1, :], a["L3_gnn_Wd1"].rearrange("o p -> p o")).then_inc(self.weights, 16)
        sp.dma_start(self.bd1[HID0:HID1, :], a["L3_gnn_bd1"].rearrange("(p o) -> p o", o=1)).then_inc(self.weights, 16)
        sp.dma_start(self.bias[:, 0, :], a["L3_gnn_be"].rearrange("(o h) -> o h", o=1).to_broadcast([P, H])).then_inc(self.weights, 16)
        sp.dma_start(self.bias[:, 1, :], a["L3_gnn_bd2"].rearrange("(o h) -> o h", o=1).to_broadcast([P, H])).then_inc(self.weights, 16)

    def load(self, sp, i, j, whole=True):
        G, n = self.G, self.G * P if whole else self.TAIL_EDGES
        at = (i * (2 * G) + j * G) * P
        sp.wait_ge(self.turned, i * 2 + (j + 1))
        sp.sem_inc(self.admitted, 1)
        if whole:
            sp.dma_start(self.raw[:, j, :, :], self.a["edge_attr_64"][ds(at, n), :].rearrange("(c p) f -> p c f", p=P)).then_inc(self.arrived[j], 16)
        else:
            for q in range(self.TAIL_CHUNKS):
                w = min(P, n - q * P)
                sp.dma_start(self.raw[0:w, j, q, :], self.a["edge_attr_64"][at + q * P:at + q * P + w, :]).then_inc(self.arrived[j], 16)
        sp.wait_ge(self.hidden, i * 2 + (j + 1))
        sp.sem_inc(self.admitted, 1)
        sp.dma_start(self.drow[self.HID0:self.HID1, j, 0:n], self.a["edge_weight1"][ds(at, n), :].rearrange("p o -> o p").to_broadcast([HID_D, n])).then_inc(self.rows_in[j], 16)
        sp.wait_ge(self.hots, i * 2 + (j + 1))
        sp.sem_inc(self.admitted, 1)
        sp.dma_start(self.trow[self.TYPE0:self.K, j, 0:n], self.a["edge_type_16"][ds(at, n)].rearrange("(o p) -> o p", o=1).to_broadcast([TYPES, n])).then_inc(self.types_in[j], 16)

    def begin_vector(self, dve):
        nc = self.nc
        dve.sem_inc(self.hots, 2)
        dve.sem_inc(self.kept, 1)
        nc.vector.memset(self.weight[:, :], 0.0).then_inc(self.zeroed, 1)
        nc.vector.memset(self.bias[:, :, :], 0.0).then_inc(self.zeroed, 1)
        nc.vector.tensor_scalar(self.type_of[:, :], self.k["part"][:, :], float(-self.TYPE0), None, ALU.add).then_inc(self.zeroed, 1)
        nc.vector.memset(self.stack[self.HID0:self.TYPE0, :, :], 0.0).then_inc(self.zeroed, 1)
        dve.wait_ge(self.zeroed, 4)
        dve.wait_ge(self.weights, 112)

    def hot_types(self, dve, i, j, whole=True):
        n = self.G * P if whole else self.TAIL_EDGES
        dve.wait_ge(self.types_in[j], i * 16 + 16)
        dve.wait_ge(self.done, i * 2 + (j + 1))
        self.nc.vector.tensor_scalar(self.stack[self.TYPE0:self.K, j, 0:n], self.trow[self.TYPE0:self.K, j, 0:n],
                                     self.type_of[self.TYPE0:self.K, 0:1], None, ALU.is_equal).then_inc(self.hots, 1)

    def keep(self, dve, i, j, n=G):
        at = i * (2 * self.G) + j * self.G
        dve.wait_ge(self.done, i * 2 + (j + 3))
        self.nc.vector.tensor_tensor(self.feat[:, ds(at, n), 2:W_REC], self.ps[:, 1, 0:n * 3 * H].rearrange("p (g w) -> p g w", g=n),
                                     self.bias[:, :, :].rearrange("p k h -> p (k h)")[:, None, :].to_broadcast([P, n, 3 * H]),
                                     ALU.add).then_inc(self.kept, 1)

    def begin_tensor(self, pe):
        pe.sem_inc(self.turned, 2)
        pe.sem_inc(self.done, 2)
        pe.wait_ge(self.weights, 112)

    def turn(self, pe, i, j, q, n):
        if q == 0:
            pe.wait_ge(self.arrived[j], i * 16 + 16 * (1 if n == self.G else self.TAIL_CHUNKS))
            pe.wait_ge(self.moved, i * 2 + (j + 1))
            pe.sem_inc(self.let, 1)
        product = self.nc.tensor.transpose(self.ps[0:ATTR, 6 + j, q * P:(q + 1) * P], self.raw[:, j, q, :], self.k["ident"][:, :])
        if q == n - 1:
            product.then_inc(self.turned, 1)

    def multiply(self, pe, i, j, q, n):
        if q == 0:
            pe.wait_ge(self.moved, i * 2 + (j + 3))
            pe.wait_ge(self.hidden, i * 2 + (j + 3))
            pe.wait_ge(self.hots, i * 2 + (j + 3))
            pe.wait_ge(self.kept, i * 2 + (j + 1))
        product = self.nc.tensor.matmul(self.ps[:, 1, q * 3 * H:(q + 1) * 3 * H], self.stack[:, j, q * P:(q + 1) * P], self.weight[:, :],
                                        start=True, stop=True, skip_group_check=True)
        if q == n - 1:
            product.then_inc(self.done, 1)

    def begin_scalar(self, act):
        act.sem_inc(self.moved, 2)
        act.sem_inc(self.hidden, 2)
        act.wait_ge(self.zeroed, 4)
        act.wait_ge(self.weights, 112)

    def fill(self, act, i, j, whole=True):
        n, chunks = (self.G * P, self.G) if whole else (self.TAIL_EDGES, self.TAIL_CHUNKS)
        at = slice(self.HID0, self.HID1)
        act.wait_ge(self.rows_in[j], i * 16 + 16)
        act.wait_ge(self.done, i * 2 + (j + 1))
        self.nc.scalar.activation(self.stack[at, j, 0:n], self.drow[at, j, 0:n], ACT.Relu, bias=self.bd1[at, 0:1],
                                  scale=self.wd1[at, 0:1]).then_inc(self.hidden, 1)
        act.wait_ge(self.turned, i * 2 + (j + 3))
        self.nc.scalar.activation(self.stack[0:ATTR, j, 0:chunks * P], self.ps[0:ATTR, 6 + j, 0:chunks * P], ACT.Copy).then_inc(self.moved, 1)


def sort_edges(nc, k, key_col, lo_col, fields, rec, chunk_block, ps, scratch, tag, a=None, feat=None):
    W = rec.shape[1]
    key_row, lo_row = scratch
    G = 4
    STEPS = NC // G
    with ExitStack() as ctx:
        c = Core(nc, ctx)
        hi_col = c.sb("hi_col" + tag, [P, NC])
        pad_col = c.sb("pad_col" + tag, [P, NC])
        key_int = c.sb("key_int" + tag, [P, NC], i32)
        tmp_int = c.sb("tmp_int" + tag, [P, NC], i32)
        hist = c.sb("hist" + tag, [P, NB])
        start = c.sb("start" + tag, [P, NB])

        with ExitStack() as ctx2:
            s = Core(nc, ctx2)
            onehot_lo = s.sb("count_lo" + tag, [P, 2, 13, P], bf16)
            onehot_hi = s.sb("count_hi" + tag, [P, 2, 13, NB], bf16)
            split = s.sem("split" + tag)
            hots = s.sem("hots" + tag)
            used = [s.sem(f"hots_used{j}" + tag) for j in range(2)]
            block = ctx2.enter_context(nc.Block())
            GC = 13

            @block.vector
            def _(dve):
                nc.vector.tensor_copy(key_int[:, :], key_col[:, :]).then_inc(split, 1)
                dve.wait_ge(split, 1)
                nc.vector.tensor_scalar(tmp_int[:, :], key_int[:, :], 7, None, ALU.arith_shift_right).then_inc(split, 1)
                dve.wait_ge(split, 2)
                nc.vector.tensor_copy(hi_col[:, :], tmp_int[:, :]).then_inc(split, 1)
                dve.wait_ge(split, 3)
                nc.vector.tensor_scalar(pad_col[:, :], hi_col[:, :], float(PADHI), float(ROWS), ALU.is_ge, ALU.mult)
                with dve.Fori(0, NC // (2 * GC)) as i:
                    for j in range(2):
                        dve.wait_ge(used[j], i + 1)
                        at = i * (2 * GC) + j * GC
                        nc.vector.tensor_tensor(onehot_lo[:, j, :, :], k["iota"][:, None, :].to_broadcast([P, GC, P]),
                                                lo_col[:, ds(at, GC)].rearrange("p (c o) -> p c o", o=1).to_broadcast([P, GC, P]),
                                                ALU.is_equal)
                        nc.vector.tensor_tensor(onehot_hi[:, j, :, :], k["iota"][:, None, 0:NB].to_broadcast([P, GC, NB]),
                                                hi_col[:, ds(at, GC)].rearrange("p (c o) -> p c o", o=1).to_broadcast([P, GC, NB]),
                                                ALU.is_equal).then_inc(hots, 1)

            @block.tensor
            def _(pe):
                for j in range(2):
                    pe.sem_inc(used[j], 1)
                pe.wait_ge(split, 1)
                nc.tensor.matmul(ps[:, 0, 0:NB], k["zeros"][:, :], k["zeros"][:, 0:NB], start=True, stop=True,
                                 skip_group_check=True)
                with pe.Fori(0, NC // (2 * GC)) as i:
                    for j in range(2):
                        pe.wait_ge(hots, i * 2 + (j + 1))
                        for q in range(GC):
                            last = nc.tensor.matmul(ps[:, 0, 0:NB], onehot_lo[:, j, q, :], onehot_hi[:, j, q, :],
                                                    start=False, stop=True, skip_group_check=True)
                        last.then_inc(used[j], 1)

        with ExitStack() as ctx2:
            s = Core(nc, ctx2)
            tot = s.sb("tot" + tag, [P, NB], i32)
            chunks = s.sb("chunks" + tag, [P, NB])
            upto = s.sb("upto" + tag, [P, NB])
            first = s.sb("first" + tag, [P, NB])
            first_t = s.sb("first_t" + tag, [NB, P])
            iota_v = s.sb("iota_v" + tag, [NB, NV])
            reached = s.sb("reached" + tag, [NB, NV])
            step = s.sem("start_steps" + tag)
            made = s.sem("iota_v_made" + tag)
            block = ctx2.enter_context(nc.Block())

            @block.gpsimd
            def _(pool):
                nc.gpsimd.iota(iota_v[:, :], [[1, NV]], base=0, channel_multiplier=0,
                               allow_small_or_imprecise_dtypes=True).then_inc(made, 1)

            @block.vector
            def _(dve):
                nc.vector.tensor_copy(hist[:, :], ps[:, 0, 0:NB]).then_inc(step, 1)
                dve.wait_ge(step, 3)
                nc.vector.tensor_scalar(tot[:, :], ps[:, 1, 0:NB], float(P - 1), None, ALU.add).then_inc(step, 1)
                dve.wait_ge(step, 4)
                nc.vector.tensor_scalar(tot[:, :], tot[:, :], 7, None, ALU.arith_shift_right).then_inc(step, 1)
                dve.wait_ge(step, 5)
                nc.vector.tensor_copy(chunks[:, :], tot[:, :]).then_inc(step, 1)
                dve.wait_ge(step, 6)
                nc.vector.tensor_tensor_scan(upto[:, :], k["ones"][:, 0:NB], chunks[:, :], 0.0, ALU.mult, ALU.add).then_inc(step, 1)
                dve.wait_ge(step, 7)
                nc.vector.tensor_tensor(first[:, :], upto[:, :], chunks[:, :], ALU.subtract).then_inc(step, 1)
                dve.wait_ge(step, 8)
                nc.vector.scalar_tensor_tensor(start[:, :], first[:, :], float(P), ps[:, 2, 0:NB], ALU.mult, ALU.add).then_inc(step, 1)
                dve.wait_ge(step, 10)
                nc.vector.tensor_copy(first_t[:, :], ps[0:NB, 3, 0:P]).then_inc(step, 1)
                dve.wait_ge(step, 11)
                dve.wait_ge(made, 1)
                nc.vector.tensor_scalar(reached[:, :], iota_v[:, :], first_t[:, 0:1], None, ALU.is_ge).then_inc(step, 1)
                dve.wait_ge(step, 13)
                nc.vector.tensor_scalar(chunk_block[0:1, :], ps[0:1, 4:6, 0:NV // 2], -1.0, None, ALU.add)

            @block.tensor
            def _(pe):
                pe.wait_ge(step, 1)
                nc.tensor.matmul(ps[:, 1, 0:NB], k["ones"][:, :], hist[:, :], start=True, stop=True).then_inc(step, 1)
                nc.tensor.matmul(ps[:, 2, 0:NB], k["tri"][:, :], hist[:, :], start=True, stop=True).then_inc(step, 1)
                pe.wait_ge(step, 9)
                nc.tensor.transpose(ps[0:NB, 3, 0:P], first[:, :], k["ident"][:, :]).then_inc(step, 1)
                pe.wait_ge(step, 12)
                for j in range(2):
                    last = nc.tensor.matmul(ps[0:1, 4 + j, 0:NV // 2], k["ones"][0:NB, 0:1],
                                            reached[:, j * (NV // 2):(j + 1) * (NV // 2)], start=True, stop=True)
                last.then_inc(step, 1)

        with ExitStack() as ctx2:
            s = Core(nc, ctx2)
            krow = s.sb("krow" + tag, [P, 2, G, P])
            lrow = s.sb("lrow" + tag, [P, 2, G, P], bf16)
            hot_lo = s.sb("hot_lo" + tag, [P, 2, G, P], bf16)
            hot_hi = s.sb("hot_hi" + tag, [P, 2, G, NB], bf16)
            hot_lo_t = s.sb("hot_lo_t" + tag, [P, 2, G, P])
            run = s.sb("run" + tag, [P, 2, G, NB])
            junk = s.sb("junk" + tag, [P, 2, G, P + NB])
            inside = s.sb("inside" + tag, [P, 2, G])
            base = s.sb("base" + tag, [P, 2, G])
            slot = s.sb("slot" + tag, [P, 2, G], i32)
            place = s.sb("place" + tag, [P, 2, G], i32)
            chunk = s.sb("chunk" + tag, [P, 2, G], i32)
            pos = s.sb("pos" + tag, [P, 2, G], i32)
            out = s.sb("out_rec" + tag, [P, 2, G, W])
            rows_in = [s.sem(f"rows_in{j}" + tag) for j in range(2)]
            hots = s.sem("one_hots" + tag)
            looked = s.sem("looked_up" + tag)
            copied = s.sem("run_copied" + tag)
            counted = s.sem("counted" + tag)
            free = [s.sem(f"rows_used{j}" + tag) for j in range(2)]
            placed = s.sem("placed" + tag)
            chain = s.sem("chain" + tag)
            packed = s.sem("packed" + tag)
            admitted = s.sem("admitted" + tag)
            sent = [[s.sem(f"sent{j}{g}" + tag) for g in range(G)] for j in range(2)]
            terms = EdgeTerms(nc, k, s, a, feat, ps) if feat is not None else None
            block = ctx2.enter_context(nc.Block())
            PAIRS = NC // (2 * G)
            tail = NC - PAIRS * 2 * G - G
            peeled = [(0, G), (1, tail)]

            @block.sync
            def _(sp):
                def load(i, j, n):
                    sp.wait_ge(free[j], i + 1)
                    at = (i * (2 * G) + j * G) * P
                    sp.dma_start(krow[:, j, 0:n, :], key_row[ds(at, n * P)].rearrange("(o n) -> o n", o=1).to_broadcast([P, n * P]).rearrange("q (c p) -> q c p", p=P)).then_inc(rows_in[j], 16)
                    sp.dma_start(lrow[:, j, 0:n, :], lo_row[ds(at, n * P)].rearrange("(o n) -> o n", o=1).to_broadcast([P, n * P]).rearrange("q (c p) -> q c p", p=P)).then_inc(rows_in[j], 16)

                if terms:
                    terms.load_weights(sp)
                with sp.Fori(0, PAIRS) as i:
                    for j in range(2):
                        load(i, j, G)
                        if terms:
                            terms.load(sp, i, j)
                for j, n in peeled:
                    load(PAIRS, j, n)
                    if terms:
                        terms.load(sp, PAIRS, j, j == 0)

            @block.vector
            def _(dve):
                for j in range(2):
                    dve.sem_inc(free[j], 1)
                dve.sem_inc(chain, 4)

                def one_hots(i, j, n):
                    at = i * (2 * G) + j * G
                    dve.wait_ge(rows_in[j], i * 32 + 32)
                    dve.wait_ge(counted, i * (2 * G) + (j * G + 1))
                    nc.vector.tensor_tensor(hot_lo[:, j, 0:n, :], k["iota"][:, None, :].to_broadcast([P, n, P]),
                                            lo_col[:, ds(at, n)].rearrange("p (c o) -> p c o", o=1).to_broadcast([P, n, P]), ALU.is_equal)
                    nc.vector.tensor_tensor(hot_hi[:, j, 0:n, :], k["iota"][:, None, 0:NB].to_broadcast([P, n, NB]),
                                            hi_col[:, ds(at, n)].rearrange("p (c o) -> p c o", o=1).to_broadcast([P, n, NB]), ALU.is_equal)
                    nc.vector.tensor_scalar(hot_lo_t[:, j, 0:n, :], lrow[:, j, 0:n, :], k["part"][:, 0:1], None, ALU.is_equal).then_inc(hots, 1)
                    for g in range(n):
                        last = nc.vector.scalar_tensor_tensor(junk[:, j, g, 0:P], krow[:, j, g, :], key_col[:, ds(at + g, 1)], k["before"][:, :],
                                                              ALU.is_equal, ALU.mult, accum_out=inside[:, j, g:g + 1])
                    last.then_inc(free[j], 1)

                def positions(i, j, n, before):
                    at = i * (2 * G) + j * G
                    for g in range(n):
                        dve.wait_ge(looked, at + (g + 1))
                        last = nc.vector.scalar_tensor_tensor(junk[:, j, g, P:P + NB], k["iota"][:, 0:NB], hi_col[:, ds(at + g, 1)], ps[:, 2 + (j * G + g) % 4, 0:NB],
                                                              ALU.is_equal, ALU.mult, accum_out=base[:, j, g:g + 1])
                        last.then_inc(chain, 1)
                    dve.wait_ge(chain, at + (n + 4))
                    if before:
                        for g in range(n):
                            dve.wait_ge(sent[j][g], i * 16)
                    nc.vector.tensor_tensor(base[:, j, 0:n], base[:, j, 0:n], inside[:, j, 0:n], ALU.add).then_inc(placed, 1)
                    dve.wait_ge(placed, i * 10 + (5 * j + 1))
                    nc.vector.tensor_tensor(slot[:, j, 0:n], base[:, j, 0:n], pad_col[:, ds(at, n)], ALU.add).then_inc(placed, 1)
                    dve.wait_ge(placed, i * 10 + (5 * j + 2))
                    nc.vector.tensor_scalar(place[:, j, 0:n], slot[:, j, 0:n], P - 1, None, ALU.bitwise_and).then_inc(placed, 1)
                    nc.vector.tensor_scalar(chunk[:, j, 0:n], slot[:, j, 0:n], 7, None, ALU.arith_shift_right).then_inc(placed, 1)
                    dve.wait_ge(placed, i * 10 + (5 * j + 4))
                    nc.vector.scalar_tensor_tensor(pos[:, j, 0:n], place[:, j, 0:n], float(NV + 1), chunk[:, j, 0:n],
                                                   ALU.mult, ALU.add).then_inc(placed, 1)

                def ahead(i, j, n):
                    one_hots(i, j, n)
                    if terms:
                        terms.hot_types(dve, i, j, n == G)

                def finish(i, j, n=G):
                    if terms:
                        terms.keep(dve, i, j, n)

                if terms:
                    terms.begin_vector(dve)
                ahead(0, 0, G)
                ahead(0, 1, G)
                positions(0, 0, G, False)
                finish(0, 0)
                ahead(1, 0, G)
                positions(0, 1, G, False)
                with dve.Fori(1, PAIRS) as i:
                    finish(i - 1, 1)
                    ahead(i, 1, G)
                    positions(i, 0, G, True)
                    finish(i, 0)
                    ahead(i + 1, 0, G)
                    positions(i, 1, G, True)
                finish(PAIRS - 1, 1)
                ahead(PAIRS, 1, tail)
                positions(PAIRS, 0, G, True)
                finish(PAIRS, 0)
                positions(PAIRS, 1, tail, True)
                finish(PAIRS, 1, tail)

            @block.tensor
            def _(pe):
                pe.sem_inc(counted, 1)
                nc.tensor.matmul(ps[:, 0, 0:NB], k["ident"][:, :], start[:, :], start=True, stop=True,
                                 skip_group_check=True).then_inc(counted, 1)

                def step(i, j, n, ahead=0):
                    at = i * (2 * G) + j * G
                    pe.wait_ge(hots, i * 2 + (j + 1))
                    for g in range(n):
                        pe.wait_ge(copied, at + (g + 1))
                        nc.tensor.matmul(ps[:, 0, 0:NB], hot_lo[:, j, g, :], hot_hi[:, j, g, :],
                                         start=False, stop=True, skip_group_check=True).then_inc(counted, 1)
                        if terms and g < ahead:
                            terms.turn(pe, i + j, 1 - j, g, ahead)
                        pe.wait_ge(chain, at + (g + 1))
                        nc.tensor.matmul(ps[:, 2 + (j * G + g) % 4, 0:NB], hot_lo_t[:, j, g, :], run[:, j, g, :],
                                         start=True, stop=True).then_inc(looked, 1)
                    if terms:
                        for g in range(n):
                            terms.multiply(pe, i, j, g, n)

                if terms:
                    terms.begin_tensor(pe)
                    for g in range(G):
                        terms.turn(pe, 0, 0, g, G)
                with pe.Fori(0, PAIRS) as i:
                    for j in range(2):
                        step(i, j, G, G)
                step(PAIRS, 0, G, tail)
                step(PAIRS, 1, tail)

            @block.scalar
            def _(act):
                def step(i, j, n, before):
                    at = i * (2 * G) + j * G
                    for g in range(n):
                        act.wait_ge(counted, at + (g + 2))
                        nc.scalar.activation(run[:, j, g, :], ps[:, 0, 0:NB], ACT.Copy).then_inc(copied, 1)
                    if before:
                        for g in range(n):
                            act.wait_ge(sent[j][g], i * 16)
                    nc.scalar.activation(out[:, j, 0:n, :], fields(at, n), ACT.Copy).then_inc(packed, 1)

                if terms:
                    terms.begin_scalar(act)
                    terms.fill(act, 0, 0)
                for j in range(2):
                    step(0, j, G, False)
                    if terms:
                        terms.fill(act, j, 1 - j)
                with act.Fori(1, PAIRS) as i:
                    for j in range(2):
                        step(i, j, G, True)
                        if terms:
                            terms.fill(act, i + j, 1 - j)
                step(PAIRS, 0, G, True)
                if terms:
                    terms.fill(act, PAIRS, 1, False)
                step(PAIRS, 1, tail, True)

            @block.gpsimd
            def _(pool):
                def step(i, j, n):
                    pool.wait_ge(placed, i * 10 + (5 * j + 5))
                    pool.wait_ge(packed, i * 2 + (j + 1))
                    pool.sem_inc(admitted, 1)
                    for g in range(n):
                        nc.gpsimd.indirect_dma_start(rec, bass.IndirectOffsetOnAxis(pos[:, j, g:g + 1], 0),
                                                     out[:, j, g, :], None).then_inc(sent[j][g], 16)

                with pool.Fori(0, PAIRS) as i:
                    for j in range(2):
                        step(i, j, G)
                for j, n in peeled:
                    step(PAIRS, j, n)
                for j in range(2):
                    for g in range(G):
                        n = dict(peeled).get(j, 0)
                        pool.wait_ge(sent[j][g], 16 * (PAIRS + (g < n)))




def sorted_index(nc, k, rec, src_i, loc, loc_row, ps, tag):
    NT = -(-NV // P)
    W = rec.shape[1]
    with ExitStack() as ctx:
        c = Core(nc, ctx)
        r = c.sb("rec_in" + tag, [P, NV + 1, W])
        turned_sb = c.sb("loc_t" + tag, [P, NT, P], bf16)
        loaded = c.sem("rec_loaded" + tag)
        split = c.sem("rec_split" + tag)
        turned = c.sem("loc_turned" + tag)
        moved = c.sem("loc_moved" + tag)
        stored = c.sem("loc_stored" + tag)
        block = ctx.enter_context(nc.Block())

        @block.sync
        def _(sp):
            sp.dma_start(r[:, :, :], rec.rearrange("(p v) w -> p v w", p=P)).then_inc(loaded, 16)
            sp.wait_ge(moved, NT)
            full = NV // P
            sp.dma_start(loc_row[0:full * P * P].rearrange("(t v p) -> v t p", v=P, p=P), turned_sb[:, 0:full, :]).then_inc(stored, 16)
            sp.dma_start(loc_row[full * P * P:NV * P].rearrange("(v p) -> v p", p=P), turned_sb[0:NV - full * P, full, :]).then_inc(stored, 16)
            sp.wait_ge(stored, 32)

        @block.vector
        def _(dve):
            dve.wait_ge(loaded, 16)
            nc.vector.tensor_copy(loc[:, :], r[:, 0:NV, 1]).then_inc(split, 1)
            nc.vector.tensor_copy(src_i[:, :], r[:, 0:NV, 0])
            for t in range(NT):
                w = min(P, NV - t * P)
                dve.wait_ge(turned, t + 1)
                nc.vector.tensor_copy(turned_sb[0:w, t, :], ps[0:w, t, 0:P]).then_inc(moved, 1)

        @block.tensor
        def _(pe):
            pe.wait_ge(split, 1)
            for t in range(NT):
                w = min(P, NV - t * P)
                nc.tensor.transpose(ps[0:w, t, 0:P], loc[:, t * P:t * P + w], k["ident"][:, :]).then_inc(turned, 1)


HIDC = 32


def load_weights(nc, top, a):
    w = {}
    jobs = []

    def mat(name, src, rows, cols):
        w[name] = top.sb("w_" + name, [rows, cols])
        jobs.append((w[name][:, :], src))

    def part(name, c0, c1, src):
        jobs.append((w[name][:, c0:c1], src))

    def col(name, src, n=P):
        w[name] = top.sb("w_" + name, [n, 1])
        jobs.append((w[name][:, :], src.rearrange("(p o) -> p o", o=1)))

    def row(name, src, n):
        w[name] = top.sb("w_" + name, [P, n])
        jobs.append((w[name][:, :], src.rearrange("(o f) -> o f", o=1).to_broadcast([P, n])))

    w["src0"] = top.sb("w_src0", [P, 2 * F])
    w["dst0"] = top.sb("w_dst0", [P, 2 * F])
    w["bias0"] = top.sb("w_bias0", [P, 2 * F])
    for n, name in enumerate(("msg", "att")):
        part("src0", n * F, (n + 1) * F, a[f"L0_gnn_{name}_W1"][0:F, :])
        part("dst0", n * F, (n + 1) * F, a[f"L0_gnn_{name}_W1"][F:2 * F, :])
        part("bias0", n * F, (n + 1) * F, a[f"L0_gnn_{name}_b1"].rearrange("(o f) -> o f", o=1).to_broadcast([P, F]))
    mat("msg_w2", a["L0_gnn_msg_W2"], F, F)
    row("msg_b2", a["L0_gnn_msg_b2"], F)
    mat("upd_w1h", a["L0_gnn_upd_W1"][0:F, :], F, F)
    mat("upd_w1a", a["L0_gnn_upd_W1"][F:2 * F, :], F, F)
    col("upd_b1", a["L0_gnn_upd_b1"])
    mat("upd_w2", a["L0_gnn_upd_W2"], F, F)
    col("upd_b2", a["L0_gnn_upd_b2"])
    row("att_w2", a["L0_gnn_att_W2"].rearrange("f o -> (f o)"), F)
    row("att_b2", a["L0_gnn_att_b2"], 1)
    mat("glb_w", a["L0_gnn_glb_W"], F, F)
    col("glb_b", a["L0_gnn_glb_b"])
    row("eps1", a["L1_gnn_eps"], 1)
    mat("w1_t", a["L1_gnn_W1"], F, F)
    mat("w2_t", a["L1_gnn_W2"], F, F)
    for name in ("b1", "gamma", "beta", "b2"):
        col("l1_" + name, a["L1_gnn_" + name])
    mat("type_emb", a["L2_gnn_type_emb"], 8, F)
    w["kv_h"] = top.sb("w_kv_h", [P, 2 * F])
    w["kv_t"] = top.sb("w_kv_t", [P, 2 * F])
    for n, name in enumerate(("Wk", "Wv")):
        part("kv_h", n * F, (n + 1) * F, a["L2_gnn_" + name][0:F, :])
        part("kv_t", n * F, (n + 1) * F, a["L2_gnn_" + name][F:2 * F, :])
    for name in ("Wq", "Wskip"):
        mat(name + "_h", a["L2_gnn_" + name][0:F, :], F, F)
        mat(name + "_t", a["L2_gnn_" + name][F:2 * F, :], F, F)
    mat("l2_Wo", a["L2_gnn_Wo"], F, F)
    for name in ("bo", "gamma", "beta"):
        col("l2_" + name, a["L2_gnn_" + name])
    for name in ("Wq", "Wk", "Wv"):
        mat("l3_" + name, a["L3_gnn_" + name], F, F)
    for name in ("bq", "bk"):
        row("l3_" + name, a["L3_gnn_" + name], F)
    col("l3_bv", a["L3_gnn_bv"])
    mat("l3_Wo", a["L3_gnn_Wo"], F, F)
    for name in ("bo", "gamma", "beta"):
        col("l3_" + name, a["L3_gnn_" + name])
    mat("Wc1", a["L3_gnn_Wc1"], 1, HIDC)
    col("bc1", a["L3_gnn_bc1"], HIDC)
    mat("Wc2", a["L3_gnn_Wc2"], HIDC, H)
    row("bc2", a["L3_gnn_bc2"], H)
    with ExitStack() as ctx:
        c = Core(nc, ctx)
        loaded = c.sem("weights_loaded")
        block = ctx.enter_context(nc.Block())

        @block.sync
        def _(sp):
            for dst, src in jobs:
                sp.dma_start(dst, src).then_inc(loaded, 16)
            sp.wait_ge(loaded, 16 * len(jobs))
    return w


def wide(ps):
    return ps[:, :, :].rearrange("p b n -> p (b n)")


SPANS = [(a, min(a + 512, NP)) for a in range(0, NP, 512)]


def load_nodes(nc, k, x_in, xt, ps):
    LAST = N - (NB - 1) * P
    with ExitStack() as ctx:
        c = Core(nc, ctx)
        raw = c.sb("x_raw", [P, NB, F])
        zeroed, loaded, turned = c.sem("x_zeroed"), c.sem("x_loaded"), c.sem("x_turned")
        block = ctx.enter_context(nc.Block())

        @block.sync
        def _(sp):
            sp.dma_start(raw[:, 0:NB - 1, :], x_in[0:(NB - 1) * P, :].rearrange("(t p) f -> p t f", p=P)).then_inc(loaded, 16)
            sp.wait_ge(zeroed, 1)
            sp.dma_start(raw[0:LAST, NB - 1, :], x_in[(NB - 1) * P:N, :]).then_inc(loaded, 16)

        @block.tensor
        def _(pe):
            pe.wait_ge(loaded, 32)
            for t in range(NB):
                last = nc.tensor.transpose(wide(ps)[:, t * P:(t + 1) * P], raw[:, t, :], k["ident"][:, :])
            last.then_inc(turned, 1)

        @block.vector
        def _(dve):
            nc.vector.memset(raw[:, NB - 1, :], 0.0).then_inc(zeroed, 1)
            dve.wait_ge(turned, 1)
            nc.vector.tensor_copy(xt[:, :], wide(ps)[:, 0:NP])


PARTS = [(0, 1024), (1024, 2048), (2048, NP)]


def layernorm(nc, k, xt, out, ps, tag, relu=True):
    with ExitStack() as ctx:
        c = Core(nc, ctx)
        cen = c.sb("cen" + tag, [P, NP])
        sq = c.sb("sq" + tag, [P, NP])
        mean_ready, centred, squared = c.sem("mean_ready" + tag), c.sem("centred" + tag), c.sem("squared" + tag)
        var_ready, rooted, inverted = c.sem("var_ready" + tag), c.sem("rooted" + tag), c.sem("inverted" + tag)
        block = ctx.enter_context(nc.Block())

        @block.tensor
        def _(pe):
            for a, b in PARTS:
                for at in range(a, b, 512):
                    last = nc.tensor.matmul(wide(ps)[:, at:min(at + 512, b)], k["mean_of"][:, :], xt[:, at:min(at + 512, b)], start=True, stop=True)
                last.then_inc(mean_ready, 1)
            for n, (a, b) in enumerate(PARTS):
                pe.wait_ge(squared, n + 1)
                for at in range(a, b, 512):
                    last = nc.tensor.matmul(wide(ps)[:, at:min(at + 512, b)], k["mean_of"][:, :], sq[:, at:min(at + 512, b)], start=True, stop=True)
                last.then_inc(var_ready, 1)

        @block.vector
        def _(dve):
            for n, (a, b) in enumerate(PARTS):
                dve.wait_ge(mean_ready, n + 1)
                nc.vector.tensor_tensor(cen[:, a:b], xt[:, a:b], wide(ps)[:, a:b], ALU.subtract).then_inc(centred, 1)
            for n, (a, b) in enumerate(PARTS):
                dve.wait_ge(rooted, n + 1)
                nc.vector.reciprocal(sq[:, a:b], sq[:, a:b]).then_inc(inverted, 1)
                dve.wait_ge(inverted, n + 1)
                if relu:
                    nc.vector.scalar_tensor_tensor(out[:, a:b], cen[:, a:b], 0.0, sq[:, a:b], ALU.max, ALU.mult)
                else:
                    nc.vector.tensor_tensor(out[:, a:b], cen[:, a:b], sq[:, a:b], ALU.mult)

        @block.scalar
        def _(act):
            for n, (a, b) in enumerate(PARTS):
                act.wait_ge(centred, n + 1)
                nc.scalar.activation(sq[:, a:b], cen[:, a:b], ACT.Square).then_inc(squared, 1)
            for n, (a, b) in enumerate(PARTS):
                act.wait_ge(var_ready, n + 1)
                nc.scalar.activation(sq[:, a:b], wide(ps)[:, a:b], ACT.Sqrt, bias=k["eps"][:, 0:1]).then_inc(rooted, 1)


def node_rows(nc, k, parts, width, bias, dest, ps, tag, dram=None):
    with ExitStack() as ctx:
        c = Core(nc, ctx)
        made = c.sem("rows_made" + tag)
        kept = c.sem("rows_kept" + tag)
        stored = c.sem("rows_stored" + tag)
        block = ctx.enter_context(nc.Block())

        @block.tensor
        def _(pe):
            for t in range(NB):
                if t >= 8:
                    pe.wait_ge(kept, t - 7)
                for n, (xt, w) in enumerate(parts):
                    last = nc.tensor.matmul(ps[:, t % 8, 0:width], xt[:, t * P:(t + 1) * P], w,
                                            start=n == 0, stop=n == len(parts) - 1)
                last.then_inc(made, 1)

        @block.vector
        def _(dve):
            for t in range(NB):
                dve.wait_ge(made, t + 1)
                if bias is None:
                    nc.vector.tensor_copy(dest[:, t, 0:width], ps[:, t % 8, 0:width]).then_inc(kept, 1)
                else:
                    nc.vector.tensor_tensor(dest[:, t, 0:width], ps[:, t % 8, 0:width], bias, ALU.add).then_inc(kept, 1)

        @block.sync
        def _(sp):
            if dram is not None:
                sp.wait_ge(kept, NB)
                sp.dma_start(dram.rearrange("(t p) f -> p t f", p=P), dest[:, :, 0:width]).then_inc(stored, 16)
                sp.wait_ge(stored, 16)


U = 8
ITERS = NV // (2 * U)
WORK = 7


def load_blocks(nc, chunk_block, at, n, most):
    return nc.values_load_multi_w_load_instructions(chunk_block[0:1, ds(at, n)], engines=[mybir.EngineType.PE],
                                                    min_val=0, max_val=most, skip_runtime_bounds_check_because=
                                                    "sort_edges counts the node blocks begun: 1 to NB, less one")[1]


def zero_accumulators(nc, k, ps):
    for b in range(WORK):
        last = nc.tensor.matmul(ps[:, b, :], k["zeros"][:, :], k["zeros4"][:, :], start=True, stop=True, skip_group_check=True)
    return last


def attention_messages(nc, k, w, g, table, here, ps, tag):
    with ExitStack() as ctx:
        c = Core(nc, ctx)
        idx = c.sb("idx" + tag, [P, 2, U], i32)
        there = c.sb("there" + tag, [P, 2, U, 2 * F])
        rows = c.sb("locrows" + tag, [P, 2, U * P], bf16)
        hot_t = c.sb("hot_t" + tag, [P, 2, U * P])
        hot_s = c.sb("hot_s" + tag, [P, 2, U, P])
        relu = c.sb("relu" + tag, [P, 2, U, F])
        prod = c.sb("prod" + tag, [P, 2, U, F])
        dot = c.sb("dot" + tag, [P, 2, U])
        att = c.sb("att" + tag, [P, 2, U])
        indexed = [c.sem(f"indexed{j}" + tag) for j in range(2)]
        admitted, passed = c.sem("adm" + tag), c.sem("passed" + tag)
        gathered = [[c.sem(f"gat{j}{q}" + tag) for q in range(U)] for j in range(2)]
        rows_in = [c.sem(f"rin{j}" + tag) for j in range(2)]
        hots = c.sem("hots" + tag)
        spread = c.sem("spread" + tag)
        summed, cut, dotted = c.sem("summed" + tag), c.sem("cut" + tag), c.sem("dotted" + tag)
        gated, weighted, added = c.sem("gated" + tag), c.sem("weighted" + tag), c.sem("added" + tag)
        block = ctx.enter_context(nc.Block())
        CH = 2 * U
        PR = U // 2

        @block.sync
        def _(sp):
            for j in range(2):
                sp.dma_start(idx[:, j, :], g["src"][:, j * U:(j + 1) * U]).then_inc(indexed[j], 16)
            with sp.Fori(0, ITERS) as i:
                for j in range(2):
                    sp.wait_ge(hots, i * 2 + (j + 1))
                    sp.dma_start(rows[:, j, :], g["loc_row"][ds((i * CH + j * U) * P, U * P)].rearrange("(o n) -> o n", o=1)
                                 .to_broadcast([P, U * P])).then_inc(rows_in[j], 16)
                    for q in range(U):
                        sp.wait_ge(gathered[j][q], i * 16 + 16)
                    sp.sem_inc(passed, 1)
                    sp.dma_start(idx[:, j, :], g["src"][:, ds(i * CH + (CH + j * U), U)]).then_inc(indexed[j], 16)
            for j in range(2):
                sp.wait_ge(indexed[j], 16 * (ITERS + 1))

        @block.gpsimd
        def _(pool):
            with pool.Fori(0, ITERS) as i:
                for j in range(2):
                    pool.wait_ge(indexed[j], i * 16 + 16)
                    for q in range(U):
                        if q % 2 == 0:
                            pool.wait_ge(cut, i * CH // 2 + (j * PR + q // 2 + 1))
                        pool.wait_ge(dotted, i * CH + (j * U + q + 1))
                        pool.sem_inc(admitted, 1)
                        nc.gpsimd.indirect_dma_start(there[:, j, q, :], None, table,
                                                     bass.IndirectOffsetOnAxis(idx[:, j, q:q + 1], 0)).then_inc(gathered[j][q], 16)

        @block.vector
        def _(dve):
            dve.sem_inc(hots, 2)
            dve.sem_inc(dotted, CH)
            def hot_nodes(i, j):
                dve.wait_ge(rows_in[j], i * 16 + 16)
                dve.wait_ge(spread, i * (2 * PR) + (j * PR + PR))
                nc.vector.tensor_scalar(hot_t[:, j, :], rows[:, j, :], k["part"][:, 0:1], None, ALU.is_equal).then_inc(hots, 1)

            def dot_att(i, j, m):
                dve.wait_ge(summed, i * (2 * PR) + (j * PR + m + 1))
                for q in (2 * m, 2 * m + 1):
                    nc.vector.scalar_tensor_tensor(prod[:, j, q, :], there[:, j, q, F:2 * F], 0.0, w["att_w2"][:, :],
                                                   ALU.max, ALU.mult, accum_out=dot[:, j, q:q + 1]).then_inc(dotted, 1)

            def weigh(i, j, m):
                if m == 0:
                    dve.wait_ge(gated, i * 2 + (j + 1))
                    dve.wait_ge(added, i * CH + (j * U + U))
                for q in (2 * m, 2 * m + 1):
                    nc.vector.tensor_scalar(hot_s[:, j, q, :], k["iota"][:, :], g["loc"][:, ds(i * CH + (j * U + q), 1)],
                                            att[:, j, q:q + 1], ALU.is_equal, ALU.mult).then_inc(weighted, 1)

            def combine(i, j, before, after):
                for m in range(PR):
                    if before is not None:
                        weigh(*before, m)
                    for q in (2 * m, 2 * m + 1):
                        dve.wait_ge(gathered[j][q], i * 16 + 16)
                    dve.wait_ge(spread, i * (2 * PR) + (2 * PR + j * PR + m + 1))
                    pair = there[:, j, 2 * m:2 * m + 2, :].rearrange("p q f -> p (q f)")
                    nc.vector.tensor_tensor(pair, pair, ps[:, WORK, :], ALU.add).then_inc(summed, 1)
                    if m:
                        dot_att(i, j, m - 1)
                    if m == 1 and after is not None:
                        hot_nodes(*after)
                dot_att(i, j, PR - 1)

            hot_nodes(0, 0)
            combine(0, 0, None, (0, 1))
            with dve.Fori(0, ITERS - 1) as i:
                combine(i, 1, (i, 0), (i + 1, 0))
                combine(i + 1, 0, (i, 1), (i + 1, 1))
            combine(ITERS - 1, 1, (ITERS - 1, 0), None)
            for m in range(PR):
                weigh(ITERS - 1, 1, m)

        @block.scalar
        def _(act):
            act.sem_inc(cut, 2 * PR)

            def step(i, j):
                act.wait_ge(added, i * CH + (j * U + U))
                for m in range(PR):
                    act.wait_ge(summed, i * (2 * PR) + (j * PR + m + 1))
                    nc.scalar.activation(relu[:, j, 2 * m:2 * m + 2, :], there[:, j, 2 * m:2 * m + 2, 0:F], ACT.Relu).then_inc(cut, 1)
                act.wait_ge(dotted, i * CH + (CH + j * U + U))
                nc.scalar.activation(att[:, j, :], dot[:, j, :], ACT.Sigmoid, bias=w["att_b2"][:, 0:1]).then_inc(gated, 1)

            with act.Fori(0, ITERS) as i:
                for j in range(2):
                    step(i, j)

        @block.tensor
        def _(pe):
            pe.sem_inc(spread, 2 * PR)
            pe.sem_inc(added, CH)
            zero_accumulators(nc, k, ps)

            def target_pair(i, j, m, blocks):
                if not isinstance(i, int) or i + j + m:
                    pe.wait_ge(summed, i * (2 * PR) + (j * PR + m))
                for q in (2 * m, 2 * m + 1):
                    last = nc.tensor.matmul(ps[:, WORK, (q % 2) * 2 * F:(q % 2 + 1) * 2 * F], hot_t[:, j, q * P:(q + 1) * P],
                                            here[:, :, :].rearrange("p t f -> p (t f)")[:, ds(blocks[q] * (2 * F), 2 * F)],
                                            start=True, stop=True, skip_group_check=True)
                last.then_inc(spread, 1)

            def add_pair(i, j, m, blocks):
                for q in (2 * m, 2 * m + 1):
                    pe.wait_ge(weighted, i * CH + (j * U + q + 1))
                    nc.tensor.matmul(wide(ps)[:, ds(blocks[q] * F, F)], hot_s[:, j, q, :], relu[:, j, q, :],
                                     start=False, stop=True, skip_group_check=True)
                    nc.tensor.matmul(wide(ps)[:, ds(blocks[q] + NP, 1)], hot_s[:, j, q, :], k["ones"][:, 0:1],
                                     start=False, stop=True, skip_group_check=True).then_inc(added, 1)

            def half_step(now, before):
                if now is not None:
                    blocks = load_blocks(nc, g["block"], now[0] * CH + now[1] * U, U, NB - 1)
                    pe.wait_ge(hots, now[0] * 2 + (now[1] + 3))
                for m in range(PR):
                    if now is not None:
                        target_pair(*now, m, blocks)
                    if before is not None and m == 0:
                        blocks_before = load_blocks(nc, g["block"], before[0] * CH + before[1] * U, U, NB - 1)
                    if before is not None:
                        add_pair(*before, m, blocks_before)

            half_step((0, 0), None)
            with pe.Fori(0, ITERS - 1) as i:
                half_step((i, 1), (i, 0))
                half_step((i + 1, 0), (i, 1))
            half_step((ITERS - 1, 1), (ITERS - 1, 0))
            half_step(None, (ITERS - 1, 1))


def collect(nc, k, ps, acc_t, sums, n_sums, tag, scale=None):
    with ExitStack() as ctx:
        c = Core(nc, ctx)
        rows = c.sb("acc_rows" + tag, [P, NP])
        out, ready, turned = c.sem("acc_out" + tag), c.sem("acc_ready" + tag), c.sem("acc_turned" + tag)
        block = ctx.enter_context(nc.Block())

        @block.vector
        def _(dve):
            if n_sums:
                nc.vector.tensor_copy(sums[:, :], wide(ps)[:, NP:NP + n_sums]).then_inc(out, 1)
            else:
                dve.sem_inc(out, 1)
            nc.vector.tensor_copy(rows[:, :], wide(ps)[:, 0:NP]).then_inc(out, 1)
            if scale is not None:
                dve.wait_ge(out, 2)
                scale(dve, rows, out)
            dve.wait_ge(turned, 1)
            nc.vector.tensor_copy(acc_t[:, :], wide(ps)[:, 0:NP])

        @block.tensor
        def _(pe):
            pe.wait_ge(out, 5 if scale is not None else 2)
            for t in range(NB):
                last = nc.tensor.transpose(wide(ps)[:, t * P:(t + 1) * P], rows[:, t * P:(t + 1) * P], k["ident"][:, :])
            last.then_inc(turned, 1)


def global_vector(nc, k, w, ht, glob, ps):
    with ExitStack() as ctx:
        c = Core(nc, ctx)
        mean = c.sb("node_mean", [P, 1])
        meaned, scaled, ready = c.sem("meaned"), c.sem("mean_scaled"), c.sem("glob_ready")
        block = ctx.enter_context(nc.Block())

        @block.vector
        def _(dve):
            nc.vector.tensor_reduce(mean[:, :], ht[:, 0:N], AX.X, ALU.add).then_inc(meaned, 1)
            dve.wait_ge(meaned, 1)
            nc.vector.tensor_scalar(mean[:, :], mean[:, :], 1.0 / N, None, ALU.mult).then_inc(scaled, 1)

        @block.tensor
        def _(pe):
            pe.wait_ge(scaled, 1)
            nc.tensor.matmul(ps[:, 0, 0:1], w["glb_w"][:, :], mean[:, :], start=True, stop=True).then_inc(ready, 1)

        @block.scalar
        def _(act):
            act.wait_ge(ready, 1)
            nc.scalar.activation(glob[:, :], ps[:, 0, 0:1], ACT.Relu, bias=w["glb_b"][:, 0:1])


def update_nodes(nc, k, w, ht, acc_t, sums, glob, ps, tag):
    with ExitStack() as ctx:
        c = Core(nc, ctx)
        bias = c.sb("msg_bias" + tag, [P, NB, F])
        agg = c.sb("agg" + tag, [P, NP])
        hid = c.sb("hid" + tag, [P, NP])
        biased, agg_made, agg_kept = c.sem("biased" + tag), c.sem("agg_made" + tag), c.sem("agg_kept" + tag)
        hid_made, hid_kept, new_made, moved = c.sem("hid_made" + tag), c.sem("hid_kept" + tag), c.sem("new_made" + tag), c.sem("h_moved" + tag)
        block = ctx.enter_context(nc.Block())

        @block.vector
        def _(dve):
            nc.vector.tensor_tensor(bias[:, :, :], w["msg_b2"][:, None, :].to_broadcast([P, NB, F]),
                                    sums[:, 0:NB].rearrange("p (t o) -> p t o", o=1).to_broadcast([P, NB, F]), ALU.mult).then_inc(biased, 1)
            dve.wait_ge(agg_made, 1)
            nc.vector.tensor_copy(agg[:, :], wide(ps)[:, 0:NP]).then_inc(agg_kept, 1)
            dve.wait_ge(hid_made, 1)
            nc.vector.tensor_scalar(ht[:, :], ht[:, :], w["upd_b2"][:, 0:1], glob[:, 0:1], ALU.add, ALU.add).then_inc(moved, 1)
            dve.wait_ge(moved, 1)
            dve.wait_ge(new_made, 1)
            nc.vector.tensor_tensor(ht[:, :], ht[:, :], wide(ps)[:, 0:NP], ALU.add)

        @block.tensor
        def _(pe):
            pe.wait_ge(biased, 1)
            for t in range(NB):
                at = slice(t * P, (t + 1) * P)
                nc.tensor.matmul(wide(ps)[:, at], w["msg_w2"][:, :], acc_t[:, at], start=True, stop=False)
                last = nc.tensor.matmul(wide(ps)[:, at], bias[:, t, :], k["ident"][:, :], start=False, stop=True)
            last.then_inc(agg_made, 1)
            pe.wait_ge(agg_kept, 1)
            for a, b in SPANS:
                nc.tensor.matmul(wide(ps)[:, a:b], w["upd_w1h"][:, :], ht[:, a:b], start=True, stop=False)
                last = nc.tensor.matmul(wide(ps)[:, a:b], w["upd_w1a"][:, :], agg[:, a:b], start=False, stop=True)
            last.then_inc(hid_made, 1)
            pe.wait_ge(hid_kept, 1)
            for a, b in SPANS:
                last = nc.tensor.matmul(wide(ps)[:, a:b], w["upd_w2"][:, :], hid[:, a:b], start=True, stop=True)
            last.then_inc(new_made, 1)

        @block.scalar
        def _(act):
            act.wait_ge(hid_made, 1)
            nc.scalar.activation(hid[:, :], wide(ps)[:, 0:NP], ACT.Relu, bias=w["upd_b1"][:, 0:1]).then_inc(hid_kept, 1)


def add_into(nc, xt, terms, tag):
    with ExitStack() as ctx:
        c = Core(nc, ctx)
        added = c.sem("x_added" + tag)
        block = ctx.enter_context(nc.Block())

        @block.vector
        def _(dve):
            for n, term in enumerate(terms):
                if n:
                    dve.wait_ge(added, n)
                nc.vector.tensor_tensor(xt[:, :], xt[:, :], term, ALU.add).then_inc(added, 1)


STEPS0 = 2


def layer0(nc, k, w, g, table, xt, ps):
    with ExitStack() as ctx:
        c = Core(nc, ctx)
        ht = c.sb("ht0", [P, NP])
        glob = c.sb("glob", [P, 1])
        layernorm(nc, k, xt, ht, ps, "0")
        global_vector(nc, k, w, ht, glob, ps)
        for step in range(STEPS0):
            tag = f"0{step}"
            with ExitStack() as rctx:
                r = Core(nc, rctx)
                here = r.sb("here" + tag, [P, NB, 2 * F])
                node_rows(nc, k, [(ht, w["src0"][:, :])], 2 * F, None, here, ps, tag + "a", dram=table)
                node_rows(nc, k, [(ht, w["dst0"][:, :])], 2 * F, w["bias0"][:, :], here, ps, tag + "b")
                attention_messages(nc, k, w, g, table, here, ps, tag)
            with ExitStack() as rctx:
                r = Core(nc, rctx)
                acc_t = r.sb("acc_t" + tag, [P, NP])
                sums = r.sb("att_sums" + tag, [P, NB])
                collect(nc, k, ps, acc_t, sums, NB, tag)
                update_nodes(nc, k, w, ht, acc_t, sums, glob, ps, tag)
        add_into(nc, xt, [ht[:, :]], "0")


def neighbour_sums(nc, k, g, table, ps, tag):
    with ExitStack() as ctx:
        c = Core(nc, ctx)
        idx = c.sb("idx" + tag, [P, 2, U], i32)
        there = c.sb("there" + tag, [P, 2, U, F])
        hot = c.sb("hot" + tag, [P, 2, U, P])
        indexed, admitted, weighted, added = c.sem("indexed" + tag), c.sem("adm" + tag), c.sem("hotted" + tag), c.sem("added" + tag)
        gathered = [[c.sem(f"gat{j}{q}" + tag) for q in range(U)] for j in range(2)]
        block = ctx.enter_context(nc.Block())
        CH = 2 * U

        @block.gpsimd
        def _(pool):
            with pool.Fori(0, ITERS) as i:
                for j in range(2):
                    pool.wait_ge(indexed, i * 2 + (j + 1))
                    for q in range(U):
                        pool.wait_ge(added, i * CH + (j * U + q + 1))
                        pool.sem_inc(admitted, 1)
                        nc.gpsimd.indirect_dma_start(there[:, j, q, :], None, table,
                                                     bass.IndirectOffsetOnAxis(idx[:, j, q:q + 1], 0)).then_inc(gathered[j][q], 16)

        @block.vector
        def _(dve):
            for j in range(2):
                nc.vector.tensor_copy(idx[:, j, :], g["src"][:, j * U:(j + 1) * U]).then_inc(indexed, 1)
            with dve.Fori(0, ITERS) as i:
                for j in range(2):
                    dve.wait_ge(added, i * CH + (j * U + U))
                    for q in range(U):
                        nc.vector.tensor_scalar(hot[:, j, q, :], k["iota"][:, :], g["loc"][:, ds(i * CH + (j * U + q), 1)],
                                                None, ALU.is_equal).then_inc(weighted, 1)
                    for q in range(U):
                        dve.wait_ge(gathered[j][q], i * 16 + 16)
                    nc.vector.tensor_copy(idx[:, j, :], g["src"][:, ds(i * CH + (CH + j * U), U)]).then_inc(indexed, 1)

        @block.tensor
        def _(pe):
            pe.sem_inc(added, CH)
            zero_accumulators(nc, k, ps)
            with pe.Fori(0, ITERS) as i:
                for j in range(2):
                    blocks = load_blocks(nc, g["block"], i * CH + j * U, U, NB - 1)
                    for q in range(U):
                        pe.wait_ge(gathered[j][q], i * 16 + 16)
                        pe.wait_ge(weighted, i * CH + (j * U + q + 1))
                        nc.tensor.matmul(wide(ps)[:, ds(blocks[q] * F, F)], hot[:, j, q, :], there[:, j, q, :],
                                         start=False, stop=True, skip_group_check=True).then_inc(added, 1)


def gin_nodes(nc, k, w, ht, acc_t, out, ps):
    with ExitStack() as ctx:
        c = Core(nc, ctx)
        cen = c.sb("gin_cen", [P, NP])
        sq = c.sb("gin_sq", [P, NP])
        st = c.sb("gin_stats", [P, 4])
        onep = c.sb("one_plus_eps", [P, 1])
        mixed, made, kept, step = c.sem("gin_mixed"), c.sem("gin_made"), c.sem("gin_kept"), c.sem("gin_steps")
        squared, rooted, cut, last_made = c.sem("gin_squared"), c.sem("gin_rooted"), c.sem("gin_cut"), c.sem("gin_last")
        block = ctx.enter_context(nc.Block())

        @block.vector
        def _(dve):
            nc.vector.tensor_scalar(onep[:, :], w["eps1"][:, :], 1.0, None, ALU.add).then_inc(mixed, 1)
            dve.wait_ge(mixed, 1)
            nc.vector.scalar_tensor_tensor(acc_t[:, :], ht[:, :], onep[:, 0:1], acc_t[:, :], ALU.mult, ALU.add).then_inc(mixed, 1)
            dve.wait_ge(made, 1)
            nc.vector.tensor_scalar(cen[:, :], wide(ps)[:, 0:NP], w["l1_b1"][:, 0:1], None, ALU.add).then_inc(step, 1)
            dve.wait_ge(step, 1)
            nc.vector.tensor_reduce(st[:, 0:1], cen[:, 0:N], AX.X, ALU.add).then_inc(step, 1)
            dve.wait_ge(step, 2)
            nc.vector.tensor_scalar(st[:, 0:1], st[:, 0:1], 1.0 / N, None, ALU.mult).then_inc(step, 1)
            dve.wait_ge(step, 3)
            nc.vector.tensor_scalar(cen[:, :], cen[:, :], st[:, 0:1], None, ALU.subtract).then_inc(step, 1)
            dve.wait_ge(squared, 1)
            nc.vector.tensor_reduce(st[:, 1:2], sq[:, 0:N], AX.X, ALU.add).then_inc(step, 1)
            dve.wait_ge(rooted, 1)
            nc.vector.reciprocal(st[:, 2:3], st[:, 2:3]).then_inc(step, 1)
            dve.wait_ge(step, 6)
            nc.vector.tensor_scalar(cen[:, :], cen[:, :], st[:, 2:3], w["l1_gamma"][:, 0:1], ALU.mult, ALU.mult).then_inc(step, 1)
            dve.wait_ge(last_made, 1)
            nc.vector.tensor_scalar(out[:, :], wide(ps)[:, 0:NP], w["l1_b2"][:, 0:1], None, ALU.add)

        @block.scalar
        def _(act):
            act.wait_ge(step, 4)
            nc.scalar.activation(sq[:, :], cen[:, :], ACT.Square).then_inc(squared, 1)
            act.wait_ge(step, 5)
            nc.scalar.activation(st[:, 2:3], st[:, 1:2], ACT.Sqrt, bias=k["eps"][:, 0:1], scale=1.0 / N).then_inc(rooted, 1)
            act.wait_ge(step, 7)
            nc.scalar.activation(sq[:, :], cen[:, :], ACT.Relu, bias=w["l1_beta"][:, 0:1]).then_inc(cut, 1)

        @block.tensor
        def _(pe):
            pe.wait_ge(mixed, 2)
            for a, b in SPANS:
                last = nc.tensor.matmul(wide(ps)[:, a:b], w["w1_t"][:, :], acc_t[:, a:b], start=True, stop=True)
            last.then_inc(made, 1)
            pe.wait_ge(cut, 1)
            for a, b in SPANS:
                last = nc.tensor.matmul(wide(ps)[:, a:b], w["w2_t"][:, :], sq[:, a:b], start=True, stop=True)
            last.then_inc(last_made, 1)


def layer1(nc, k, w, g, table, xt, ps):
    with ExitStack() as ctx:
        c = Core(nc, ctx)
        ht = c.sb("ht1", [P, NP])
        acc_t = c.sb("acc_t1", [P, NP])
        layernorm(nc, k, xt, ht, ps, "1")
        with ExitStack() as rctx:
            rows = Core(nc, rctx).sb("rows1", [P, NB, F])
            node_rows(nc, k, [(ht, k["ident"][:, :])], F, None, rows, ps, "1", dram=table)
        neighbour_sums(nc, k, g, table, ps, "1")
        collect(nc, k, ps, acc_t, None, 0, "1")
        gin_nodes(nc, k, w, ht, acc_t, acc_t, ps)
        add_into(nc, xt, [acc_t[:, :]], "1")


SQ = NV // 4


def edge_products(nc, k, g, table, wide_row, here, width, got, spool, ps, tag, terms=None):
    with ExitStack() as ctx:
        c = Core(nc, ctx)
        extra = width - F
        idx = c.sb("idx" + tag, [P, 2, U], i32)
        there = c.sb("there" + tag, [P, 2, U, wide_row])
        rows = c.sb("locrows" + tag, [P, 2, U * P], bf16)
        hot_t = c.sb("hot_t" + tag, [P, 2, U * P])
        prod = c.sb("prod" + tag, [P, 2, U, F])
        indexed, admitted, hots, spread = c.sem("indexed" + tag), c.sem("adm" + tag), c.sem("hots" + tag), c.sem("spread" + tag)
        multiplied, summed = c.sem("multiplied" + tag), c.sem("headed" + tag)
        gathered = [[c.sem(f"gat{j}{q}" + tag) for q in range(U)] for j in range(2)]
        rows_in = [c.sem(f"rin{j}" + tag) for j in range(2)]
        spooled = [c.sem(f"spooled{j}" + tag) for j in range(2)]
        terms_in = c.sem("terms_in" + tag)
        block = ctx.enter_context(nc.Block())
        CH = 2 * U
        PR = U // 2

        @block.sync
        def _(sp):
            with sp.Fori(0, ITERS) as i:
                for j in range(2):
                    sp.wait_ge(hots, i * 2 + (j + 1))
                    sp.dma_start(rows[:, j, :], g["loc_row"][ds((i * CH + j * U) * P, U * P)].rearrange("(o n) -> o n", o=1)
                                 .to_broadcast([P, U * P])).then_inc(rows_in[j], 16)
                    if terms is not None:
                        at = i * CH + j * U
                        sp.dma_start(terms[0][:, ds(at, U), :], terms[1][:, ds(at, U), :]).then_inc(terms_in, 16)
            if terms is not None:
                sp.wait_ge(terms_in, 16 * 2 * ITERS)

        @block.scalar
        def _(act):
            if spool is not None:
                with act.Fori(0, ITERS) as i:
                    for j in range(2):
                        for q in range(U):
                            act.wait_ge(gathered[j][q], i * 16 + 16)
                        act.dma_start(spool[:, ds(i * CH + j * U, U), :], there[:, j, :, F:wide_row]).then_inc(spooled[j], 16)
                for j in range(2):
                    act.wait_ge(spooled[j], 16 * ITERS)

        @block.gpsimd
        def _(pool):
            def gather(i, j, again):
                pool.wait_ge(indexed, i * 2 + (j + 1))
                if again and spool is not None:
                    pool.wait_ge(spooled[j], i * 16)
                for q in range(U):
                    if q % 2 == 0:
                        pool.wait_ge(multiplied, i * (2 * PR) + (j * PR + q // 2 + 1))
                        pool.sem_inc(admitted, 1)
                    nc.gpsimd.indirect_dma_start(there[:, j, q, :], None, table,
                                                 bass.IndirectOffsetOnAxis(idx[:, j, q:q + 1], 0)).then_inc(gathered[j][q], 16)

            for j in range(2):
                gather(0, j, False)
            with pool.Fori(1, ITERS) as i:
                for j in range(2):
                    gather(i, j, True)

        @block.vector
        def _(dve):
            dve.sem_inc(hots, 2)
            dve.sem_inc(multiplied, 2 * PR)
            for j in range(2):
                nc.vector.tensor_copy(idx[:, j, :], g["src"][:, j * U:(j + 1) * U]).then_inc(indexed, 1)

            def one_hots(i, j):
                dve.wait_ge(rows_in[j], i * 16 + 16)
                dve.wait_ge(spread, i * (2 * PR) + (j * PR + PR))
                nc.vector.tensor_scalar(hot_t[:, j, :], rows[:, j, :], k["part"][:, 0:1], None, ALU.is_equal).then_inc(hots, 1)

            def combine(i, j):
                at = i * CH + j * U

                def heads(m):
                    dve.wait_ge(multiplied, i * (2 * PR) + (2 * PR + j * PR + m + 1))
                    nc.vector.tensor_reduce(got[:, ds(at + 2 * m, 2), 0, :], prod[:, j, 2 * m:2 * m + 2, :].rearrange("p q (h d) -> p q h d", h=H),
                                            AX.X, ALU.add).then_inc(summed, 1)

                for m in range(PR):
                    for q in (2 * m, 2 * m + 1):
                        dve.wait_ge(gathered[j][q], i * 16 + 16)
                    dve.wait_ge(spread, i * (2 * PR) + (2 * PR + j * PR + m + 1))
                    bank = ps[:, WORK, 0:2 * width].rearrange("p (q f) -> p q f", q=2)
                    if extra:
                        nc.vector.tensor_copy(got[:, ds(at + 2 * m, 2), 1, :], bank[:, :, F:width])
                    nc.vector.tensor_tensor(prod[:, j, 2 * m:2 * m + 2, :], there[:, j, 2 * m:2 * m + 2, 0:F], bank[:, :, 0:F],
                                            ALU.mult).then_inc(multiplied, 1)
                    if m:
                        heads(m - 1)
                heads(PR - 1)
                nc.vector.tensor_copy(idx[:, j, :], g["src"][:, ds(at + CH, U)]).then_inc(indexed, 1)

            one_hots(0, 0)
            with dve.Fori(0, ITERS - 1) as i:
                one_hots(i, 1)
                combine(i, 0)
                one_hots(i + 1, 0)
                combine(i, 1)
            one_hots(ITERS - 1, 1)
            combine(ITERS - 1, 0)
            combine(ITERS - 1, 1)

        @block.tensor
        def _(pe):
            pe.sem_inc(spread, 2 * PR)

            def target_rows(i, j):
                blocks = load_blocks(nc, g["block"], i * CH + j * U, U, NB - 1)
                pe.wait_ge(hots, i * 2 + (j + 3))
                for m in range(PR):
                    pe.wait_ge(multiplied, i * (2 * PR) + (2 * PR + j * PR + m))
                    for q in (2 * m, 2 * m + 1):
                        last = nc.tensor.matmul(ps[:, WORK, (q % 2) * width:(q % 2 + 1) * width], hot_t[:, j, q * P:(q + 1) * P],
                                                here[:, :, :].rearrange("p t f -> p (t f)")[:, ds(blocks[q] * width, width)],
                                                start=True, stop=True, skip_group_check=True)
                    last.then_inc(spread, 1)

            with pe.Fori(0, ITERS) as i:
                for j in range(2):
                    target_rows(i, j)


def hgt_weights(nc, k, g, got, ex, ps):
    with ExitStack() as ctx:
        c = Core(nc, ctx)
        empty = c.sb("empty", [P, NV])
        top1 = c.sb("top1", [P, 1])
        row = c.sb("top_row", [1, P])
        used, step, turned = c.sem("rel_used"), c.sem("hgt_steps"), c.sem("top_turned")
        spread = c.sem("top_spread")
        block = ctx.enter_context(nc.Block())

        @block.vector
        def _(dve):
            nc.vector.tensor_scalar(empty[:, :], g["loc"][:, :], 0.0, -1e30, ALU.is_lt, ALU.mult).then_inc(step, 1)
            nc.vector.scalar_tensor_tensor(ex[:, :, :], got[:, :, 0, :], float(DH) ** -0.5, ex[:, :, :], ALU.mult, ALU.mult).then_inc(used, 1)
            dve.wait_ge(step, 1)
            dve.wait_ge(used, 1)
            nc.vector.tensor_tensor(ex[:, :, :], ex[:, :, :], empty[:, :].rearrange("p (v o) -> p v o", o=1).to_broadcast([P, NV, H]), ALU.add).then_inc(step, 1)
            dve.wait_ge(step, 2)
            nc.vector.tensor_reduce(top1[:, :], ex[:, :, :], AX.XY, ALU.max).then_inc(step, 1)
            dve.wait_ge(turned, 1)
            nc.vector.tensor_reduce(row[:, 0:1], ps[0:1, 0, 0:P], AX.X, ALU.max).then_inc(step, 1)
            dve.wait_ge(spread, 1)
            nc.vector.tensor_scalar(top1[:, :], ps[:, 1, 0:1], -1.0, None, ALU.mult).then_inc(step, 1)

        @block.tensor
        def _(pe):
            pe.wait_ge(step, 3)
            nc.tensor.transpose(ps[0:1, 0, 0:P], top1[:, :], k["ident"][:, :]).then_inc(turned, 1)
            pe.wait_ge(step, 4)
            nc.tensor.matmul(ps[:, 1, 0:1], k["ones"][0:1, :], row[:, 0:1], start=True, stop=True).then_inc(spread, 1)

        @block.scalar
        def _(act):
            act.wait_ge(step, 5)
            nc.scalar.activation(ex[:, :, :], ex[:, :, :], ACT.Exp, bias=top1[:, 0:1])


def hgt_messages(nc, k, g, ex, spool, ps):
    tag = "2m"
    with ExitStack() as ctx:
        c = Core(nc, ctx)
        val = c.sb("val" + tag, [P, 2, U, F])
        msg = c.sb("msg" + tag, [P, 2, U, F])
        hot = c.sb("hot" + tag, [P, 2, U, P])
        val_in = [c.sem(f"val_in{j}" + tag) for j in range(2)]
        mass = c.sb("mass" + tag, [P, 2, U, H])
        multiplied, placed, added = c.sem("multiplied" + tag), c.sem("placed" + tag), c.sem("added" + tag)
        block = ctx.enter_context(nc.Block())
        CH = 2 * U

        @block.sync
        def _(sp):
            with sp.Fori(0, ITERS) as i:
                for j in range(2):
                    sp.wait_ge(multiplied, i * 2 + (j + 1))
                    sp.dma_start(val[:, j, :, :], spool[:, ds(i * CH + j * U, U), :]).then_inc(val_in[j], 16)

        @block.vector
        def _(dve):
            dve.sem_inc(multiplied, 2)
            with dve.Fori(0, ITERS) as i:
                for j in range(2):
                    at = i * CH + j * U
                    dve.wait_ge(added, i * 2 + (j + 1))
                    for q in range(U):
                        nc.vector.tensor_scalar(hot[:, j, q, :], k["iota"][:, :], g["loc"][:, ds(at + q, 1)], None, ALU.is_equal)
                    dve.wait_ge(val_in[j], i * 16 + 16)
                    nc.vector.tensor_tensor(msg[:, j, :, :].rearrange("p q (h d) -> p (q h) d", h=H), val[:, j, :, :].rearrange("p q (h d) -> p (q h) d", h=H),
                                            ex[:, ds(at, U), :].rearrange("p q (h o) -> p (q h) o", o=1).to_broadcast([P, U * H, DH]),
                                            ALU.mult).then_inc(multiplied, 1)

        @block.scalar
        def _(act):
            with act.Fori(0, ITERS) as i:
                for j in range(2):
                    act.wait_ge(added, i * 2 + (j + 1))
                    nc.scalar.activation(mass[:, j, :, :], ex[:, ds(i * CH + j * U, U), :], ACT.Copy).then_inc(placed, 1)

        @block.tensor
        def _(pe):
            pe.sem_inc(added, 2)
            zero_accumulators(nc, k, ps)
            with pe.Fori(0, ITERS) as i:
                for j in range(2):
                    at = i * CH + j * U
                    blocks = load_blocks(nc, g["block"], at, U, NB - 1)
                    pe.wait_ge(placed, i * 2 + (j + 1))
                    pe.wait_ge(multiplied, i * 2 + (j + 3))
                    for q in range(U):
                        nc.tensor.matmul(wide(ps)[:, ds(blocks[q] * F, F)], hot[:, j, q, :], msg[:, j, q, :],
                                         start=False, stop=True, skip_group_check=True)
                        last = nc.tensor.matmul(wide(ps)[:, ds(blocks[q] * H + NP, H)], hot[:, j, q, :], mass[:, j, q, :],
                                                start=False, stop=True, skip_group_check=True)
                    last.then_inc(added, 1)


def type_rows(nc, k, w, kinds, tet, ps):
    T = 8
    with ExitStack() as ctx:
        c = Core(nc, ctx)
        kind = c.sb("node_kind", [T, NP], i32)
        hot = c.sb("node_kind_hot", [T, NP])
        padded, loaded, hotted, made = c.sem("kind_padded"), c.sem("kind_loaded"), c.sem("kind_hot"), c.sem("tet_made")
        block = ctx.enter_context(nc.Block())

        @block.sync
        def _(sp):
            sp.wait_ge(padded, 1)
            sp.dma_start(kind[:, 0:N], kinds.rearrange("(o n) -> o n", o=1).to_broadcast([T, N])).then_inc(loaded, 16)

        @block.vector
        def _(dve):
            nc.vector.memset(kind[:, :], -1).then_inc(padded, 1)
            dve.wait_ge(loaded, 16)
            nc.vector.tensor_scalar(hot[:, :], kind[:, :], k["part"][0:T, 0:1], None, ALU.is_equal).then_inc(hotted, 1)
            dve.wait_ge(made, 1)
            nc.vector.tensor_copy(tet[:, :], wide(ps)[:, 0:NP])

        @block.tensor
        def _(pe):
            pe.wait_ge(hotted, 1)
            for a, b in SPANS:
                last = nc.tensor.matmul(wide(ps)[:, a:b], w["type_emb"][:, :], hot[:, a:b], start=True, stop=True)
            last.then_inc(made, 1)


def project(nc, k, parts, bias, add, out, ps, tag):
    with ExitStack() as ctx:
        c = Core(nc, ctx)
        made, kept = c.sem("proj_made" + tag), c.sem("proj_kept" + tag)
        block = ctx.enter_context(nc.Block())

        @block.tensor
        def _(pe):
            for a, b in SPANS:
                for n, (wt, xt) in enumerate(parts):
                    last = nc.tensor.matmul(wide(ps)[:, a:b], wt, xt[:, a:b], start=n == 0, stop=n == len(parts) - 1)
            last.then_inc(made, 1)

        @block.vector
        def _(dve):
            dve.wait_ge(made, 1)
            if add is None:
                nc.vector.tensor_scalar(out[:, :], wide(ps)[:, 0:NP], bias, None, ALU.add)
            else:
                nc.vector.scalar_tensor_tensor(out[:, :], wide(ps)[:, 0:NP], bias, add[:, :], ALU.add, ALU.add)


def elu_into(nc, xt, y, low, gamma, beta):
    with ExitStack() as ctx:
        c = Core(nc, ctx)
        step, done = c.sem("elu_steps"), c.sem("elu_exp")
        block = ctx.enter_context(nc.Block())

        @block.vector
        def _(dve):
            nc.vector.tensor_scalar(y[:, :], y[:, :], gamma, beta, ALU.mult, ALU.add).then_inc(step, 1)
            dve.wait_ge(step, 1)
            nc.vector.tensor_scalar(low[:, :], y[:, :], 0.0, None, ALU.min).then_inc(step, 1)
            nc.vector.scalar_tensor_tensor(xt[:, :], y[:, :], 0.0, xt[:, :], ALU.max, ALU.add).then_inc(step, 1)
            dve.wait_ge(done, 1)
            dve.wait_ge(step, 3)
            nc.vector.scalar_tensor_tensor(xt[:, :], low[:, :], -1.0, xt[:, :], ALU.add, ALU.add)

        @block.scalar
        def _(act):
            act.wait_ge(step, 2)
            nc.scalar.activation(low[:, :], low[:, :], ACT.Exp).then_inc(done, 1)


def layer2(nc, k, w, g, rec, table, spool, xt, kinds, ps):
    with ExitStack() as ctx:
        c = Core(nc, ctx)
        ht = c.sb("ht2", [P, NP])
        tet = c.sb("tet", [P, NP])
        layernorm(nc, k, xt, ht, ps, "2")
        type_rows(nc, k, w, kinds, tet, ps)
        with ExitStack() as ectx:
            e = Core(nc, ectx)
            ex = e.sb("ex", [P, NV, H])
            with ExitStack() as gctx:
                got = Core(nc, gctx).sb("got2", [P, NV, 1, H])
                with ExitStack() as rctx:
                    rows = Core(nc, rctx).sb("rows2", [P, NB, 2 * F])
                    node_rows(nc, k, [(ht, w["kv_h"][:, :]), (tet, w["kv_t"][:, :])], 2 * F, None, rows, ps, "2kv", dram=table)
                with ExitStack() as rctx:
                    here = Core(nc, rctx).sb("here2", [P, NB, F])
                    node_rows(nc, k, [(ht, w["Wq_h"][:, :]), (tet, w["Wq_t"][:, :])], F, None, here, ps, "2q")
                    records = rec.rearrange("(p v) w -> p v w", p=P)
                    edge_products(nc, k, g, table, 2 * F, here, F, got, spool, ps, "2",
                                  terms=(ex, records[:, :, 2 + 2 * H:2 + 3 * H]))
                hgt_weights(nc, k, g, got, ex, ps)
            hgt_messages(nc, k, g, ex, spool, ps)
        acc_t = c.sb("acc_t2", [P, NP])
        sums = c.sb("sums2", [P, NB * H])

        def normalise(dve, rows, out):
            nc.vector.tensor_scalar(sums[:, :], sums[:, :], 1e-16, None, ALU.add).then_inc(out, 1)
            dve.wait_ge(out, 3)
            nc.vector.reciprocal(sums[:, :], sums[:, :]).then_inc(out, 1)
            dve.wait_ge(out, 4)
            heads = rows[:, :].rearrange("p (g d) -> p g d", d=DH)
            nc.vector.tensor_tensor(heads, heads, sums[:, :].rearrange("p (g o) -> p g o", o=1).to_broadcast([P, NB * H, DH]), ALU.mult).then_inc(out, 1)

        collect(nc, k, ps, acc_t, sums, NB * H, "2", scale=normalise)
        project(nc, k, [(w["l2_Wo"][:, :], acc_t), (w["Wskip_h"][:, :], ht), (w["Wskip_t"][:, :], tet)], w["l2_bo"][:, 0:1], None, acc_t, ps, "2")
        layernorm(nc, k, acc_t, ht, ps, "2b", relu=False)
        elu_into(nc, xt, ht, acc_t, w["l2_gamma"][:, 0:1], w["l2_beta"][:, 0:1])


SEGS = P // H
SEGC = NV // SEGS
SEGE = SEGC * P
BIG = 1.5e38


def segment_rows(nc, k, g, got, row, same, gid_row, gid8, ps):
    with ExitStack() as ctx:
        c = Core(nc, ctx)
        blk = c.sb("blk_f", [1, NV])
        gid = c.sb("gid", [P, NV])
        before = c.sb("last_before", [P, 1])
        inner = c.sb("inner", [P, 1], i32)
        inner_f = c.sb("inner_f", [P, 1])
        ready, spread, ids, turned, kept = c.sem("blk_ready"), c.sem("blk_spread"), c.sem("ids_ready"), c.sem("seg_turned"), c.sem("seg_kept")
        before_set = c.sem("before_set")
        shifted, masks, firsts = c.sem("shifted"), c.sem("masks_made"), c.sem("firsts")
        block = ctx.enter_context(nc.Block())

        @block.gpsimd
        def _(pool):
            nc.gpsimd.iota(inner[:, :], [[1, 1]], base=0, channel_multiplier=1).then_inc(masks, 1)

        @block.vector
        def _(dve):
            nc.vector.tensor_copy(blk[:, :], g["block"][:, :]).then_inc(ready, 1)
            dve.wait_ge(spread, 1)
            for n in range(2):
                half = slice(n * (NV // 2), (n + 1) * (NV // 2))
                nc.vector.scalar_tensor_tensor(gid[:, half], ps[:, n, 0:NV // 2], float(P), g["loc"][:, half], ALU.mult, ALU.add).then_inc(ids, 1)
            dve.wait_ge(ids, 2)
            nc.vector.tensor_copy(gid8[:, :].rearrange("p (c h s) -> p c h s", h=H, s=SEGS),
                                  gid[:, :].rearrange("p (s c) -> p c s", s=SEGS)[:, :, None, :].to_broadcast([P, SEGC, H, SEGS])).then_inc(ids, 1)
            for t in range(SEGC):
                dve.wait_ge(turned, t + 1)
                nc.vector.tensor_copy(row[:, t * P:(t + 1) * P], ps[:, 2 + t % 6, 0:P])
                nc.vector.tensor_copy(gid_row[:, t * P:(t + 1) * P], ps[:, 2 + t % 6, P:2 * P]).then_inc(kept, 1)
            dve.wait_ge(kept, SEGC)
            nc.vector.tensor_tensor(same[:, 1:SEGE], gid_row[:, 1:SEGE], gid_row[:, 0:SEGE - 1], ALU.is_equal)
            dve.wait_ge(masks, 1)
            nc.vector.tensor_scalar(inner[:, :], inner[:, :], SEGS - 1, None, ALU.bitwise_and).then_inc(firsts, 1)
            dve.wait_ge(firsts, 1)
            nc.vector.tensor_scalar(inner_f[:, :], inner[:, :], 0.0, None, ALU.is_gt).then_inc(firsts, 1)
            dve.wait_ge(firsts, 2)
            dve.wait_ge(shifted, 16)
            nc.vector.scalar_tensor_tensor(same[:, 0:1], gid_row[:, 0:1], before[:, 0:1], inner_f[:, :], ALU.is_equal, ALU.mult)

        @block.sync
        def _(sp):
            sp.wait_ge(kept, SEGC)
            sp.wait_ge(before_set, 1)
            sp.dma_start(before[1:P, :], gid_row[0:P - 1, SEGE - 1:SEGE]).then_inc(shifted, 16)

        @block.scalar
        def _(act):
            nc.scalar.activation(before[:, :], k["ones"][:, 0:1], ACT.Copy).then_inc(before_set, 1)

        @block.tensor
        def _(pe):
            pe.wait_ge(ready, 1)
            for n in range(2):
                last = nc.tensor.matmul(ps[:, n, 0:NV // 2], k["ones"][0:1, :], blk[:, n * (NV // 2):(n + 1) * (NV // 2)], start=True, stop=True)
            last.then_inc(spread, 1)
            pe.wait_ge(ids, 3)
            scores = got[:, :, :].rearrange("p v h -> p (v h)")
            for t in range(SEGC):
                if t >= 6:
                    pe.wait_ge(kept, t - 5)
                nc.tensor.transpose(ps[:, 2 + t % 6, 0:P], scores[:, t * P:(t + 1) * P], k["ident"][:, :])
                nc.tensor.transpose(ps[:, 2 + t % 6, P:2 * P], gid8[:, t * P:(t + 1) * P], k["ident"][:, :]).then_inc(turned, 1)


def carried(nc, k, carry, local, over, ps, tag, reverse, most):
    with ExitStack() as ctx:
        c = Core(nc, ctx)
        loc_r = c.sb("loc_r" + tag, [1, P])
        over_r = c.sb("over_r" + tag, [1, P])
        run_r = c.sb("run_r" + tag, [1, P + 2])
        turned, step, back = c.sem("carry_turned" + tag), c.sem("carry_steps" + tag), c.sem("carry_back" + tag)
        block = ctx.enter_context(nc.Block())

        @block.tensor
        def _(pe):
            nc.tensor.transpose(ps[0:1, 0, 0:P], local, k["ident"][:, :])
            nc.tensor.transpose(ps[0:1, 0, P:2 * P], over, k["ident"][:, :]).then_inc(turned, 1)
            pe.wait_ge(step, 4)
            at = 2 if reverse else 0
            nc.tensor.matmul(ps[:, 1, 0:1], run_r[:, at:at + P], k["ones"][0:1, 0:1], start=True, stop=True).then_inc(back, 1)

        @block.vector
        def _(dve):
            nc.vector.memset(run_r[:, :], 0.0).then_inc(step, 1)
            dve.wait_ge(turned, 1)
            nc.vector.tensor_copy(loc_r[:, :], ps[0:1, 0, 0:P]).then_inc(step, 1)
            nc.vector.tensor_copy(over_r[:, :], ps[0:1, 0, P:2 * P]).then_inc(step, 1)
            dve.wait_ge(step, 3)
            out, a, b = run_r[:, 1:P + 1], over_r[:, :], loc_r[:, :]
            if reverse:
                out, a, b = out[:, ::-1], a[:, ::-1], b[:, ::-1]
            nc.vector.tensor_tensor_scan(out, a, b, 0.0 if not most else -BIG, ALU.min if most else ALU.mult,
                                         ALU.max if most else ALU.add).then_inc(step, 1)
            dve.wait_ge(back, 1)
            nc.vector.tensor_copy(carry[:, :], ps[:, 1, 0:1])


def spans_of(nc, k, row, same, gate, out, ps, tag, most):
    with ExitStack() as ctx:
        c = Core(nc, ctx)
        whole = c.sb("whole" + tag, [P, 1])
        over = c.sb("over" + tag, [P, 1])
        carry = c.sb("carry" + tag, [P, 1])
        nxt = c.sb("next" + tag, [P, 1])
        ops = (ALU.min, ALU.max) if most else (ALU.mult, ALU.add)
        neutral = -BIG if most else 0.0

        with ExitStack() as s:
            step, moved, zeroed = Core(nc, s).sem("span_a" + tag), Core(nc, s).sem("span_m" + tag), Core(nc, s).sem("span_z" + tag)
            block = s.enter_context(nc.Block())

            @block.sync
            def _(sp):
                sp.wait_ge(zeroed, 1)
                sp.dma_start(nxt[0:P - 1, :], same[1:P, 0:1]).then_inc(moved, 16)
                sp.wait_ge(moved, 16)

            @block.vector
            def _(dve):
                nc.vector.memset(nxt[:, :], 0.0).then_inc(zeroed, 1)
                if most:
                    nc.vector.tensor_scalar(gate[:, :], same[:, :], 2 * BIG, BIG, ALU.mult, ALU.subtract).then_inc(step, 1)
                else:
                    nc.vector.tensor_copy(gate[:, :], same[:, :]).then_inc(step, 1)
                nc.vector.tensor_reduce(whole[:, :], same[:, :], AX.X, ALU.min).then_inc(step, 1)
                dve.wait_ge(step, 2)
                nc.vector.tensor_tensor_scan(out[:, :], gate[:, :], row[:, :], neutral, *ops).then_inc(step, 1)
                if most:
                    nc.vector.tensor_scalar(over[:, :], whole[:, :], 2 * BIG, BIG, ALU.mult, ALU.subtract)
                else:
                    nc.vector.tensor_copy(over[:, :], whole[:, :])
        carried(nc, k, carry, out[:, SEGE - 1:SEGE], over[:, :], ps, tag + "f", False, most)
        with ExitStack() as s:
            step = Core(nc, s).sem("span_b" + tag)
            block = s.enter_context(nc.Block())

            @block.vector
            def _(dve):
                nc.vector.tensor_tensor_scan(out[:, :], gate[:, :], row[:, :], carry[:, 0:1], *ops).then_inc(step, 1)
                dve.wait_ge(step, 1)
                nc.vector.tensor_copy(gate[:, 0:SEGE - 1], same[:, 1:SEGE]).then_inc(step, 1)
                nc.vector.tensor_copy(gate[:, SEGE - 1:SEGE], nxt[:, :]).then_inc(step, 1)
                dve.wait_ge(step, 3)
                nc.vector.scalar_tensor_tensor(out[:, :], gate[:, :], 0.0, out[:, :], ALU.is_equal, ALU.mult).then_inc(step, 1)
                nc.vector.tensor_reduce(over[:, :], gate[:, :], AX.X, ALU.min).then_inc(step, 1)
                dve.wait_ge(step, 5)
                nc.vector.tensor_tensor_scan(whole_row(out), whole_row(gate), whole_row(out), 0.0, ALU.mult, ALU.add).then_inc(step, 1)

        carried(nc, k, carry, out[:, 0:1], over[:, :], ps, tag + "b", True, False)
        with ExitStack() as s:
            step = Core(nc, s).sem("span_c" + tag)
            block = s.enter_context(nc.Block())

            @block.vector
            def _(dve):
                nc.vector.tensor_tensor_scan(whole_row(gate), whole_row(gate), k["zeros"][:, 0:1].to_broadcast([P, SEGE]), carry[:, 0:1], ALU.mult, ALU.add).then_inc(step, 1)
                dve.wait_ge(step, 1)
                nc.vector.tensor_tensor(out[:, :], out[:, :], gate[:, :], ALU.add)


def whole_row(t):
    return t[:, ::-1]


def softmax_mass(nc, k, row, same, gate, tmp, ps):
    def alone(fn):
        with ExitStack() as s:
            c = Core(nc, s)
            block = s.enter_context(nc.Block())
            fn(block, c)

    spans_of(nc, k, row, same, gate, tmp, ps, "x", True)

    def exps(block, c):
        centred = c.sem("row_centred")

        @block.vector
        def _(dve):
            nc.vector.tensor_tensor(row[:, :], row[:, :], tmp[:, :], ALU.subtract).then_inc(centred, 1)

        @block.scalar
        def _(act):
            act.wait_ge(centred, 1)
            nc.scalar.activation(row[:, :], row[:, :], ACT.Exp)

    alone(exps)
    spans_of(nc, k, row, same, gate, tmp, ps, "s", False)

    def divide(block, c):
        inverted = c.sem("row_inverted")

        @block.vector
        def _(dve):
            nc.vector.reciprocal(tmp[:, :], tmp[:, :]).then_inc(inverted, 1)
            dve.wait_ge(inverted, 1)
            nc.vector.tensor_tensor(row[:, :], row[:, :], tmp[:, :], ALU.mult)

    alone(divide)


def rows_back(nc, k, row, got, ps):
    with ExitStack() as ctx:
        c = Core(nc, ctx)
        turned, kept = c.sem("back_turned"), c.sem("back_kept")
        block = ctx.enter_context(nc.Block())
        dest = got[:, :, :].rearrange("p (s c) h -> p c h s", s=SEGS)

        @block.tensor
        def _(pe):
            for t in range(SEGC):
                if t >= 8:
                    pe.wait_ge(kept, t - 7)
                nc.tensor.transpose(ps[:, t % 8, 0:P], row[:, t * P:(t + 1) * P], k["ident"][:, :]).then_inc(turned, 1)

        @block.vector
        def _(dve):
            for t in range(SEGC):
                dve.wait_ge(turned, t + 1)
                nc.vector.tensor_copy(dest[:, t, :, :], ps[:, t % 8, 0:P].rearrange("p (h s) -> p h s", h=H)).then_inc(kept, 1)


def weight_sums(nc, k, g, got, ps):
    with ExitStack() as ctx:
        c = Core(nc, ctx)
        parts = c.sb("weight_parts", [P, NV, 3 * H], bf16)
        rest = c.sb("weight_rest", [P, NV, H])
        hot = c.sb("hot3m", [P, 2, U, P], bf16)
        now = c.sb("parts_now", [P, 2, U, 3 * H], bf16)
        split, weighted, added = c.sem("weights_split"), c.sem("hotted3m"), c.sem("added3m")
        placed = c.sem("parts_placed")
        block = ctx.enter_context(nc.Block())
        CH = 2 * U

        @block.vector
        def _(dve):
            nc.vector.tensor_copy(parts[:, :, 0:H], got[:, :, :]).then_inc(split, 1)
            dve.wait_ge(split, 1)
            nc.vector.tensor_tensor(rest[:, :, :], got[:, :, :], parts[:, :, 0:H], ALU.subtract).then_inc(split, 1)
            dve.wait_ge(split, 2)
            nc.vector.tensor_copy(parts[:, :, H:2 * H], rest[:, :, :]).then_inc(split, 1)
            dve.wait_ge(split, 3)
            nc.vector.tensor_tensor(parts[:, :, 2 * H:3 * H], rest[:, :, :], parts[:, :, H:2 * H], ALU.subtract).then_inc(split, 1)
            with dve.Fori(0, ITERS) as i:
                for j in range(2):
                    dve.wait_ge(added, i * 2 + (j + 1))
                    for q in range(U):
                        last = nc.vector.tensor_scalar(hot[:, j, q, :], k["iota_bf"][:, :], g["loc"][:, ds(i * CH + (j * U + q), 1)], None, ALU.is_equal)
                    last.then_inc(weighted, 1)

        @block.scalar
        def _(act):
            act.wait_ge(split, 4)
            with act.Fori(0, ITERS) as i:
                for j in range(2):
                    act.wait_ge(added, i * 2 + (j + 1))
                    nc.scalar.activation(now[:, j, :, :], parts[:, ds(i * CH + j * U, U), :], ACT.Copy).then_inc(placed, 1)

        @block.tensor
        def _(pe):
            pe.sem_inc(added, 2)
            zero_accumulators(nc, k, ps)
            with pe.Fori(0, ITERS) as i:
                for j in range(2):
                    at = i * CH + j * U
                    blocks = load_blocks(nc, g["block"], at, U, NB - 1)
                    pe.wait_ge(placed, i * 2 + (j + 1))
                    pe.wait_ge(weighted, i * 2 + (j + 1))
                    for q in range(U):
                        last = nc.tensor.matmul(wide(ps)[0:3 * H, ds(blocks[q] * P, P)], now[:, j, q, :],
                                                hot[:, j, q, :], start=False, stop=True, skip_group_check=True)
                    last.then_inc(added, 1)


def edge_scores(nc, k, rec, pairs, got):
    with ExitStack() as ctx:
        c = Core(nc, ctx)
        term = c.sb("terms_in", [P, 2, SQ, 2 * H])
        score = c.sb("score", [P, SQ, H])
        term_in = [c.sem(f"term_in{j}") for j in range(2)]
        a1, a2, a3 = c.sem("score_a"), c.sem("score_b"), c.sem("score_c")
        block = ctx.enter_context(nc.Block())
        records = rec.rearrange("(p v) w -> p v w", p=P)

        @block.sync
        def _(sp):
            for n in range(4):
                if n >= 2:
                    sp.wait_ge(a3, n - 1)
                sp.dma_start(term[:, n % 2, :, :], records[:, n * SQ:(n + 1) * SQ, 2:2 + 2 * H]).then_inc(term_in[n % 2], 16)

        by_run = got[:, :, :].rearrange("p v h -> p (v h)").rearrange("p (c h s) -> p s c h", h=H, s=SEGS)

        @block.vector
        def _(dve):
            for n in range(4):
                dve.wait_ge(term_in[n % 2], 16 * (n // 2 + 1))
                at = slice(n * SQ, (n + 1) * SQ)
                nc.vector.scalar_tensor_tensor(score[:, :, :], pairs[:, at, 0, :], float(DH) ** -0.5, term[:, n % 2, :, 0:H], ALU.mult, ALU.add).then_inc(a1, 1)
                dve.wait_ge(a1, n + 1)
                nc.vector.tensor_tensor(score[:, :, :], score[:, :, :], pairs[:, at, 1, :], ALU.mult).then_inc(a2, 1)
                dve.wait_ge(a2, n + 1)
                nc.vector.tensor_tensor(by_run[:, n * 4:(n + 1) * 4, :, :], score[:, :, :].rearrange("p (s c) h -> p s c h", c=SEGC),
                                        term[:, n % 2, :, H:2 * H].rearrange("p (s c) h -> p s c h", c=SEGC), ALU.add).then_inc(a3, 1)
                dve.wait_ge(a3, n + 1)


def conservation(nc, k, w, vec, here, ps):
    with ExitStack() as ctx:
        c = Core(nc, ctx)
        row = c.sb("vec_row", [1, NP])
        hid = c.sb("vec_hid", [HIDC, NP])
        padded, loaded, made, kept, out, biased = c.sem("vec_padded"), c.sem("vec_loaded"), c.sem("vec_made"), c.sem("vec_kept"), c.sem("vec_out"), c.sem("vec_biased")
        block = ctx.enter_context(nc.Block())

        @block.sync
        def _(sp):
            sp.wait_ge(padded, 1)
            sp.dma_start(row[:, 0:N], vec.rearrange("n o -> o n")).then_inc(loaded, 16)

        @block.vector
        def _(dve):
            nc.vector.memset(row[:, :], 0.0).then_inc(padded, 1)
            dve.wait_ge(out, 1)
            nc.vector.tensor_tensor(here[:, :, F:F + H], ps[:, 7, 0:NB * H].rearrange("p (t h) -> p t h", h=H),
                                    w["bc2"][:, None, :].to_broadcast([P, NB, H]), ALU.add).then_inc(biased, 1)

        @block.tensor
        def _(pe):
            pe.wait_ge(loaded, 16)
            for a, b in SPANS:
                last = nc.tensor.matmul(wide(ps)[0:HIDC, a:b], w["Wc1"][:, :], row[:, a:b], start=True, stop=True)
            last.then_inc(made, 1)
            pe.wait_ge(kept, 1)
            for t in range(NB):
                last = nc.tensor.matmul(ps[:, 7, t * H:(t + 1) * H], hid[:, t * P:(t + 1) * P], w["Wc2"][:, :], start=True, stop=True, skip_group_check=True)
            last.then_inc(out, 1)

        @block.scalar
        def _(act):
            act.wait_ge(made, 1)
            nc.scalar.activation(hid[:, :], wide(ps)[0:HIDC, 0:NP], ACT.Relu, bias=w["bc1"][:, 0:1]).then_inc(kept, 1)
            act.wait_ge(biased, 1)
            nc.scalar.activation(here[:, :, F:F + H], here[:, :, F:F + H], ACT.Sigmoid)


def keep_sums(nc, sums, spread, ps):
    with ExitStack() as ctx:
        c = Core(nc, ctx)
        filled = c.sem("spread_filled")
        block = ctx.enter_context(nc.Block())

        @block.vector
        def _(dve):
            nc.vector.tensor_copy(sums[:, :], wide(ps)[0:3 * H, 0:NP])

        @block.gpsimd
        def _(pool):
            nc.gpsimd.memset(spread[:, :], 0.0).then_inc(filled, 1)
            for part in range(3):
                pool.wait_ge(filled, part + 1)
                heads = spread[:, :].rearrange("r (h d) -> r h d", d=DH)
                nc.gpsimd.affine_select(out=heads, in_=heads, compare_op=ALU.not_equal, fill=1.0, base=-H * part,
                                        pattern=[[-1, H], [0, DH]], channel_multiplier=1).then_inc(filled, 1)


def weigh_values(nc, v_t, sums, spread, acc_t, ps):
    with ExitStack() as ctx:
        c = Core(nc, ctx)
        made = c.sem("wv_made")
        block = ctx.enter_context(nc.Block())

        @block.tensor
        def _(pe):
            for a, b in SPANS:
                last = nc.tensor.matmul(wide(ps)[:, a:b], spread[:, :], sums[:, a:b], start=True, stop=True)
            last.then_inc(made, 1)

        @block.vector
        def _(dve):
            dve.wait_ge(made, 1)
            nc.vector.tensor_tensor(acc_t[:, :], v_t[:, :], wide(ps)[:, 0:NP], ALU.mult)


def scale_add_store(nc, k, xt, y, gamma, beta, out, ps):
    LAST = N - (NB - 1) * P
    with ExitStack() as ctx:
        c = Core(nc, ctx)
        rows = c.sb("out_rows", [P, NB, F])
        step, turned, stored = c.sem("fin_steps"), c.sem("fin_turned"), c.sem("out_stored")
        block = ctx.enter_context(nc.Block())

        @block.vector
        def _(dve):
            nc.vector.tensor_scalar(y[:, :], y[:, :], gamma, beta, ALU.mult, ALU.add).then_inc(step, 1)
            dve.wait_ge(step, 1)
            nc.vector.tensor_tensor(xt[:, :], xt[:, :], y[:, :], ALU.add).then_inc(step, 1)
            dve.wait_ge(turned, 1)
            nc.vector.tensor_copy(rows[:, :, :].rearrange("p t f -> p (t f)"), wide(ps)[:, 0:NP]).then_inc(step, 1)

        @block.tensor
        def _(pe):
            pe.wait_ge(step, 2)
            for t in range(NB):
                last = nc.tensor.transpose(wide(ps)[:, t * P:(t + 1) * P], xt[:, t * P:(t + 1) * P], k["ident"][:, :])
            last.then_inc(turned, 1)

        @block.sync
        def _(sp):
            sp.wait_ge(step, 3)
            sp.dma_start(out[0:(NB - 1) * P, :].rearrange("(t p) f -> p t f", p=P), rows[:, 0:NB - 1, :]).then_inc(stored, 16)
            sp.dma_start(out[(NB - 1) * P:N, :], rows[0:LAST, NB - 1, :]).then_inc(stored, 16)
            sp.wait_ge(stored, 32)


def layer3(nc, k, w, g, rec, table, xt, vec, out, ps):
    with ExitStack() as ctx:
        c = Core(nc, ctx)
        ht = c.sb("ht3", [P, NP])
        layernorm(nc, k, xt, ht, ps, "3")
        with ExitStack() as ectx:
            got = Core(nc, ectx).sb("got3", [P, NV, H])
            with ExitStack() as gctx:
                pairs = Core(nc, gctx).sb("pairs3", [P, NV, 2, H])
                with ExitStack() as rctx:
                    here = Core(nc, rctx).sb("here3", [P, NB, F + H])
                    node_rows(nc, k, [(ht, w["l3_Wq"][:, :])], F, w["l3_bq"][:, :], here, ps, "3q", dram=table)
                    node_rows(nc, k, [(ht, w["l3_Wk"][:, :])], F, w["l3_bk"][:, :], here, ps, "3k")
                    conservation(nc, k, w, vec, here, ps)
                    edge_products(nc, k, g, table, F, here, F + H, pairs, None, ps, "3")
                edge_scores(nc, k, rec, pairs, got)
            with ExitStack() as rctx:
                r = Core(nc, rctx)
                row = r.sb("score_rows", [P, SEGE])
                same = r.sb("same", [P, SEGE])
                gate = r.sb("gate", [P, SEGE])
                tmp = r.sb("span", [P, SEGE])
                segment_rows(nc, k, g, got, row, same, gate, tmp, ps)
                softmax_mass(nc, k, row, same, gate, tmp, ps)
                rows_back(nc, k, row, got, ps)
            weight_sums(nc, k, g, got, ps)
        acc_t = c.sb("acc_t3", [P, NP])
        with ExitStack() as rctx:
            r = Core(nc, rctx)
            v_t = r.sb("v_t", [P, NP])
            sums = r.sb("sums3", [3 * H, NP])
            spread = r.sb("spread3", [3 * H, F])
            keep_sums(nc, sums, spread, ps)
            project(nc, k, [(w["l3_Wv"][:, :], ht)], w["l3_bv"][:, 0:1], None, v_t, ps, "3v")
            weigh_values(nc, v_t, sums, spread, acc_t, ps)
        project(nc, k, [(w["l3_Wo"][:, :], acc_t)], w["l3_bo"][:, 0:1], ht, acc_t, ps, "3")
        layernorm(nc, k, acc_t, ht, ps, "3b", relu=False)
        scale_add_store(nc, k, xt, ht, w["l3_gamma"][:, 0:1], w["l3_beta"][:, 0:1], out, ps)


def fill_records(nc, feat, feat_s, rec, rec_s):
    with ExitStack() as ctx:
        c = Core(nc, ctx)
        zeroed, marked, stored = c.sem("feat_zeroed"), c.sem("feat_marked"), c.sem("rec_filled")
        block = ctx.enter_context(nc.Block())

        @block.vector
        def _(dve):
            nc.vector.memset(feat[:, :, :], 0.0).then_inc(zeroed, 1)
            nc.vector.memset(feat_s[:, :, :], 0.0).then_inc(zeroed, 1)
            dve.wait_ge(zeroed, 2)
            nc.vector.memset(feat[:, :, 1:2], -1.0).then_inc(marked, 1)
            nc.vector.memset(feat_s[:, :, 1:2], -1.0).then_inc(marked, 1)

        @block.sync
        def _(sp):
            sp.wait_ge(marked, 2)
            sp.dma_start(rec.rearrange("(p v) w -> p v w", p=P), feat[:, :, :]).then_inc(stored, 16)
            sp.dma_start(rec_s.rearrange("(p v) w -> p v w", p=P), feat_s[:, :, :]).then_inc(stored, 16)
            sp.wait_ge(stored, 32)


def clear_index(nc, indices):
    with ExitStack() as ctx:
        block = ctx.enter_context(nc.Block())

        @block.vector
        def _(dve):
            for g in indices:
                nc.vector.memset(g["src"][:, NV:NV + 2 * U], 0)


def build(nc, a, out):
    Core.spent.clear()
    with ExitStack() as ctx:
        top = Core(nc, ctx)
        ps = top.psum("ps", [P, 8, 512])
        k = constants(nc, top)
        rec = top.dram("rec", [P * (NV + 1), W_REC])
        rec_s = top.dram("rec_s", [P * (NV + 1), 2])
        by_dst, by_src = {}, {}
        for name, g in (("d", by_dst), ("s", by_src)):
            g["block"] = top.sb("block_" + name, [1, NV], i32)
            g["src"] = top.sb("gather_" + name, [P, NV + 2 * U], i32)
            g["loc"] = top.sb("loc_" + name, [P, NV])
            g["loc_row"] = top.dram("loc_row_" + name, [NV * P], bf16)
        KEYS = -(-NC // P) * P * P
        rows_d = (top.dram("key_row_d", [KEYS]), top.dram("lo_row_d", [KEYS], bf16))
        rows_s = (top.dram("key_row_s", [KEYS]), top.dram("lo_row_s", [KEYS], bf16))
        with ExitStack() as sctx:
            s = Core(nc, sctx)
            feat = s.sb("feat", [P, NV + 1, W_REC])
            feat_s = s.sb("feat_s", [P, NV + 1, 2])
            fill_records(nc, feat, feat_s, rec, rec_s)
            load_keys(nc, k, a["src"], feat[:, 0:NC, 0], feat_s[:, 0:NC, 1], *rows_s, ps, "s")
            load_keys(nc, k, a["dst"], feat_s[:, 0:NC, 0], feat[:, 0:NC, 1], *rows_d, ps, "d")
            sort_edges(nc, k, feat[:, 0:NC, 0], feat_s[:, 0:NC, 1], lambda c, n: feat_s[:, ds(c, n), :], rec_s, by_src["block"], ps, rows_s, "s",
                       a, feat)
            sort_edges(nc, k, feat_s[:, 0:NC, 0], feat[:, 0:NC, 1], lambda c, n: feat[:, ds(c, n), :], rec, by_dst["block"], ps, rows_d, "d")
        clear_index(nc, [by_dst, by_src])
        sorted_index(nc, k, rec, by_dst["src"][:, 0:NV], by_dst["loc"], by_dst["loc_row"], ps, "id")
        sorted_index(nc, k, rec_s, by_src["src"][:, 0:NV], by_src["loc"], by_src["loc_row"], ps, "is")
        w = load_weights(nc, top, a)
        xt = top.sb("xt", [P, NP])
        load_nodes(nc, k, a["x"], xt, ps)
        table2 = top.dram("table_wide", [NP, 2 * F])
        table1 = top.dram("table_narrow", [NP, F])
        spool = top.dram("value_spool", [P, NV, F])
        layer0(nc, k, w, by_dst, table2, xt, ps)
        layer1(nc, k, w, by_src, table1, xt, ps)
        layer2(nc, k, w, by_dst, rec, table2, spool, xt, a["node_type_8"], ps)
        layer3(nc, k, w, by_dst, rec, table1, xt, a["node_vec1"], out, ps)


def kernel(**inputs):
    import concourse.bacc as bacc
    from concourse.bass_utils import run_bass_kernel_spmd

    nc = bacc.Bacc("TRN2", target_bir_lowering=False, num_devices=1)
    arrays, a = {}, {}
    for name, value in inputs.items():
        v = np.asarray(value)
        if name in ("L1_gnn_W1", "L1_gnn_W2"):
            v = v.T
        if v.ndim == 0:
            v = v.reshape(1)
        v = np.ascontiguousarray(v)
        arrays["in_" + name] = v
        a[name] = nc.dram_tensor("in_" + name, v.shape, mybir.dt.from_np(v.dtype), kind="ExternalInput").ap()
    out = nc.dram_tensor("out", (N, F), f32, kind="ExternalOutput").ap()
    build(nc, a, out)
    result = run_bass_kernel_spmd(nc, [arrays], core_ids=[0])
    return result.results[0]["out"]
```
